# Optimizing a Trainium2 kernel written in Bass

```python
import numpy as np
import jax
import jax.numpy as jnp

def _softmax(x, axis=-1):
    return jax.nn.softmax(x, axis=axis)

def _gelu(x):
    return jax.nn.gelu(x, approximate=True)

def _silu(x):
    return jax.nn.silu(x)

def _sigmoid(x):
    return jax.nn.sigmoid(x)

def _layernorm(x, axis=-1, eps=1e-05):
    m = jnp.mean(x, axis=axis, keepdims=True)
    v = jnp.var(x, axis=axis, keepdims=True)
    return (x - m) / jnp.sqrt(v + eps)

def _scatter_add(tgt, idx, src, axis=0):
    return tgt.at[idx].add(src)

def _segment_sum(src, seg, n):
    return jax.ops.segment_sum(src, seg, n)
kernel_name = 'mk_recurrent_d2_jaxref_r4_daafbe'

def setup_inputs(seed: int=0):
    np.random.seed(seed)
    _w = jnp.asarray

    def _L0_attn_setup():
        import jax, jax.numpy as jnp
        import numpy as np
        NUM_HEADS = 16
        WINDOW = 128
        PERSIST = 16
        key = jax.random.key(seed)
        ks = jax.random.split(key, 6)
        B, S, D, L = (2, 512, 512, 128)
        sd = 1.0 / np.sqrt(D)
        sl = 1.0 / np.sqrt(L)
        return {'x': jax.random.normal(ks[0], (B, S, D), dtype=jnp.float32), 'Wq': jax.random.normal(ks[1], (D, D), dtype=jnp.float32) * sd, 'Wkv': jax.random.normal(ks[2], (D, L), dtype=jnp.float32) * sd, 'Wk': jax.random.normal(ks[3], (L, D), dtype=jnp.float32) * sl, 'Wv': jax.random.normal(ks[4], (L, D), dtype=jnp.float32) * sl, 'Wo': jax.random.normal(ks[5], (D, D), dtype=jnp.float32) * sd}
    _L0_attn_in = _L0_attn_setup()

    def _L0_ffn_setup():
        import jax, jax.numpy as jnp
        import numpy as np
        NUM_EXPERTS = 32
        TOP_K = 6
        N_GROUPS = 4
        N_LIMITED_GROUPS = 2
        key = jax.random.key(seed)
        ks = jax.random.split(key, 8)
        H, M = (512, 352)
        SH = 2 * M
        s = 0.02
        return {'hidden_states': jax.random.normal(ks[0], (4, 512, H), jnp.float32), 'gate_w': jax.random.normal(ks[1], (H, NUM_EXPERTS), jnp.float32) * s, 'w_gate': jax.random.normal(ks[2], (NUM_EXPERTS, H, M), jnp.float32) * s, 'w_up': jax.random.normal(ks[3], (NUM_EXPERTS, H, M), jnp.float32) * s, 'w_down': jax.random.normal(ks[4], (NUM_EXPERTS, M, H), jnp.float32) * s, 'sw_gate': jax.random.normal(ks[5], (H, SH), jnp.float32) * s, 'sw_up': jax.random.normal(ks[6], (H, SH), jnp.float32) * s, 'sw_down': jax.random.normal(ks[7], (SH, H), jnp.float32) * s}
    _L0_ffn_in = _L0_ffn_setup()

    def _L1_attn_setup():
        import jax, jax.numpy as jnp
        import numpy as np
        B, S, D = (4, 1024, 512)
        IDENTITY_WEIGHT = 0.5
        ROT_DIM = D // 2

        def _layernorm(x, gamma, beta, eps=1e-05):
            mu = jnp.mean(x, axis=-1, keepdims=True)
            var = jnp.var(x, axis=-1, keepdims=True)
            return (x - mu) * jax.lax.rsqrt(var + eps) * gamma + beta

        def _rotary(t, rot_dim, theta=10000.0):
            seq = t.shape[-2]
            inv_freq = 1.0 / theta ** (jnp.arange(0, rot_dim, 2, dtype=jnp.float32) / rot_dim)
            freqs = jnp.arange(seq, dtype=jnp.float32)[:, None] * inv_freq[None, :]
            freqs = jnp.repeat(freqs, 2, axis=-1)
            cos, sin = (jnp.cos(freqs), jnp.sin(freqs))
            t_rot, t_pass = (t[..., :rot_dim], t[..., rot_dim:])
            x1, x2 = (t_rot[..., 0::2], t_rot[..., 1::2])
            rot_half = jnp.stack([-x2, x1], axis=-1).reshape(t_rot.shape)
            return jnp.concatenate([t_rot * cos + rot_half * sin, t_pass], axis=-1)

        def _cos_sim(x):
            return x / jnp.linalg.norm(x, axis=-1, keepdims=True)
        key = jax.random.key(seed)
        ks = jax.random.split(key, 3)
        scale = 0.02
        return {'X': jax.random.normal(ks[0], (B, S, D), jnp.float32), 'W_in': jax.random.normal(ks[1], (D, 3 * D), jnp.float32) * scale, 'b_in': jnp.zeros((3 * D,), jnp.float32), 'W_out': jax.random.normal(ks[2], (D, D), jnp.float32) * scale, 'b_out': jnp.zeros((D,), jnp.float32), 'gamma': jnp.ones((D,), jnp.float32), 'beta': jnp.zeros((D,), jnp.float32)}
    _L1_attn_in = _L1_attn_setup()

    def _L1_ffn_setup():
        import jax, jax.numpy as jnp
        import numpy as np
        HIDDEN = 512
        INTER = 2048
        MOE_INTER = 256
        N_ROUTED = 8
        NUM_LOCAL = 8
        TOP_K = 2
        B, S = (4, 512)

        def _mlp(x, gw, uw, dw):
            g = x @ gw.T
            u = x @ uw.T
            return g * jax.nn.sigmoid(g) * u @ dw.T
        key = jax.random.key(seed)
        ks = jax.random.split(key, 8)
        std = 0.02
        return {'hidden_states': jax.random.normal(ks[0], (B, S, HIDDEN), jnp.float32), 'router_weight': jax.random.normal(ks[1], (N_ROUTED, HIDDEN), jnp.float32) * std, 'sh_gate': jax.random.normal(ks[2], (INTER, HIDDEN), jnp.float32) * std, 'sh_up': jax.random.normal(ks[3], (INTER, HIDDEN), jnp.float32) * std, 'sh_down': jax.random.normal(ks[4], (HIDDEN, INTER), jnp.float32) * std, 'r_gate': jax.random.normal(ks[5], (MOE_INTER, HIDDEN), jnp.float32) * std, 'r_up': jax.random.normal(ks[6], (MOE_INTER, HIDDEN), jnp.float32) * std, 'r_down': jax.random.normal(ks[7], (HIDDEN, MOE_INTER), jnp.float32) * std}
    _L1_ffn_in = _L1_ffn_setup()
    _d = {'L0_attn_x': _L0_attn_in['x'], 'L0_attn_Wq': _L0_attn_in['Wq'], 'L0_attn_Wkv': _L0_attn_in['Wkv'], 'L0_attn_Wk': _L0_attn_in['Wk'], 'L0_attn_Wv': _L0_attn_in['Wv'], 'L0_attn_Wo': _L0_attn_in['Wo'], 'L0_ffn_gate_w': _L0_ffn_in['gate_w'], 'L0_ffn_w_gate': _L0_ffn_in['w_gate'], 'L0_ffn_w_up': _L0_ffn_in['w_up'], 'L0_ffn_w_down': _L0_ffn_in['w_down'], 'L0_ffn_sw_gate': _L0_ffn_in['sw_gate'], 'L0_ffn_sw_up': _L0_ffn_in['sw_up'], 'L0_ffn_sw_down': _L0_ffn_in['sw_down'], 'L1_attn_W_in': _L1_attn_in['W_in'], 'L1_attn_b_in': _L1_attn_in['b_in'], 'L1_attn_W_out': _L1_attn_in['W_out'], 'L1_attn_b_out': _L1_attn_in['b_out'], 'L1_attn_gamma': _L1_attn_in['gamma'], 'L1_attn_beta': _L1_attn_in['beta'], 'L1_ffn_router_weight': _L1_ffn_in['router_weight'], 'L1_ffn_sh_gate': _L1_ffn_in['sh_gate'], 'L1_ffn_sh_up': _L1_ffn_in['sh_up'], 'L1_ffn_sh_down': _L1_ffn_in['sh_down'], 'L1_ffn_r_gate': _L1_ffn_in['r_gate'], 'L1_ffn_r_up': _L1_ffn_in['r_up'], 'L1_ffn_r_down': _L1_ffn_in['r_down']}
    _x0 = _d['L0_attn_x']
    _d['L0_attn_x'] = jax.random.normal(jax.random.fold_in(jax.random.key(seed), 1), (2, 2048, 512), dtype=_x0.dtype)
    del _x0
    return _d

def reference(L0_attn_x, L0_attn_Wq, L0_attn_Wkv, L0_attn_Wk, L0_attn_Wv, L0_attn_Wo, L0_ffn_gate_w, L0_ffn_w_gate, L0_ffn_w_up, L0_ffn_w_down, L0_ffn_sw_gate, L0_ffn_sw_up, L0_ffn_sw_down, L1_attn_W_in, L1_attn_b_in, L1_attn_W_out, L1_attn_b_out, L1_attn_gamma, L1_attn_beta, L1_ffn_router_weight, L1_ffn_sh_gate, L1_ffn_sh_up, L1_ffn_sh_down, L1_ffn_r_gate, L1_ffn_r_up, L1_ffn_r_down):

    def _L0_attn_ref(x, Wq, Wkv, Wk, Wv, Wo):
        import jax, jax.numpy as jnp
        import numpy as np
        NUM_HEADS = 16
        WINDOW = 128
        PERSIST = 16
        B, S, D = x.shape
        H = NUM_HEADS
        hd = D // H
        scale = hd ** (-0.5)
        q = (x @ Wq).reshape(B, S, H, hd)
        kv_latent = x @ Wkv
        k = (kv_latent @ Wk).reshape(B, S, H, hd)
        v = (kv_latent @ Wv).reshape(B, S, H, hd)
        qi = jnp.arange(S)[:, None]
        ki = jnp.arange(S)[None, :]
        mask = (ki <= qi) & ((qi - ki < WINDOW) | (ki < PERSIST))
        scores = jnp.einsum('bqhd,bkhd->bhqk', q, k) * scale
        scores = jnp.where(mask[None, None], scores, jnp.finfo(scores.dtype).min)
        attn = jax.nn.softmax(scores, axis=-1)
        out = jnp.einsum('bhqk,bkhd->bqhd', attn, v).reshape(B, S, D)
        return out @ Wo

    def _L0_ffn_ref(hidden_states, gate_w, w_gate, w_up, w_down, sw_gate, sw_up, sw_down):
        import jax, jax.numpy as jnp
        import numpy as np
        NUM_EXPERTS = 32
        TOP_K = 6
        N_GROUPS = 4
        N_LIMITED_GROUPS = 2
        B, S, H = hidden_states.shape
        E, K = (NUM_EXPERTS, TOP_K)
        x = hidden_states.reshape(-1, H)
        T = x.shape[0]
        scores = jax.nn.sigmoid(x @ gate_w)
        original_scores = scores
        epg = E // N_GROUPS
        sg = scores.reshape(T, N_GROUPS, epg)
        group_scores = jnp.max(sg, axis=-1)
        _, top_groups = jax.lax.top_k(group_scores, N_LIMITED_GROUPS)
        mask = jnp.ones((T, N_GROUPS), dtype=bool)
        mask = mask.at[jnp.arange(T)[:, None], top_groups].set(False)
        sg = jnp.where(mask[:, :, None], -jnp.inf, sg)
        masked_scores = sg.reshape(T, E)
        _, selected_experts = jax.lax.top_k(masked_scores, K)
        weights = jnp.take_along_axis(original_scores, selected_experts, axis=-1)
        weights = weights / jnp.sum(weights, axis=-1, keepdims=True)
        sel_flat = selected_experts.ravel()
        x_exp = jnp.repeat(x, K, axis=0)
        sort_idx = jnp.argsort(sel_flat)
        xs = x_exp[sort_idx]
        group_sizes = jnp.bincount(sel_flat, length=E).astype(jnp.int32)
        g = jax.lax.ragged_dot(xs, w_gate, group_sizes)
        u = jax.lax.ragged_dot(xs, w_up, group_sizes)
        d = jax.lax.ragged_dot(jax.nn.silu(g) * u, w_down, group_sizes)
        unsort_idx = jnp.argsort(sort_idx)
        out = d[unsort_idx].reshape(T, K, H)
        expert_out = jnp.sum(out * weights[..., None], axis=1)
        shared = jax.nn.silu(x @ sw_gate) * (x @ sw_up) @ sw_down
        return (expert_out + shared).reshape(B, S, H)

    def _L1_attn_ref(X, W_in, b_in, W_out, b_out, gamma, beta):
        import jax, jax.numpy as jnp
        import numpy as np
        B, S, D = (4, 1024, 512)
        IDENTITY_WEIGHT = 0.5
        ROT_DIM = D // 2

        def _layernorm(x, gamma, beta, eps=1e-05):
            mu = jnp.mean(x, axis=-1, keepdims=True)
            var = jnp.var(x, axis=-1, keepdims=True)
            return (x - mu) * jax.lax.rsqrt(var + eps) * gamma + beta

        def _rotary(t, rot_dim, theta=10000.0):
            seq = t.shape[-2]
            inv_freq = 1.0 / theta ** (jnp.arange(0, rot_dim, 2, dtype=jnp.float32) / rot_dim)
            freqs = jnp.arange(seq, dtype=jnp.float32)[:, None] * inv_freq[None, :]
            freqs = jnp.repeat(freqs, 2, axis=-1)
            cos, sin = (jnp.cos(freqs), jnp.sin(freqs))
            t_rot, t_pass = (t[..., :rot_dim], t[..., rot_dim:])
            x1, x2 = (t_rot[..., 0::2], t_rot[..., 1::2])
            rot_half = jnp.stack([-x2, x1], axis=-1).reshape(t_rot.shape)
            return jnp.concatenate([t_rot * cos + rot_half * sin, t_pass], axis=-1)

        def _cos_sim(x):
            return x / jnp.linalg.norm(x, axis=-1, keepdims=True)
        Xn = _layernorm(X, gamma, beta)
        QKV = Xn @ W_in + b_in
        Q, K, V = jnp.split(QKV, 3, axis=-1)
        K = _rotary(K, ROT_DIM)
        V = _rotary(V, ROT_DIM)
        A = jnp.sum(_cos_sim(K) * _cos_sim(V), axis=-2)
        A = (1.0 - IDENTITY_WEIGHT) * A + IDENTITY_WEIGHT
        Y = A[:, None, :] * Q
        Y = Y @ W_out + b_out
        return Y + X

    def _L1_ffn_ref(hidden_states, router_weight, sh_gate, sh_up, sh_down, r_gate, r_up, r_down):
        import jax, jax.numpy as jnp
        import numpy as np
        HIDDEN = 512
        INTER = 2048
        MOE_INTER = 256
        N_ROUTED = 8
        NUM_LOCAL = 8
        TOP_K = 2
        B, S = (4, 512)

        def _mlp(x, gw, uw, dw):
            g = x @ gw.T
            u = x @ uw.T
            return g * jax.nn.sigmoid(g) * u @ dw.T
        Bsz, Seq, H = hidden_states.shape
        x = hidden_states.reshape(-1, H)
        logits = x.astype(jnp.float32) @ router_weight.astype(jnp.float32).T
        topk_vals, topk_idx = jax.lax.top_k(logits, TOP_K)
        topk_w = jax.nn.softmax(topk_vals, axis=-1)
        slot_mask = (topk_idx < NUM_LOCAL).astype(topk_w.dtype)
        comb_w = jnp.sum(topk_w * slot_mask, axis=-1).astype(x.dtype)
        shared = _mlp(x, sh_gate, sh_up, sh_down)
        routed = _mlp(x, r_gate, r_up, r_down) * comb_w[:, None]
        return (shared + routed).reshape(Bsz, Seq, H)
    x = L0_attn_x
    xn = _layernorm(x, axis=-1)
    s = _L0_attn_ref(xn, L0_attn_Wq, L0_attn_Wkv, L0_attn_Wk, L0_attn_Wv, L0_attn_Wo)
    g = _silu(_L0_ffn_ref(xn, L0_ffn_gate_w, L0_ffn_w_gate, L0_ffn_w_up, L0_ffn_w_down, L0_ffn_sw_gate, L0_ffn_sw_up, L0_ffn_sw_down))
    x = x + s * g
    xn = _layernorm(x, axis=-1)
    s = _L1_attn_ref(xn, L1_attn_W_in, L1_attn_b_in, L1_attn_W_out, L1_attn_b_out, L1_attn_gamma, L1_attn_beta)
    g = _silu(_L1_ffn_ref(xn, L1_ffn_router_weight, L1_ffn_sh_gate, L1_ffn_sh_up, L1_ffn_sh_down, L1_ffn_r_gate, L1_ffn_r_up, L1_ffn_r_down))
    x = x + s * g
    return x

_drawn_inputs = setup_inputs


def setup_inputs(seed=0):
    import zlib

    import numpy as np

    out = dict(_drawn_inputs(seed))
    spreads = {'L1_attn_b_in': (0.0, 0.1),
     'L1_attn_b_out': (0.0, 0.1),
     'L1_attn_gamma': (1.0, 0.2),
     'L1_attn_beta': (0.0, 0.1)}
    factors = {}
    for name, (base, spread) in spreads.items():
        noise = np.random.default_rng([zlib.crc32(name.encode()), seed]).standard_normal(out[name].shape)
        drawn = base * np.exp(spread * noise) if base else spread * noise
        out[name] = jnp.asarray(drawn.astype(out[name].dtype))
    for name, factor in factors.items():
        out[name] = (out[name] * factor).astype(out[name].dtype)
    return out
```

```python
from contextlib import ExitStack

import concourse.bass as bass
import numpy as np
from concourse import mybir

ALU = mybir.AluOpType
ACT = mybir.ActivationFunctionType
AX = mybir.AxisListType
F32 = mybir.dt.float32
F32R = mybir.dt.float32r
I32 = mybir.dt.int32
U32 = mybir.dt.uint32

P = 128
D = 512
KC = D // P
B, S = 2, 2048
T = B * S
TILES = T // P
GT = 4
G = GT * P
GROUPS = T // G
EPS = 1e-5

NH, HD = 16, 32
WINDOW, PERSIST = 128, 16
SCALE = float(HD) ** -0.5
BT = S // P
LAT = 128
NEG = -1.0e30

E, TOPK, NG, TOPG, EPG = 32, 6, 4, 2, 8
M = 352
MC = 3
MR = M - 2 * P
SH = 2 * M
SHB = 6
SHR = SH - 5 * P
MINT = 3
MAXT = T * TOPK // P + E * MINT
MINTILES = T * TOPK // P
SIG_ONE = 16.6355
SIG_ZERO = -88.7

INTER, MOE_INTER = 2048, 256
FB = (INTER + MOE_INTER) // P
NROUTED = 8
RH = D // 4


class Env:
    pass


def mask_table():
    m = np.full((BT, P, 2 * P + PERSIST), NEG, np.float32)
    for i in range(BT):
        qi = i * P + np.arange(P)[:, None]
        ki = np.concatenate([(i - 1) * P + np.arange(2 * P), np.arange(PERSIST)])[None, :]
        own = np.arange(2 * P + PERSIST)[None, :] < 2 * P
        near = (ki <= qi) & (qi - ki < WINDOW)
        seen = np.where(own, near & (ki >= 0) & ((ki >= PERSIST) | (i == 0)), i > 0)
        m[i][seen] = 0.0
    return m


def scope(nc):
    ctx, sems = ExitStack(), []

    def clear():
        if sems:
            nc.clear_and_free_semaphores(sems)
            nc.all_engine_barrier()
    ctx.callback(clear)

    def sem(name):
        sems.append(nc.alloc_semaphore(name))
        return sems[-1]
    sb = lambda name, shape, dt=F32: ctx.enter_context(nc.sbuf_tensor(name, shape, dt))
    ps = lambda name, shape, dt=F32: ctx.enter_context(nc.psum_tensor(name, shape, dt))
    return ctx, sb, ps, sem


def f(ap):
    return ap.bitcast(F32)


def mm3(pe, out, lhs, rhs, first, last, **kw):
    pe.matmul(out, lhs[0], rhs[1], start=first, stop=False, **kw)
    pe.matmul(out, lhs[1], rhs[0], start=False, stop=False, **kw)
    return pe.matmul(out, lhs[0], rhs[0], start=False, stop=last, **kw)


class Chain:

    def __init__(self, eng, sem, base=0):
        self.eng, self.sem, self.base, self.n = eng, sem, base, 0

    def __call__(self, ins):
        self.n += 1
        return ins.then_inc(self.sem, 1)

    def wait(self):
        self.eng.wait_ge(self.sem, self.base + self.n)


def at(ap, i):
    rest = " ".join("bcdefg"[:len(ap.shape) - 1])
    first = rest.split()[0]
    return ap[bass.ds(i, 1)].rearrange(f"a {rest} -> (a {first}) {' '.join(rest.split()[1:])}")


def rstd_chain(dve, c, mv, r, tmp):
    c(dve.reciprocal(r[:, :], r[:, :]))
    c.wait()
    c(dve.tensor_tensor(tmp[:, :], r[:, :], r[:, :], ALU.mult))
    c.wait()
    c(dve.tensor_tensor(tmp[:, :], tmp[:, :], mv, ALU.mult))
    c.wait()
    c(dve.tensor_scalar(tmp[:, :], tmp[:, :], -0.5, 1.5, ALU.mult, ALU.add))
    c.wait()
    c(dve.tensor_tensor(r[:, :], r[:, :], tmp[:, :], ALU.mult))
    c.wait()


def phase_front(nc, env):
    ctx, sb, ps, sem = scope(nc)
    RING = 6
    ITEMS = 18
    x_v = env.x.rearrange("(g j p) d -> g p j d", p=P, j=GT)
    xn_v = env.xn_d.rearrange("(g j p) d -> g p j d", p=P, j=GT)
    v_v = env.v_d.rearrange("(g j p) d -> g p j d", p=P, j=GT)
    with ctx:
        x_sb = [sb(f"f_x{i}", [P, GT, D]) for i in range(2)]
        xn = [sb(f"f_xn{i}", [P, GT, D]) for i in range(2)]
        xT = [[sb(f"f_xT{i}{h}", [P, KC, G], F32R) for h in range(2)] for i in range(2)]
        qk = [sb(f"f_qk{i}", [P, 8, 2, G], F32R) for i in range(2)]
        vst = [sb(f"f_v{i}", [P, GT, NH, 2, HD], F32R) for i in range(2)]
        lat = [sb(f"f_lat{h}", [P, G], F32R) for h in range(2)]
        wraw = xn[1]
        wq = [sb(f"f_wq{h}", [P, KC, D], F32R) for h in range(2)]
        wkv = [sb(f"f_wkv{h}", [P, KC, LAT], F32R) for h in range(2)]
        wk = [sb(f"f_wk{h}", [P, 1, D], F32R) for h in range(2)]
        wv = [sb(f"f_wv{h}", [P, 1, D], F32R) for h in range(2)]
        wg = [sb(f"f_wg{h}", [P, KC, E], F32R) for h in range(2)]
        st = sb("f_st", [P, GT, 6])
        mv = sb("f_mv", [P, GT, 2])
        var = sb("f_var", [P, GT])
        rstd = sb("f_rstd", [P, GT])
        tmp = sb("f_tmp", [P, GT])
        bank = [ps(f"f_ps{i}", [P, D]) for i in range(RING)]

        w_in, w_used, w_hi = sem("f_w_in"), sem("f_w_used"), sem("f_w_hi")
        id_step = sem("f_id")
        x_in = [sem(f"f_x_in{i}") for i in range(2)]
        normed = sem("f_normed")
        xn_out = [sem(f"f_xn_out{i}") for i in range(2)]
        xn_free = sem("f_xn_free")
        var_ready, root_ready = sem("f_var_ready"), sem("f_root_ready")
        dve_step = sem("f_dve_step")
        full = sem("f_full")
        hi_done = sem("f_hi_done")
        lo_done = sem("f_lo_done")
        st_out = [sem(f"f_st_out{i}") for i in range(2)]
        st_free = sem("f_st_free")
        block = ctx.enter_context(nc.Block())

        weights = [
            (env.Wq.rearrange("(c p) n -> p c n", p=P), wq, KC, D),
            (env.Wkv.rearrange("(c p) n -> p c n", p=P), wkv, KC, LAT),
            (env.Wk.rearrange("(c p) n -> p c n", p=P), wk, 1, D),
            (env.Wv.rearrange("(c p) n -> p c n", p=P), wv, 1, D),
            (env.gate_w.rearrange("(c p) n -> p c n", p=P), wg, KC, E),
        ]

        def dest(b, j, h):
            if j < 4:
                return xT[b][h][:, :, j * P:(j + 1) * P]
            if j == 5:
                return lat[h][:, :]
            if j < 14:
                return qk[b][:, j - 6, h, :]
            return vst[b][:, j - 14, :, h, :]

        def psum(b, j):
            src = bank[(b * ITEMS + j) % RING][:, :]
            if j < 4:
                return src.rearrange("p (c t) -> p c t", c=KC)
            return src if j < 14 else src.rearrange("p (h d) -> p h d", d=HD)

        @block.sync
        def _(sp):
            for i, (src, _, c, n) in enumerate(weights):
                if i:
                    sp.wait_ge(w_used, i)
                sp.dma_start(wraw[:, 0:c, 0:n], src).then_inc(w_in, 16)
            with sp.Fori(0, GROUPS // 2) as gp:
                for b in range(2):
                    g = 2 * gp + b
                    sp.wait_ge(normed, g + 3)
                    sp.dma_start(at(xn_v, g), xn[b][:, :, :]).then_inc(xn_out[b], 16)
                    sp.wait_ge(lo_done, (g + 1) * ITEMS + RING)
                    tok = bass.ds(g * G, G)
                    for h in range(2):
                        for w in range(2):
                            sp.dma_start(env.qk_d[w, h, :, tok].rearrange("(m p) t -> p m t", p=P),
                                         f(qk[b][:, 4 * w:4 * w + 4, h, :])).then_inc(st_out[b], 16)
                        sp.dma_start(at(env.xT_d[h], g), f(xT[b][h][:, :, :])).then_inc(st_out[b], 16)
                    sp.dma_start(at(v_v, g), f(vst[b][:, :, :, :, :]).rearrange("p j h l d -> p j (h l d)"))\
                      .then_inc(st_out[b], 16)
                    sp.wait_ge(xn_out[b], 16 * gp + 16)
                    sp.sem_inc(xn_free, 1)
                    sp.wait_ge(st_out[b], 112 * gp + 112)
                    sp.sem_inc(st_free, 1)

        @block.gpsimd
        def _(pool):
            pool.memset(env.ident[:, :], 0.0).then_inc(id_step, 1)
            pool.wait_ge(id_step, 1)
            pool.affine_select(out=env.ident[:, :], in_=env.ident[:, :], compare_op=ALU.not_equal, fill=1.0,
                               base=0, pattern=[[-1, P]], channel_multiplier=1).then_inc(id_step, 1)
            pool.wait_ge(normed, 2)
            with pool.Fori(0, GROUPS // 2) as gp:
                for b in range(2):
                    g = 2 * gp + b
                    pool.wait_ge(normed, g + 1)
                    pool.dma_start(x_sb[b][:, :, :], at(x_v, g)).then_inc(x_in[b], 16)

        @block.scalar
        def _(act):
            for i, (_, dst, c, n) in enumerate(weights):
                act.wait_ge(w_in, 16 * (i + 1))
                act.activation(dst[0][:, :, :], wraw[:, 0:c, 0:n], ACT.Copy).then_inc(w_hi, 1)

            def root(g):
                act.wait_ge(var_ready, g + 1)
                act.activation(rstd[:, :], var[:, :], ACT.Sqrt).then_inc(root_ready, 1)

            def hi(g, b):
                act.wait_ge(st_free, g + 1)
                for j in range(ITEMS):
                    if j == 4:
                        continue
                    act.wait_ge(full, g * ITEMS + j + 1)
                    act.activation(dest(b, j, 0), psum(b, j), ACT.Copy).then_inc(hi_done, 1)
            root(0)
            with act.Fori(0, GROUPS // 2 - 1) as gp:
                for b in range(2):
                    root(2 * gp + b + 1)
                    hi(2 * gp + b, b)
            root(GROUPS - 1)
            hi(GROUPS - 2, 0)
            hi(GROUPS - 1, 1)

        @block.vector
        def _(dve):
            dve.sem_inc(normed, 2)
            dve.sem_inc(xn_free, 2)
            dve.sem_inc(st_free, 2)
            dve.sem_inc(lo_done, RING)
            for i, (_, dst, c, n) in enumerate(weights):
                dve.wait_ge(w_hi, i + 1)
                dve.tensor_tensor(dst[1][:, :, :], wraw[:, 0:c, 0:n], f(dst[0][:, :, :]), ALU.subtract)\
                   .then_inc(w_used, 1)

            def norm(g, b, gp):
                c = Chain(dve, dve_step, g * (2 * GT + 5))
                dve.wait_ge(x_in[b], 16 * gp + 16)
                for j in range(GT):
                    c(dve.bn_stats(st[:, j, :], x_sb[b][:, j, :]))
                c.wait()
                dve.memset(tmp[:, 0:1], 0.0)
                for j in range(GT):
                    c(dve.bn_aggr(mv[:, j, :], st[:, j, :]))
                c.wait()
                dve.tensor_scalar(var[:, :], mv[:, :, 1], EPS, None, ALU.add).then_inc(var_ready, 1)
                dve.wait_ge(root_ready, g + 1)
                rstd_chain(dve, c, var[:, :], rstd, tmp)
                dve.wait_ge(xn_free, g + 1)
                for j in range(GT):
                    ins = dve.tensor_scalar(xn[b][:, j, :], x_sb[b][:, j, :], mv[:, j, 0:1], rstd[:, j:j + 1],
                                            ALU.subtract, ALU.mult)
                ins.then_inc(normed, 1)

            def lo(g, b):
                for j in range(ITEMS):
                    if j == 4:
                        dve.wait_ge(full, g * ITEMS + j + 1)
                        dve.tensor_copy(env.logits[:, bass.ds(g * GT, GT), :],
                                        psum(b, j)[:, 0:GT * E].rearrange("p (j e) -> p j e", e=E))\
                           .then_inc(lo_done, 1)
                        continue
                    dve.wait_ge(hi_done, g * (ITEMS - 1) + j + (j < 4))
                    dve.tensor_tensor(dest(b, j, 1), psum(b, j), f(dest(b, j, 0)), ALU.subtract)\
                       .then_inc(lo_done, 1)
            norm(0, 0, 0)
            with dve.Fori(0, GROUPS // 2 - 1) as gp:
                norm(2 * gp + 1, 1, gp)
                lo(2 * gp, 0)
                norm(2 * gp + 2, 0, gp + 1)
                lo(2 * gp + 1, 1)
            norm(GROUPS - 1, 1, GROUPS // 2 - 1)
            lo(GROUPS - 2, 0)
            lo(GROUPS - 1, 1)

        @block.tensor
        def _(pe):
            pe.wait_ge(id_step, 2)
            pe.wait_ge(w_used, len(weights))
            with pe.Fori(0, GROUPS // 2) as gp:
                for b in range(2):
                    g = 2 * gp + b

                    def out(j):
                        pe.wait_ge(lo_done, g * ITEMS + j + 1)
                        return bank[(b * ITEMS + j) % RING]
                    pe.wait_ge(normed, g + 3)
                    for j in range(GT):
                        o = out(j)
                        for c in range(KC):
                            ins = pe.transpose(o[:, c * P:(c + 1) * P], xn[b][:, j, c * P:(c + 1) * P],
                                               env.ident[:, :])
                        ins.then_inc(full, 1)
                    pe.wait_ge(lo_done, g * ITEMS + 4 + RING)
                    x2 = lambda c, t: [xT[b][h][:, c, t] for h in range(2)]
                    o = out(4)
                    for j in range(GT):
                        for c in range(KC):
                            ins = mm3(pe, o[:, j * E:(j + 1) * E], x2(c, slice(j * P, j * P + P)),
                                      [wg[h][:, c, :] for h in range(2)], c == 0, c == KC - 1)
                    ins.then_inc(full, 1)
                    o = out(5)
                    for c in range(KC):
                        ins = mm3(pe, o[:, :], [wkv[h][:, c, :] for h in range(2)], x2(c, slice(0, G)),
                                  c == 0, c == KC - 1)
                    ins.then_inc(full, 1)
                    for m in range(4):
                        o = out(6 + m)
                        for c in range(KC):
                            ins = mm3(pe, o[:, :], [wq[h][:, c, m * P:(m + 1) * P] for h in range(2)],
                                      x2(c, slice(0, G)), c == 0, c == KC - 1)
                        ins.then_inc(full, 1)
                    pe.wait_ge(lo_done, g * ITEMS + 6 + RING)
                    for m in range(4):
                        o = out(10 + m)
                        ins = mm3(pe, o[:, :], [wk[h][:, 0, m * P:(m + 1) * P] for h in range(2)],
                                  [lat[h][:, :] for h in range(2)], True, True)
                        ins.then_inc(full, 1)
                    for j in range(GT):
                        o = out(14 + j)
                        ins = mm3(pe, o[:, :], [lat[h][:, j * P:(j + 1) * P] for h in range(2)],
                                  [wv[h][:, 0, :] for h in range(2)], True, True)
                        ins.then_inc(full, 1)


def phase_route(nc, env):
    ctx, sb, ps, sem = scope(nc)
    TE = TILES * E
    with ctx:
        lc = sb("r_lc", [P, TILES, NG, EPG])
        gmax = sb("r_gmax", [P, TILES, NG])
        cmp = sb("r_cmp", [P, TILES, NG])
        rank = sb("r_rank", [P, TILES, NG])
        v8 = sb("r_v8", [P, TILES, 8])
        i8 = sb("r_i8", [P, TILES, 8], U32)
        i8f = sb("r_i8f", [P, TILES, 8])
        ex = sb("r_ex", [P, TILES, TOPK])
        wsum = sb("r_wsum", [P, TILES])
        eid = sb("r_eid", [P, E])
        hot = [sb(f"r_hot{k}", [P, TILES, E]) for k in range(TOPK)]
        hit = sb("r_hit", [P, TILES, E])
        before = sb("r_before", [P, P])
        ones = sb("r_ones", [P, P])
        one_row = sb("r_one_row", [P, TE])
        cnt = sb("r_cnt", [P, E, TILES])
        run = sb("r_run", [P, E, TILES])
        start = sb("r_start", [P, E])
        tot = sb("r_tot", [P, E])
        nt_i = sb("r_nt_i", [P, E], I32)
        nt_s = sb("r_nt_s", [P, E], I32)
        nt = sb("r_nt", [P, E])
        last = sb("r_last", [P, E])
        base = sb("r_base", [P, E])
        pos = sb("r_pos", [P, TILES, E])
        prod = sb("r_prod", [P, TILES, E])
        slot = sb("r_slot", [P, TILES, TOPK])
        first_f = sb("r_first_f", [P, E + 1])
        tokid = sb("r_tokid", [P, TILES])
        tok1 = [sb(f"r_tok1{i}", [P, 1]) for i in range(2)]
        slot6 = [sb(f"r_slot6{i}", [P, TOPK], I32) for i in range(2)]
        NIDS = 3
        HALF = MAXT // NIDS
        zero = sb("r_zero", [HALF, P])
        zrow = sb("r_zrow", [P, D])
        ids = [sb(f"r_ids{i}", [HALF, P]) for i in range(NIDS)]
        pr = ps("r_pr", [P, 2, 512])
        pc = ps("r_pc", [P, 2, 512])
        pt = ps("r_pt", [P, NIDS, 512])

        dve_step, c_ready, e_in, e_out = sem("r_dve"), sem("r_c"), sem("r_e_in"), sem("r_e_out")
        hits, counted, done = sem("r_hits"), sem("r_counted"), sem("r_done")
        zeroed, copied, ids_in, turned = sem("r_zeroed"), sem("r_copied"), sem("r_ids_in"), sem("r_turned")
        scat = [sem(f"r_scat{i}") for i in range(2)]
        tail, passed = sem("r_tail"), sem("r_passed")
        scat_free, scattered = sem("r_scat_free"), sem("r_scattered")
        block = ctx.enter_context(nc.Block())
        te = lambda t: t.rearrange("p t e -> p (t e)")

        @block.gpsimd
        def _(pool):
            c = Chain(pool, c_ready)
            c(pool.iota(eid[:, :], [[1, E]], base=0, channel_multiplier=0,
                        allow_small_or_imprecise_dtypes=True))
            c(pool.iota(tokid[:, :], [[P, TILES]], base=0, channel_multiplier=1,
                        allow_small_or_imprecise_dtypes=True))
            c(pool.memset(ones[:, :], 1.0))
            c(pool.memset(one_row[:, :], 1.0))
            c(pool.memset(zero[:, :], 0.0))
            c(pool.memset(zrow[:, :], 0.0))
            c(pool.memset(before[:, :], 1.0))
            c.wait()
            c(pool.affine_select(out=before[:, :], in_=before[:, :], compare_op=ALU.is_gt, fill=0.0,
                                 base=0, pattern=[[1, P]], channel_multiplier=-1))
            pool.wait_ge(zeroed, 16 * NIDS)
            pool.wait_ge(done, 1)
            pool.sem_inc(scat_free, 2)
            with pool.Fori(0, TILES // 2) as tp:
                for b in range(2):
                    t = 2 * tp + b
                    pool.wait_ge(scat_free, t + 1)
                    pool.tensor_copy(slot6[b][:, :], env.slot_i[:, bass.ds(t, 1), :].rearrange("p a k -> p (a k)"))\
                        .then_inc(copied, 1)
                    pool.tensor_copy(tok1[b][:, :], tokid[:, bass.ds(t, 1)]).then_inc(copied, 1)
                    pool.wait_ge(copied, 2 * t + 2)
                    pool.sem_inc(passed, 1)
                    for k in range(TOPK):
                        pool.indirect_dma_start(
                            env.ids_d, bass.IndirectOffsetOnAxis(ap=slot6[b][:, k:k + 1].bitcast(U32), axis=0),
                            tok1[b][:, :], None).then_inc(scat[b], 16)
                    if b == 1:
                        for bb in range(2):
                            pool.wait_ge(scat[bb], 96 * tp + 96)
                        pool.sem_inc(scat_free, 2)
            pool.sem_inc(scattered, 1)

        @block.sync
        def _(sp):
            sp.wait_ge(c_ready, 8)
            rows = env.ids_d.rearrange("(h r n) a -> h r (n a)", n=P, h=NIDS)
            for h in range(NIDS):
                sp.dma_start(rows[h], zero[:, :]).then_inc(zeroed, 16)
            for i in range(MINTILES, MAXT):
                sp.dma_start(env.ys_d[i * P:(i + 1) * P, :], zrow[:, :]).then_inc(tail, 16)
            sp.wait_ge(tail, 16 * (MAXT - MINTILES))
            sp.wait_ge(scattered, 1)
            for h in range(NIDS):
                sp.dma_start(ids[h][:, :], rows[h]).then_inc(ids_in, 16)

        @block.scalar
        def _(act):
            act.wait_ge(e_in, 1)
            act.activation(ex[:, :, :], v8[:, :, 0:TOPK], ACT.Exp, scale=-1.0).then_inc(e_out, 1)

        @block.tensor
        def _(pe):
            pe.wait_ge(hits, 1)
            pe.wait_ge(c_ready, 8)
            for h in range(2):
                rhs = te(hit[:, :, :])[:, 512 * h:512 * h + 512]
                pe.matmul(pr[:, h, :], before[:, :], rhs, start=True, stop=True)
                ins = pe.matmul(pc[:, h, :], ones[:, :], rhs, start=True, stop=True)
            ins.then_inc(counted, 1)
            pe.wait_ge(ids_in, 16 * NIDS)
            for h in range(NIDS):
                ins = pe.transpose(pt[:, h, 0:HALF], ids[h][:, :], env.ident[0:HALF, 0:HALF])
            ins.then_inc(turned, 1)

        @block.vector
        def _(dve):
            c = Chain(dve, dve_step)

            def do(ins):
                c(ins)
                c.wait()
            do(dve.tensor_scalar(te(lc[:, :, :, :].rearrange("p t g e -> p t (g e)")), te(env.logits[:, :, :]),
                                 SIG_ONE, SIG_ZERO, ALU.min, ALU.max))
            do(dve.tensor_reduce(gmax[:, :, :], lc[:, :, :, :], AX.X, ALU.max))
            do(dve.memset(rank[:, :, :], 0.0))
            for h in range(NG):
                for lo, hi, op in ((0, h, ALU.is_gt), (h + 1, NG, ALU.is_ge)):
                    if lo == hi:
                        continue
                    do(dve.tensor_tensor(cmp[:, :, lo:hi],
                                         gmax[:, :, h:h + 1].to_broadcast([P, TILES, hi - lo]),
                                         gmax[:, :, lo:hi], op))
                    do(dve.tensor_tensor(rank[:, :, lo:hi], rank[:, :, lo:hi], cmp[:, :, lo:hi], ALU.add))
            do(dve.tensor_scalar(rank[:, :, :], rank[:, :, :], TOPG - 0.5, NEG, ALU.is_gt, ALU.mult))
            do(dve.tensor_tensor(lc[:, :, :, :], lc[:, :, :, :],
                                 rank[:, :, :].unsqueeze(3).to_broadcast([P, TILES, NG, EPG]), ALU.add))
            flat = lc[:, :, :, :].rearrange("p t g e -> p t (g e)")
            for t in range(TILES):
                c(dve.max(v8[:, t, :], flat[:, t, :]))
            c.wait()
            for t in range(TILES):
                ins = dve.max_index(i8[:, t, :], v8[:, t, :], flat[:, t, :])
                c(ins)
            c.wait()
            dve.sem_inc(e_in, 1)
            do(dve.tensor_copy(i8f[:, :, :], i8[:, :, :]))
            dve.wait_ge(c_ready, 8)
            for k in range(TOPK):
                c(dve.tensor_tensor(hot[k][:, :, :], i8f[:, :, k:k + 1].to_broadcast([P, TILES, E]),
                                    eid[:, :].unsqueeze(1).to_broadcast([P, TILES, E]), ALU.is_equal))
            c.wait()
            do(dve.tensor_tensor(hit[:, :, :], hot[0][:, :, :], hot[1][:, :, :], ALU.add))
            for k in range(2, TOPK):
                do(dve.tensor_tensor(hit[:, :, :], hit[:, :, :], hot[k][:, :, :], ALU.add))
            dve.sem_inc(hits, 1)
            dve.wait_ge(e_out, 1)
            do(dve.tensor_scalar(ex[:, :, :], ex[:, :, :], 1.0, None, ALU.add))
            do(dve.reciprocal(ex[:, :, :], ex[:, :, :]))
            do(dve.tensor_reduce(wsum[:, :], ex[:, :, :], AX.X, ALU.add))
            do(dve.reciprocal(wsum[:, :], wsum[:, :]))
            do(dve.tensor_tensor(env.wexp[:, :, :], ex[:, :, :],
                                 wsum[:, :].unsqueeze(2).to_broadcast([P, TILES, TOPK]), ALU.mult))
            dve.wait_ge(counted, 1)
            do(dve.tensor_copy(cnt[:, :, :].rearrange("p e t -> p t e"),
                               pc[:, :, :].rearrange("p h (t e) -> p (h t) e", e=E)))
            do(dve.tensor_tensor_scan(run[:, :, :].rearrange("p e t -> p (e t)"), one_row[:, :],
                                      cnt[:, :, :].rearrange("p e t -> p (e t)"), 0.0, ALU.mult, ALU.add))
            c(dve.memset(start[:, 0:1], 0.0))
            do(dve.tensor_copy(start[:, 1:E], run[:, 0:E - 1, TILES - 1]))
            do(dve.tensor_tensor(tot[:, :], run[:, :, TILES - 1], start[:, :], ALU.subtract))
            do(dve.tensor_scalar(nt_i[:, :], tot[:, :], float(P - 1), None, ALU.add))
            do(dve.tensor_scalar(nt_s[:, :], nt_i[:, :], 7, None, ALU.logical_shift_right))
            do(dve.tensor_scalar(nt[:, :], nt_s[:, :], float(MINT), None, ALU.max))
            do(dve.tensor_tensor_scan(last[:, :], one_row[:, 0:E], nt[:, :], 0.0, ALU.mult, ALU.add))
            c(dve.memset(first_f[:, 0:1], 0.0))
            do(dve.tensor_copy(first_f[:, 1:E + 1], last[:, :]))
            c(dve.tensor_copy(env.first[:, :], first_f[:, :]))
            do(dve.tensor_scalar(base[:, :], first_f[:, 0:E], float(P), None, ALU.mult))
            do(dve.tensor_tensor(base[:, :], base[:, :], start[:, :], ALU.subtract))
            do(dve.tensor_tensor(run[:, :, :], run[:, :, :], cnt[:, :, :], ALU.subtract))
            do(dve.tensor_tensor(pos[:, :, :].rearrange("p t e -> p e t"), run[:, :, :],
                                 base[:, :].unsqueeze(2).to_broadcast([P, E, TILES]), ALU.add))
            do(dve.tensor_tensor(te(pos[:, :, :]), te(pos[:, :, :]),
                                 pr[:, :, :].rearrange("p h n -> p (h n)"), ALU.add))
            for k in range(TOPK):
                do(dve.tensor_tensor(prod[:, :, :], pos[:, :, :], hot[k][:, :, :], ALU.mult))
                do(dve.tensor_reduce(slot[:, :, k], prod[:, :, :], AX.X, ALU.add))
            do(dve.tensor_copy(env.slot_i[:, :, :], slot[:, :, :]))
            dve.sem_inc(done, 1)
            dve.wait_ge(turned, 1)
            for h in range(NIDS):
                dve.tensor_copy(env.ids[:, h * HALF:(h + 1) * HALF], pt[:, h, 0:HALF])


def split_weights(nc, name, weights, raw):
    ctx, _, _, sem = scope(nc)
    R = len(raw)
    with ctx:
        w_in = [sem(f"{name}_in{i}") for i in range(R)]
        w_hi, w_used = sem(name + "_hi"), sem(name + "_used")
        block = ctx.enter_context(nc.Block())

        @block.sync
        def _(sp):
            for i, (src, _, c, n) in enumerate(weights):
                if i >= R:
                    sp.wait_ge(w_used, i - R + 1)
                sp.dma_start(raw[i % R][:, 0:c, 0:n], src).then_inc(w_in[i % R], 16)

        @block.scalar
        def _(act):
            for i, (_, dst, c, n) in enumerate(weights):
                act.wait_ge(w_in[i % R], 16 * (i // R + 1))
                act.activation(dst[0], raw[i % R][:, 0:c, 0:n], ACT.Copy).then_inc(w_hi, 1)

        @block.vector
        def _(dve):
            for i, (_, dst, c, n) in enumerate(weights):
                dve.wait_ge(w_hi, i + 1)
                dve.tensor_tensor(dst[1], raw[i % R][:, 0:c, 0:n], f(dst[0]), ALU.subtract).then_inc(w_used, 1)


def phase_attend(nc, env):
    ctx, sb, ps, sem = scope(nc)
    U = 4
    N = U * NH
    HH = NH // 2
    W = 2 * P + PERSIST
    ST = 3 * HD
    with ctx:
        qs = [sb(f"a_q{i}", [ST, NH, P], F32R) for i in range(2)]
        ks = [sb(f"a_k{i}", [ST, NH, P], F32R) for i in range(U)]
        vb = [sb(f"a_v{i}", [P, NH, 2 * HD], F32R) for i in range(U)]
        kp = sb("a_kp", [ST, B, NH, PERSIST], F32R)
        vp = sb("a_vp", [P, B, 2, HH, 2 * HD], F32R)
        mask = [sb(f"a_mask{i}", [P, W]) for i in range(2)]
        sm = [sb(f"a_sm{i}", [P, W]) for i in range(2)]
        nmax = [sb(f"a_nmax{i}", [P, 1]) for i in range(2)]
        pr = [sb(f"a_pr{i}", [P, HH, W]) for i in range(2)]
        pp = [sb(f"a_pp{i}", [P, P]) for i in range(2)]
        rs = [sb(f"a_rs{i}", [P, HH]) for i in range(2)]
        rl = sb("a_rl", [P, HH])
        pT = [[sb(f"a_pT{i}{h}", [P, 2 * P], F32R) for h in range(2)] for i in range(2)]
        ppT = [sb(f"a_ppT{h}", [P, P], F32R) for h in range(2)]
        o1 = sb("a_o1", [P, HH, HD])
        o2 = sb("a_o2", [P, HH, HD])
        o = sb("a_o", [P, NH, HD])
        oT = [sb(f"a_oT{h}", [P, KC, P], F32R) for h in range(2)]
        wo = [sb(f"a_wo{h}", [P, KC, D], F32R) for h in range(2)]
        wraw = sb("a_wraw", [P, KC, D])
        y = [sb(f"a_y{i}", [P, D]) for i in range(2)]
        split_weights(nc, "a_ws", [(env.Wo.rearrange("(c p) n -> p c n", p=P),
                                   [w[:, :, :] for w in wo], KC, D)], [wraw])

        psS = [ps(f"a_psS{i}", [P, D]) for i in range(2)]
        psP = [ps(f"a_psP{i}", [P, D]) for i in range(2)]
        psO = [ps(f"a_psO{i}", [P, HH, 2, HD]) for i in range(2)]
        psX = ps("a_psX", [P, KC, P])
        psY = ps("a_psY", [P, D])

        once, cleared = sem("a_once"), sem("a_cleared")
        pool_passed, dve_passed = sem("a_pool_passed"), sem("a_dve_passed")
        q_in = [sem(f"a_q_in{i}") for i in range(2)]
        kv_in = [sem(f"a_kv_in{i}") for i in range(U)]
        s_full, s_used = sem("a_s_full"), sem("a_s_used")
        p_ready, pT_full = sem("a_p_ready"), sem("a_pT_full")
        pT_hi, pT_split, pv_done = sem("a_pT_hi"), sem("a_pT_split"), sem("a_pv_done")
        o_full, o_used = sem("a_o_full"), sem("a_o_used")
        o_ready = sem("a_o_ready")
        x_full, x_hi, x_split = sem("a_x_full"), sem("a_x_hi"), sem("a_x_split")
        y_full, y_ready = sem("a_y_full"), sem("a_y_ready")
        y_out = [sem(f"a_y_out{i}") for i in range(2)]
        y_free = sem("a_y_free")
        dve_step, pp_ready = sem("a_dve"), sem("a_pp_ready")
        block = ctx.enter_context(nc.Block())
        v_v = env.v_d.rearrange("(i p) n -> i p n", p=P)
        s_v = env.s_d.rearrange("(i p) n -> i p n", p=P)

        def turns(eng, body):
            with eng.Fori(0, B) as b:
                with eng.Fori(0, BT // U) as q:
                    body(b, q, b * BT + q * U)

        EXTRA = {}
        for u in range(U):
            for at_step, what in ((9, ("persT", u, 0)), (11, ("persV", u, 0)), (17, ("persT", u, 1)),
                                  (19, ("persV", u, 1)), (22, ("oT", u, 0)), (24, ("proj", u, 0))):
                EXTRA.setdefault(u * NH + at_step, []).append(what)
        STEPS = range(max(EXTRA) + 1)

        @block.gpsimd
        def _(pool):
            pool.memset(f(vp[:, :, :, :, :]).rearrange("p b a h d -> p (b a h d)"), 0.0).then_inc(cleared, 1)
            pool.memset(f(ks[U - 1][:, :, :]), 0.0).then_inc(cleared, 1)
            pool.memset(f(vb[U - 1][:, :, :]), 0.0).then_inc(cleared, 1)


            def body(b, q, t0):
                def persistent(u, half):
                    n = 2 * (t0 + u) + half
                    pool.wait_ge(x_full, 3 * (t0 + u) + half + 1)
                    pool.wait_ge(p_ready, (t0 + u) * NH + (half + 1) * HH + 2)
                    pool.sem_inc(pool_passed, 1)
                    pool.tensor_copy(pp[half][:, :].rearrange("p (h k) -> p h k", h=HH), pr[half][:, :, 2 * P:W])\
                        .then_inc(pp_ready, 1)

                def store(u):
                    pool.wait_ge(y_ready, t0 + u + 2)
                    pool.dma_start(at(s_v, t0 + u), y[u % 2][:, :]).then_inc(y_out[u % 2], 16)
                    pool.wait_ge(y_out[u % 2], 16 * (b * (BT // 2) + q * (U // 2) + u // 2 + 1))
                    pool.sem_inc(y_free, 1)
                for u in range(U):
                    persistent(u, 0)
                    if u:
                        store(u - 1)
                    persistent(u, 1)
                store(U - 1)
            turns(pool, body)

        @block.sync
        def _(sp):
            sp.wait_ge(cleared, 3)
            for b in range(B):
                for j, h in ((0, 0), (1, 0), (2, 1)):
                    sp.dma_start(f(kp[j * HD:(j + 1) * HD, b, :, :]),
                                 env.qk_d[1, h, :, b * S:b * S + PERSIST].rearrange("(m p) t -> p m t", p=HD))\
                      .then_inc(once, 16)
                for h in range(NH):
                    sp.dma_start(f(vp[PERSIST * (h % HH):PERSIST * (h % HH + 1), b, h // HH, h % HH, :]),
                                 env.v_d[b * S:b * S + PERSIST, 2 * HD * h:2 * HD * (h + 1)]).then_inc(once, 16)

            def body(b, q, t0):
                for u in range(U):
                    sp.wait_ge(pv_done, (t0 + u + 1) * NH)
                    tok = bass.ds((t0 + u) * P, P)
                    src = lambda w, h: env.qk_d[w, h, :, tok].rearrange("(m p) t -> p m t", p=HD)
                    for j, (hq, hk) in enumerate(((0, 0), (1, 0), (0, 1))):
                        sp.dma_start(f(qs[u % 2][j * HD:(j + 1) * HD, :, :]), src(0, hq)).then_inc(q_in[u % 2], 16)
                        sp.dma_start(f(ks[u][j * HD:(j + 1) * HD, :, :]), src(1, hk)).then_inc(kv_in[u], 16)
                    sp.dma_start(f(vb[u][:, :, :]).rearrange("p h d -> p (h d)"), at(v_v, t0 + u))\
                      .then_inc(kv_in[u], 16)
                    sp.dma_start(mask[u % 2][:, :], at(env.mask, q * U + u)).then_inc(q_in[u % 2], 16)
            turns(sp, body)

        def loaded(b, q, u):
            return 64 * (b * (BT // 2) + q * (U // 2) + u // 2 + 1)

        @block.tensor
        def _(pe):
            pe.wait_ge(once, 16 * B * (3 + NH))

            def body(b, q, t0):
                n0 = t0 * NH

                def score(s):
                    u, h = divmod(s, NH)
                    if h == 0:
                        pe.wait_ge(q_in[u % 2], loaded(b, q, u))
                        pe.wait_ge(kv_in[u], 64 * (b * (BT // U) + q + 1))
                    pe.wait_ge(s_used, n0 + s + 1)
                    out, w = psS[s % 2], qs[u % 2][:, h, :]
                    pe.matmul(out[:, 0:P], w, ks[(u - 1) % U][:, h, :], start=True, stop=True)
                    pe.matmul(out[:, P:2 * P], w, ks[u][:, h, :], start=True, stop=True)
                    pe.matmul(out[:, 2 * P:W], w, kp[:, bass.ds(b, 1), h, :].rearrange("p a k -> p (a k)"),
                              start=True, stop=True).then_inc(s_full, 1)

                def turn(s):
                    u, h = divmod(s, NH)
                    pe.wait_ge(p_ready, n0 + s + 3)
                    pe.wait_ge(pT_split, n0 + s + 1)
                    for c in range(2):
                        ins = pe.transpose(psP[s % 2][:, c * P:(c + 1) * P],
                                           pr[(h // HH) % 2][:, h % HH, c * P:(c + 1) * P], env.ident[:, :])
                    ins.then_inc(pT_full, 1)

                def values(s):
                    u, h = divmod(s, NH)
                    half = h // HH
                    pe.wait_ge(pT_split, n0 + s + 3)
                    if h % HH == 0:
                        pe.wait_ge(o_used, 2 * (t0 + u) + half + 1)
                    out = psO[half][:, h % HH, :, :]
                    for k, (c, v, part) in enumerate((c, v, part) for c, v in ((0, vb[(u - 1) % U]), (1, vb[u]))
                                                     for part in (1, 0)):
                        ins = pe.matmul(out, pT[s % 2][part][:, c * P:(c + 1) * P],
                                        v[:, h, :].rearrange("p (a d) -> p a d", a=2),
                                        start=(h % HH == 0 and k == 0), stop=False, skip_group_check=True)
                    ins.then_inc(pv_done, 1)

                def extra(what, u, half):
                    x = 3 * (t0 + u)
                    if what == "persT":
                        pe.wait_ge(x_split, x + half + 1)
                        pe.wait_ge(pp_ready, 2 * (t0 + u) + half + 3)
                        pe.transpose(psX[:, 0, :], pp[half][:, :], env.ident[:, :]).then_inc(x_full, 1)
                    if what == "persV":
                        pe.wait_ge(x_split, x + half + 2)
                        for part in (1, 0):
                            ins = pe.matmul(psO[half][:, :, :, :].rearrange("p h a d -> p (h a d)"), ppT[part][:, :],
                                            vp[:, bass.ds(b, 1), half, :, :].rearrange("p a h d -> p (a h d)"),
                                            start=False, stop=(part == 0), skip_group_check=True)
                        ins.then_inc(o_full, 1)
                    if what == "oT":
                        pe.wait_ge(o_ready, 2 * (t0 + u) + 2)
                        pe.wait_ge(x_split, x + 3)
                        for c in range(KC):
                            ins = pe.transpose(psX[:, c, :], o[:, c * 4:(c + 1) * 4, :].rearrange("p h d -> p (h d)"),
                                               env.ident[:, :])
                        ins.then_inc(x_full, 1)
                    if what == "proj":
                        pe.wait_ge(x_split, x + 4)
                        pe.wait_ge(y_ready, t0 + u + 1)
                        for c in range(KC):
                            ins = mm3(pe, psY[:, :], [oT[h][:, c, :] for h in range(2)],
                                      [wo[h][:, c, :] for h in range(2)], c == 0, c == KC - 1)
                        ins.then_inc(y_full, 1)

                score(0)
                score(1)
                for s in STEPS:
                    if s + 2 < N:
                        score(s + 2)
                    if s < N:
                        turn(s)
                    if 1 <= s <= N:
                        values(s - 1)
                    for e in EXTRA.get(s, []):
                        extra(*e)
            turns(pe, body)

        @block.scalar
        def _(act):
            def body(b, q, t0):
                n0 = t0 * NH

                def exps(s):
                    u, h = divmod(s, NH)
                    half = h // HH
                    if h % HH == 0:
                        act.wait_ge(pp_ready, 2 * (t0 + u) + half + 1)
                        act.wait_ge(o_used, 2 * (t0 + u) + half + 1)
                    act.wait_ge(s_used, n0 + s + 3)
                    act.activation(pr[half][:, h % HH, :], sm[s % 2][:, :], ACT.Exp, bias=nmax[s % 2][:, :],
                                   scale=-1.0, accum_out=rs[half][:, h % HH:h % HH + 1]).then_inc(p_ready, 1)

                def hi(s):
                    act.wait_ge(pv_done, n0 + s + 2 * NH - 1)
                    act.wait_ge(pT_full, n0 + s + 1)
                    act.activation(pT[s % 2][0][:, :], psP[s % 2][:, 0:2 * P], ACT.Copy).then_inc(pT_hi, 1)

                def extra(what, u, half):
                    x = 3 * (t0 + u)
                    if what == "persT":
                        act.wait_ge(o_full, 2 * (t0 + u) + half + 1)
                        act.wait_ge(x_full, x + half + 4)
                        act.activation(ppT[0][:, :], psX[:, 0, :], ACT.Copy).then_inc(x_hi, 1)
                    if what == "oT":
                        act.wait_ge(y_full, t0 + u + 1)
                        act.wait_ge(x_full, x + 6)
                        act.activation(oT[0][:, :, :], psX[:, :, :], ACT.Copy).then_inc(x_hi, 1)

                exps(0)
                for s in STEPS:
                    if s + 1 < N:
                        exps(s + 1)
                    if s < N:
                        hi(s)
                    for e in EXTRA.get(s, []):
                        extra(*e)
            turns(act, body)

        @block.vector
        def _(dve):
            for s, k in ((s_used, 2), (p_ready, 2), (pT_split, 2), (pv_done, 2 * NH), (x_full, 3), (pp_ready, 2), (o_used, 2),
                         (x_split, 1), (o_full, 1), (y_full, 1), (y_ready, 1), (y_free, 2)):
                dve.sem_inc(s, k)

            def body(b, q, t0):
                n0 = t0 * NH
                c = Chain(dve, dve_step, t0 * 4)

                def top(s):
                    u, h = divmod(s, NH)
                    if h == 0:
                        dve.wait_ge(q_in[u % 2], loaded(b, q, u))
                    dve.wait_ge(p_ready, n0 + s + 1)
                    dve.wait_ge(s_full, n0 + s + 1)
                    dve.sem_inc(dve_passed, 1)
                    dve.tensor_tensor_reduce(out=sm[s % 2][:, :], in0=psS[s % 2][:, 0:W], in1=mask[u % 2][:, :],
                                             scale=-SCALE, scalar=3.0e38, op0=ALU.add, op1=ALU.min,
                                             accum_out=nmax[s % 2][:, :]).then_inc(s_used, 1)

                def lo(s):
                    dve.wait_ge(pT_hi, n0 + s + 1)
                    dve.tensor_tensor(pT[s % 2][1][:, :], psP[s % 2][:, 0:2 * P], f(pT[s % 2][0][:, :]),
                                      ALU.subtract).then_inc(pT_split, 1)

                def extra(what, u, half):
                    x = 3 * (t0 + u)
                    if what == "persT":
                        dve.wait_ge(x_hi, x + half + 1)
                        dve.tensor_tensor(ppT[1][:, :], psX[:, 0, :], f(ppT[0][:, :]), ALU.subtract)\
                           .then_inc(x_split, 1)
                    if what == "persV":
                        dve.wait_ge(o_full, 2 * (t0 + u) + half + 2)
                        c(dve.reciprocal(rl[:, :], rs[half][:, :]))
                        c.wait()
                        rb = rl[:, :].unsqueeze(2).to_broadcast([P, HH, HD])
                        c(dve.tensor_tensor(o1[:, :, :], psO[half][:, :, 0, :], rb, ALU.mult))
                        dve.tensor_tensor(o2[:, :, :], psO[half][:, :, 1, :], rb, ALU.mult).then_inc(o_used, 1)
                        dve.wait_ge(o_used, 2 * (t0 + u) + half + 3)
                        dve.tensor_tensor(o[:, half * HH:(half + 1) * HH, :], o1[:, :, :], o2[:, :, :], ALU.add)\
                           .then_inc(o_ready, 1)
                    if what == "oT":
                        dve.wait_ge(x_hi, x + 3)
                        dve.tensor_tensor(oT[1][:, :, :], psX[:, :, :], f(oT[0][:, :, :]), ALU.subtract)\
                           .then_inc(x_split, 1)
                    if what == "proj":
                        dve.wait_ge(y_free, t0 + u + 1)
                        dve.wait_ge(y_full, t0 + u + 2)
                        dve.tensor_copy(y[u % 2][:, :], psY[:, :]).then_inc(y_ready, 1)

                top(0)
                top(1)
                for s in STEPS:
                    if s + 2 < N:
                        top(s + 2)
                    if s < N:
                        lo(s)
                    for e in EXTRA.get(s, []):
                        extra(*e)
            turns(dve, body)


def phase_presplit(nc, env):
    ctx, sb, _, sem = scope(nc)
    with ctx:
        raw = [sb(f"s_raw{i}", [P, KC, 2, P]) for i in range(2)]
        out = [[sb(f"s_out{i}{h}", [P, KC, 2, P], F32R) for h in range(2)] for i in range(2)]
        w_in = [sem(f"s_in{i}") for i in range(2)]
        w_out = [sem(f"s_out{i}") for i in range(2)]
        w_hi, w_lo, raw_free, out_free = sem("s_hi"), sem("s_lo"), sem("s_raw_free"), sem("s_out_free")
        block = ctx.enter_context(nc.Block())

        @block.gpsimd
        def _(pool):
            pool.wait_ge(w_lo, 2)
            with pool.Fori(0, FB // 2) as mp:
                for b in range(2):
                    m = 2 * mp + b
                    pool.wait_ge(w_lo, m + 1)
                    pool.dma_start(raw[b][:, :, :, :], at(env.wgu1, m)).then_inc(w_in[b], 16)

        @block.scalar
        def _(act):
            with act.Fori(0, FB // 2) as mp:
                for b in range(2):
                    m = 2 * mp + b
                    act.wait_ge(out_free, m + 1)
                    act.wait_ge(w_in[b], 16 * mp + 16)
                    act.activation(out[b][0][:, :, :, :], raw[b][:, :, :, :], ACT.Copy).then_inc(w_hi, 1)

        @block.vector
        def _(dve):
            dve.sem_inc(w_lo, 2)
            dve.sem_inc(out_free, 2)
            with dve.Fori(0, FB // 2) as mp:
                for b in range(2):
                    m = 2 * mp + b
                    dve.wait_ge(w_hi, m + 1)
                    dve.tensor_tensor(out[b][1][:, :, :, :], raw[b][:, :, :, :], f(out[b][0][:, :, :, :]),
                                      ALU.subtract).then_inc(w_lo, 1)

        @block.sync
        def _(sp):
            with sp.Fori(0, FB // 2) as mp:
                for b in range(2):
                    m = 2 * mp + b
                    sp.wait_ge(w_lo, m + 3)
                    for h in range(2):
                        sp.dma_start(at(env.wgu1_d[h], m), f(out[b][h][:, :, :, :])).then_inc(w_out[b], 16)
                    sp.wait_ge(w_out[b], 32 * mp + 32)
                    sp.sem_inc(out_free, 1)


def phase_ffn(nc, env, name, xT_d, blocks, last, wgu, down, out_d, final):
    ctx, sb, ps, sem = scope(nc)
    stream = final
    RW = 3 if stream else 1
    with ctx:
        x2 = [[sb(f"{name}_x{i}{h}", [P, KC, G], F32R) for h in range(2)] for i in range(2)]
        wd = [sb(f"{name}_wd{h}", [P, blocks, D], F32R) for h in range(2)]
        if stream:
            gu = [[sb(f"{name}_gu{i}{h}", [P, KC, 2, P], F32R) for h in range(2)] for i in range(RW)]
        else:
            gu = [[sb(f"{name}_gu{h}", [P, KC, 2, SH], F32R) for h in range(2)]]
        sg = [sb(f"{name}_sg{i}", [P, G]) for i in range(2)]
        hv = [sb(f"{name}_h{i}", [P, G]) for i in range(2)]
        h2 = [[sb(f"{name}_hT{i}{h}", [P, G], F32R) for h in range(2)] for i in range(2)]
        y = [sb(f"{name}_y{i}", [P, D]) for i in range(2)]
        if final:
            cmb = [sb(f"{name}_cmb{i}", [P, G]) for i in range(2)]
            m2 = [sb(f"{name}_m{h}", [P, KC, D], F32R) for h in range(2)]
            cb = sb(f"{name}_cb", [P, D])
            x1 = sb(f"{name}_x1", [P, GT, D])
            xn = sb(f"{name}_xn", [P, GT, D])
            stat = sb(f"{name}_stat", [P, GT, 3])
            res = [sb(f"{name}_res{i}", [P, D]) for i in range(2)]
        wctx, wsb, _, _ = scope(nc)
        with wctx:
            raw = [wsb(f"{name}_raw{i}", [P, 2, D]) for i in range(2)]
            ws = []
            full_blocks = blocks if last == P else blocks - 1
            dv = down[0:full_blocks * P, :].rearrange("(c p) n -> p c n", p=P)
            for c in range(0, full_blocks, 2):
                k = min(2, full_blocks - c)
                ws.append((dv[:, c:c + k, :], [w[:, c:c + k, :] for w in wd], k, D))
            if not stream:
                for c in range(KC):
                    for a in range(2):
                        for n0 in (0, SH // 2):
                            ws.append((wgu[:, c, a, n0:n0 + SH // 2].unsqueeze(1),
                                       [w[:, c, a, n0:n0 + SH // 2].unsqueeze(1) for w in gu[0]], 1, SH // 2))
            split_weights(nc, name + "_ws", ws, raw)
            if last != P:
                lw = wsb(f"{name}_rawl", [last, 1, D])
                split_weights(nc, name + "_wl", [(down[full_blocks * P:, :].unsqueeze(1),
                                                  [w[0:last, full_blocks:, :] for w in wd], 1, D)], [lw])
        psG = [ps(f"{name}_psG{i}", [P, G]) for i in range(2)]
        psU = [ps(f"{name}_psU{i}", [P, G]) for i in range(2)]
        psY = [ps(f"{name}_psY{i}", [P, D]) for i in range(GT)]
        x_in = [sem(f"{name}_x_in{i}") for i in range(2)]
        w_in = [sem(f"{name}_w_in{i}") for i in range(RW)]
        gu_full = sem(f"{name}_gu_full")
        sg_ready, h_ready = sem(f"{name}_sg"), sem(f"{name}_h")
        h_hi, h_split = sem(f"{name}_h_hi"), sem(f"{name}_h_split")
        d_done = sem(f"{name}_d_done")
        y_ready, y_free = sem(f"{name}_y_ready"), sem(f"{name}_y_free")
        y_out = [sem(f"{name}_y_out{i}") for i in range(2)]
        dve_step = sem(f"{name}_dve")
        block = ctx.enter_context(nc.Block())
        width = lambda m: P if m < blocks - 1 else last
        routed = lambda m: final and m >= blocks - 2
        NR = 2 + 1 + 2 * GT if final else 0
        XN = 16 * (2 * GT + 1 if final else 2)
        if final:
            m_in, m_ready = sem(f"{name}_m_in"), sem(f"{name}_m_ready")
            x1_in, stat_ready, xn_ready = sem(f"{name}_x1_in"), sem(f"{name}_stat_ready"), sem(f"{name}_xn_ready")
            p_full, p_used = sem(f"{name}_p_full"), sem(f"{name}_p_used")
            res_ready = sem(f"{name}_res_ready")
            proj = [psG[0], psU[0], psG[1], psU[1]]
        out_v = out_d.rearrange("(i p) d -> i p d", p=P)

        @block.sync
        def _(sp):
            with sp.Fori(0, GROUPS // 2) as gp:
                for b in range(2):
                    g = 2 * gp + b
                    sp.wait_ge(gu_full, (g + 1) * blocks + 2)
                    for h in range(2):
                        if final:
                            for j in range(GT):
                                sp.dma_start(f(x2[b][h][:, :, j * P:(j + 1) * P]), at(xT_d[h], g * GT + j))\
                                  .then_inc(x_in[b], 16)
                        else:
                            sp.dma_start(f(x2[b][h][:, :, :]), at(xT_d[h], g)).then_inc(x_in[b], 16)
                    if final:
                        sp.dma_start(cmb[b][:, :], at(env.comb_d.rearrange("(g j) t -> g (j t)", j=GT), g)
                                     .unsqueeze(0).to_broadcast([P, G])).then_inc(x_in[b], 16)
                    if stream:
                        for m in range(blocks):
                            sp.wait_ge(gu_full, g * blocks + m + 2 * blocks + 1 - RW)
                            for h in range(2):
                                sp.dma_start(f(gu[m % RW][h][:, :, :, :]), wgu[h, m]).then_inc(w_in[m % RW], 16)
                            if m == blocks // 2:
                                sp.wait_ge(res_ready, g * GT + 1)
                                sp.dma_start(x1[:, :, :], at(env.x1_d.rearrange("(g j p) d -> g p j d", j=GT, p=P), g))\
                                  .then_inc(x1_in, 16)

        @block.gpsimd
        def _(pool):
            done, buf = (res_ready, res) if final else (y_ready, y)

            def store(g):
                for j in range(GT):
                    pool.wait_ge(done, g * GT + j + 1 + (1 if final else GT))
                    pool.dma_start(at(out_v, g * GT + j), buf[j % 2][:, :]).then_inc(y_out[j % 2], 16)
                    pool.wait_ge(y_out[j % 2], g * (16 * GT // 2) + 16 * (j // 2 + 1))
                    pool.sem_inc(y_free, 1)
            if final:
                with pool.Fori(0, B) as bt:
                    for h in range(2):
                        pool.dma_start(f(m2[h][:, :, :]), at(env.m_d[:, h], bt)).then_inc(m_in, 16)
                    pool.dma_start(cb[:, :], at(env.cb_d, bt)).then_inc(m_in, 16)
                    pool.wait_ge(m_in, 48 * bt + 48)
                    pool.sem_inc(m_ready, GROUPS // B)
                    with pool.Fori(0, GROUPS // B) as g:
                        store(bt * (GROUPS // B) + g)
            else:
                with pool.Fori(0, GROUPS) as g:
                    store(g)

        @block.tensor
        def _(pe):
            with pe.Fori(0, GROUPS // 2) as gp:
                for b in range(2):
                    g = 2 * gp + b
                    m0 = g * blocks

                    def down_of(m):
                        pe.wait_ge(h_split, m0 + m + 1)
                        k = width(m)
                        for j in range(GT):
                            if m == 0:
                                pe.wait_ge(y_ready, g * GT + j + 1)
                            ins = mm3(pe, psY[j][:, :], [h2[m % 2][h][0:k, j * P:(j + 1) * P] for h in range(2)],
                                      [wd[h][0:k, m, :] for h in range(2)], m == 0, m == blocks - 1)
                        ins.then_inc(d_done, 1)
                    pe.wait_ge(x_in[b], XN * (gp + 1))
                    def attend(j):
                        if j % 2 == 0:
                            pe.wait_ge(h_ready, m0 + blocks + 1 + j // 2)
                        for c in range(KC):
                            ins = mm3(pe, proj[j][:, :], [x2[b][h][:, c, j * P:(j + 1) * P] for h in range(2)],
                                      [m2[h][:, c, :] for h in range(2)], c == 0, c == KC - 1)
                        ins.then_inc(p_full, 1)
                    for m in range(blocks):
                        if final and m < 2:
                            pe.wait_ge(p_used, g * GT + 2 * m + 2)
                        if stream:
                            pe.wait_ge(w_in[m % RW], 32 * (g * (blocks // RW) + m // RW + 1))
                        pe.wait_ge(h_ready, m0 + m + 1)
                        k = width(m)
                        for a, dst in ((0, psG), (1, psU)):
                            for c in range(KC):
                                if stream:
                                    w = [gu[m % RW][h][:, c, a, :] for h in range(2)]
                                else:
                                    w = [gu[0][h][:, c, a, m * P:m * P + k] for h in range(2)]
                                ins = mm3(pe, dst[m % 2][0:k, :], w, [x2[b][h][:, c, :] for h in range(2)],
                                          c == 0, c == KC - 1)
                        ins.then_inc(gu_full, 1)
                        if m:
                            down_of(m - 1)
                    if final:
                        pe.wait_ge(m_ready, g + 1)
                        attend(0)
                        attend(1)
                    down_of(blocks - 1)
                    if final:
                        attend(2)
                        attend(3)

        @block.scalar
        def _(act):
            with act.Fori(0, GROUPS) as g:
                m0 = g * blocks

                def hi(m):
                    act.wait_ge(d_done, m0 + m + 1)
                    act.wait_ge(h_ready, m0 + m + 3)
                    k = width(m)
                    act.activation(h2[m % 2][0][0:k, :], hv[m % 2][0:k, :], ACT.Copy).then_inc(h_hi, 1)
                for m in range(blocks):
                    act.wait_ge(gu_full, m0 + m + 1 + 2 * blocks)
                    act.wait_ge(h_ready, m0 + m + 1)
                    k = width(m)
                    act.activation(sg[m % 2][0:k, :], psG[m % 2][0:k, :], ACT.Silu).then_inc(sg_ready, 1)
                    hi(m)
                    if final and m == blocks - 5:
                        act.wait_ge(x1_in, 16 * g + 16)
                        act.wait_ge(stat_ready, g + 1)
                        for j in range(GT):
                            ins = act.activation(xn[:, j, :], x1[:, j, :], ACT.Identity, bias=stat[:, j, 1:2],
                                                 scale=stat[:, j, 0:1])
                        ins.then_inc(xn_ready, 1)
                for j in range(GT):
                    act.wait_ge(d_done, m0 + blocks + 2)
                    act.wait_ge(y_free, g * GT + j + 1)
                    act.activation(y[j % 2][:, :], psY[j][:, :], ACT.Silu if final else ACT.Copy).then_inc(y_ready, 1)

        @block.vector
        def _(dve):
            for s, k in ((gu_full, 2 * blocks), (h_ready, 2), (d_done, 2), (y_ready, GT), (y_free, 2)):
                dve.sem_inc(s, k)
            if final:
                dve.sem_inc(res_ready, 1)
                dve.sem_inc(p_used, GT)
            with dve.Fori(0, GROUPS // 2) as gp:
                for b in range(2):
                    g = 2 * gp + b
                    m0 = g * blocks
                    c = Chain(dve, dve_step, g * NR)
                    for m in range(blocks):
                        if final and m == 4:
                            c(dve.tensor_copy(stat[:, :, :], env.stat[:, bass.ds(g * GT, GT), :]))
                            c.wait()
                            dve.sem_inc(stat_ready, 1)
                        k = width(m)
                        dve.wait_ge(sg_ready, m0 + m + 1)
                        ins = dve.tensor_tensor(hv[m % 2][0:k, :], sg[m % 2][0:k, :], psU[m % 2][0:k, :], ALU.mult)
                        if routed(m):
                            c(ins)
                            c.wait()
                            dve.wait_ge(x_in[b], XN * (gp + 1))
                            ins = dve.tensor_tensor(hv[m % 2][0:k, :], hv[m % 2][0:k, :], cmb[b][0:k, :], ALU.mult)
                        ins.then_inc(h_ready, 1)
                        dve.wait_ge(h_hi, m0 + m + 1)
                        dve.tensor_tensor(h2[m % 2][1][0:k, :], hv[m % 2][0:k, :], f(h2[m % 2][0][0:k, :]),
                                          ALU.subtract).then_inc(h_split, 1)
                    if final:
                        for j in range(GT):
                            r = res[j % 2][:, :]
                            dve.wait_ge(y_free, g * GT + j + 1)
                            dve.wait_ge(p_full, g * GT + j + 1)
                            dve.scalar_tensor_tensor(r, proj[j][:, :], stat[:, j, 2:3], cb[:, :], ALU.mult, ALU.add)\
                               .then_inc(p_used, 1)
                            dve.wait_ge(p_used, g * GT + j + 1 + GT)
                            dve.wait_ge(xn_ready, g + 1)
                            c(dve.tensor_tensor(r, r, xn[:, j, :], ALU.add))
                            c.wait()
                            dve.wait_ge(y_ready, g * GT + j + 1 + GT)
                            c(dve.tensor_tensor(r, r, y[j % 2][:, :], ALU.mult))
                            c.wait()
                            dve.tensor_tensor(r, r, x1[:, j, :], ALU.add).then_inc(res_ready, 1)


def phase_experts(nc, env):
    ctx, sb, ps, sem = scope(nc)
    with ctx:
        raw_gu = [sb(f"e_rawgu{i}", [P, KC, 2, M]) for i in range(2)]
        raw_d = [sb(f"e_rawd{i}", [P, MC, D]) for i in range(2)]
        gu = [[sb(f"e_gu{i}{h}", [P, KC, 2, M], F32R) for h in range(2)] for i in range(2)]
        wd = [[sb(f"e_wd{i}{h}", [P, MC, D], F32R) for h in range(2)] for i in range(2)]
        idx = sb("e_idx", [P, 1], I32)
        xg = sb("e_xg", [P, D])
        xT = [sb(f"e_xT{h}", [P, KC, P], F32R) for h in range(2)]
        sg = sb("e_sg", [P, M])
        hv = sb("e_h", [P, M])
        hT = [sb(f"e_hT{h}", [P, MC, P], F32R) for h in range(2)]
        y = sb("e_y", [P, D])
        psX = ps("e_psX", [P, KC, P])
        psH = ps("e_psH", [P, MC, P])
        psG = ps("e_psG", [P, D])
        psU = ps("e_psU", [P, D])
        psY = ps("e_psY", [P, D])

        CR = 3
        done = lambda i: i + 1 + CR
        cleared, passed = sem("e_cleared"), sem("e_passed")
        w_in = [sem(f"e_w_in{i}") for i in range(2)]
        w_hi, w_split = sem("e_w_hi"), sem("e_w_split")
        idx_ready, x_in = sem("e_idx_ready"), sem("e_x_in")
        xT_full, xT_hi, xT_split = sem("e_xT_full"), sem("e_xT_hi"), sem("e_xT_split")
        gu_full, sg_ready, h_ready = sem("e_gu_full"), sem("e_sg_ready"), sem("e_h_ready")
        hT_full, hT_hi, hT_split = sem("e_hT_full"), sem("e_hT_hi"), sem("e_hT_split")
        y_full, y_ready, y_free, y_out = sem("e_y_full"), sem("e_y_ready"), sem("e_y_free"), sem("e_y_out")
        block = ctx.enter_context(nc.Block())
        ys_v = env.ys_d.rearrange("(i p) d -> i p d", p=P)

        def first_of(eng, e):
            e = slice(e, e + 1) if isinstance(e, int) else bass.ds(e, 1)
            return eng.value_load(env.first[0:1, e], min_val=0, max_val=MAXT)

        def experts(eng, begin, tile, split, load, finish):
            def one(e, half, b, first=False):
                start, end = first_of(eng, e), first_of(eng, e + 1)
                begin(e)
                tile(start, b, None if first else 1 - b, 0)
                tile(start + 1, b, None if first else 1 - b, 1)
                if not (isinstance(e, int) and e == E - 1):
                    split(e + 1, half + b, 1 - b, start)
                with eng.Fori(start + 2, end) as i:
                    tile(i, b, b, 2)
                if not (isinstance(e, int) and e + 3 >= E):
                    load(e + 3, 1 - b)
            load(0, 0)
            load(1, 1)
            split(0, 0, 0, None)
            load(2, 0)
            one(0, 0, 0, True)
            with eng.Fori(0, E // 2 - 2) as ep:
                one(2 * ep + 1, ep, 1)
                one(2 * ep + 2, ep + 1, 0)
            for e in range(E - 3, E):
                one(e, e // 2, e % 2)
            finish(first_of(eng, E), 1)

        nothing = lambda *_: None

        @block.gpsimd
        def _(pool):
            for i in range(2):
                pool.memset(raw_d[i][:, :, :], 0.0).then_inc(cleared, 1)
            total = first_of(pool, E)
            with pool.Fori(0, total) as i:
                pool.wait_ge(xT_full, done(i - 1))
                pool.sem_inc(passed, 1)
                pool.tensor_copy(idx[:, :], env.ids[:, bass.ds(i, 1)]).then_inc(idx_ready, 1)
                pool.wait_ge(idx_ready, i + 1)
                pool.sem_inc(passed, 1)
                pool.indirect_dma_start(xg[:, :], None, env.xn_d,
                                        bass.IndirectOffsetOnAxis(ap=idx[:, :].bitcast(U32), axis=0))\
                    .then_inc(x_in, 16)

        @block.sync
        def _(sp):
            total = first_of(sp, E)
            with sp.Fori(0, total) as i:
                sp.wait_ge(y_ready, done(i))
                sp.dma_start(at(ys_v, i), y[:, :]).then_inc(y_out, 16)
                sp.wait_ge(y_out, 16 * i + 16)
                sp.sem_inc(y_free, 1)

        @block.tensor
        def _(pe):
            def turn_h(i):
                pe.wait_ge(h_ready, done(i))
                pe.wait_ge(hT_split, done(i - 1))
                for c in range(MC):
                    k = P if c < MC - 1 else MR
                    ins = pe.transpose(psH[0:k, c, :], hv[:, c * P:c * P + k], env.ident[:, :])
                ins.then_inc(hT_full, 1)

            def down(i, b):
                pe.wait_ge(hT_split, done(i))
                pe.wait_ge(y_ready, done(i - 1))
                for c in range(MC):
                    k = P if c < MC - 1 else MR
                    ins = mm3(pe, psY[:, :], [hT[h][0:k, c, :] for h in range(2)],
                              [wd[b][h][0:k, c, :] for h in range(2)], c == 0, c == MC - 1)
                ins.then_inc(y_full, 1)

            def tile(i, b, old, j):
                pe.wait_ge(x_in, 16 * i + 16)
                pe.wait_ge(xT_split, done(i - 1))
                for c in range(KC):
                    ins = pe.transpose(psX[:, c, :], xg[:, c * P:(c + 1) * P], env.ident[:, :])
                ins.then_inc(xT_full, 1)
                if old is not None:
                    down(i - 2, old)
                if old is not None or j:
                    turn_h(i - 1)
                pe.wait_ge(xT_split, done(i))
                pe.wait_ge(h_ready, done(i - 1))
                for a, dst in ((0, psG), (1, psU)):
                    for c in range(KC):
                        ins = mm3(pe, dst[:, 0:M], [xT[h][:, c, :] for h in range(2)],
                                  [gu[b][h][:, c, a, :] for h in range(2)], c == 0, c == KC - 1)
                ins.then_inc(gu_full, 1)

            def finish(n, b):
                down(n - 2, b)
                turn_h(n - 1)
                down(n - 1, b)
            experts(pe, lambda e: pe.wait_ge(w_split, e + 1), tile, nothing, nothing, finish)

        @block.scalar
        def _(act):
            def load(e, b):
                if not (isinstance(e, int) and e < 2):
                    act.wait_ge(w_split, e - 1)
                wgt = lambda w: w[e] if isinstance(e, int) else at(w, e)
                for a, w in enumerate((env.w_gate, env.w_up)):
                    act.dma_start(raw_gu[b][:, :, a, :], wgt(w).rearrange("(c p) m -> p c m", p=P)).then_inc(w_in[b], 16)
                act.dma_start(raw_d[b][:, 0:MC - 1, :],
                              wgt(env.w_down)[0:2 * P, :].rearrange("(c p) n -> p c n", p=P)).then_inc(w_in[b], 16)
                act.dma_start(raw_d[b][0:MR, MC - 1, :], wgt(env.w_down)[2 * P:M, :]).then_inc(w_in[b], 16)

            def split(e, half, b, start):
                if start is not None:
                    act.wait_ge(y_full, done(start - 1))
                act.wait_ge(w_in[b], 64 * (half + 1))
                act.activation(gu[b][0][:, :, :, :], raw_gu[b][:, :, :, :], ACT.Copy)
                act.activation(wd[b][0][:, :, :], raw_d[b][:, :, :], ACT.Copy).then_inc(w_hi, 1)

            def hi_h(i):
                act.wait_ge(y_full, done(i - 1))
                act.wait_ge(hT_full, done(i))
                act.activation(hT[0][:, :, :], psH[:, :, :], ACT.Copy).then_inc(hT_hi, 1)

            def tile(i, b, old, j):
                act.wait_ge(gu_full, done(i - 1))
                act.wait_ge(xT_full, done(i))
                act.activation(xT[0][:, :, :], psX[:, :, :], ACT.Copy).then_inc(xT_hi, 1)
                if old is not None or j:
                    hi_h(i - 1)
                act.wait_ge(gu_full, done(i))
                act.wait_ge(h_ready, done(i - 1))
                act.activation(sg[:, :], psG[:, 0:M], ACT.Silu).then_inc(sg_ready, 1)
            act.wait_ge(cleared, 2)
            experts(act, nothing, tile, split, load, lambda n, b: hi_h(n - 1))

        @block.vector
        def _(dve):
            for s in (xT_full, xT_hi, xT_split, gu_full, sg_ready, h_ready, hT_full, hT_hi, hT_split,
                      y_full, y_ready, y_free):
                dve.sem_inc(s, CR)
            dve.memset(psH[:, :, :], 0.0)

            def split(e, half, b, start):
                dve.wait_ge(w_hi, e + 1)
                dve.tensor_tensor(gu[b][1][:, :, :, :], raw_gu[b][:, :, :, :], f(gu[b][0][:, :, :, :]), ALU.subtract)
                dve.tensor_tensor(wd[b][1][:, :, :], raw_d[b][:, :, :], f(wd[b][0][:, :, :]), ALU.subtract)\
                   .then_inc(w_split, 1)

            def lo_h(i):
                dve.wait_ge(hT_hi, done(i))
                dve.tensor_tensor(hT[1][:, :, :], psH[:, :, :], f(hT[0][:, :, :]), ALU.subtract).then_inc(hT_split, 1)

            def out(i):
                dve.wait_ge(y_free, done(i - 1))
                dve.wait_ge(y_full, done(i))
                dve.tensor_copy(y[:, :], psY[:, :]).then_inc(y_ready, 1)

            def tile(i, b, old, j):
                dve.wait_ge(xT_hi, done(i))
                dve.tensor_tensor(xT[1][:, :, :], psX[:, :, :], f(xT[0][:, :, :]), ALU.subtract).then_inc(xT_split, 1)
                if old is not None:
                    out(i - 2)
                if old is not None or j:
                    lo_h(i - 1)
                dve.wait_ge(sg_ready, done(i))
                dve.wait_ge(hT_full, done(i - 1))
                dve.tensor_tensor(hv[:, :], sg[:, :], psU[:, 0:M], ALU.mult).then_inc(h_ready, 1)

            def finish(n, b):
                out(n - 2)
                lo_h(n - 1)
                out(n - 1)
            experts(dve, nothing, tile, split, nothing, finish)


def phase_l1_weights(nc, env):
    ctx, sb, ps, sem = scope(nc)
    with ctx:
        w = sb("i_w", [P, KC, 3, D])
        wc = sb("i_wc", [P, KC, 3, D])
        gamma = sb("i_gamma", [P, KC])
        beta = sb("i_beta", [P, KC])
        brow = sb("i_brow", [1, 3, D])
        ones = sb("i_ones", [P, P])
        mean = sb("i_mean", [P, P])
        betar = sb("i_betar", [P, KC, P])
        bq = sb("i_bq", [P, D])
        psM = [ps(f"i_psM{a}", [P, D]) for a in range(3)]
        psB = [ps(f"i_psB{a}", [P, D]) for a in range(3)]
        psT = [ps(f"i_psT{a}", [P, D]) for a in range(2)]
        loaded, ready, scaled = sem("i_loaded"), sem("i_ready"), sem("i_scaled")
        summed, centred, hi_done, biased = sem("i_summed"), sem("i_centred"), sem("i_hi"), sem("i_biased")
        turned, t_used = sem("i_turned"), sem("i_t_used")
        block = ctx.enter_context(nc.Block())

        @block.sync
        def _(sp):
            sp.dma_start(w[:, :, :, :].rearrange("p c a n -> p c (a n)"), env.W_in.rearrange("(c p) n -> p c n", p=P))\
                .then_inc(loaded, 16)
            sp.dma_start(gamma[:, :], env.gamma).then_inc(loaded, 16)
            sp.dma_start(beta[:, :], env.beta).then_inc(loaded, 16)
            sp.dma_start(brow[:, :, :].rearrange("p a n -> p (a n)"), env.b_in.unsqueeze(0)).then_inc(loaded, 16)

        @block.gpsimd
        def _(pool):
            pool.memset(ones[:, :], 1.0).then_inc(ready, 1)
            pool.memset(mean[:, :], 1.0 / D).then_inc(ready, 1)

        @block.vector
        def _(dve):
            dve.wait_ge(loaded, 64)
            for c in range(KC):
                dve.tensor_scalar(wc[:, c, :, :], w[:, c, :, :], gamma[:, c:c + 1], None, ALU.mult)\
                    .then_inc(scaled, 1)
            dve.wait_ge(ready, 2)
            for c in range(KC):
                dve.tensor_scalar(betar[:, c, :], ones[:, :], beta[:, c:c + 1], None, ALU.mult).then_inc(scaled, 1)
            dve.wait_ge(summed, 1)
            dve.wait_ge(scaled, 2 * KC)
            for c in range(KC):
                for a in range(3):
                    dve.tensor_tensor(wc[:, c, a, :], wc[:, c, a, :], psM[a][:, :], ALU.subtract).then_inc(centred, 1)
            dve.wait_ge(summed, 2)
            dve.tensor_copy(bq[:, :], psB[0][:, :]).then_inc(biased, 1)
            for a in range(2):
                dve.tensor_copy(env.bkv[:, a, :], psB[1 + a][:, :])
            for c in range(KC):
                dve.wait_ge(hi_done, c + 1)
                dve.tensor_tensor(env.wkv1[1][:, c, :, :], wc[:, c, 1:3, :], f(env.wkv1[0][:, c, :, :]), ALU.subtract)
            for n in range(KC + 1):
                dve.wait_ge(turned, n + 1)
                src = psT[n % 2][:, :].rearrange("p (c k) -> p c k", c=KC)
                dst = env.wqT[:, n, :].rearrange("p (c k) -> p c k", c=KC) if n < KC else env.bqT[:, :, :]
                dve.tensor_copy(dst, src).then_inc(t_used, 1)

        @block.scalar
        def _(act):
            for c in range(KC):
                act.wait_ge(centred, 3 * c + 3)
                act.activation(env.wkv1[0][:, c, :, :], wc[:, c, 1:3, :], ACT.Copy).then_inc(hi_done, 1)

        @block.tensor
        def _(pe):
            pe.wait_ge(scaled, 2 * KC)
            pe.wait_ge(ready, 2)
            for a in range(3):
                for c in range(KC):
                    ins = pe.matmul(psM[a][:, :], mean[:, :], wc[:, c, a, :], start=c == 0, stop=c == KC - 1)
            ins.then_inc(summed, 1)
            for a in range(3):
                for c in range(KC):
                    pe.matmul(psB[a][:, :], betar[:, c, :], w[:, c, a, :], start=c == 0, stop=False)
                ins = pe.matmul(psB[a][:, :], ones[0:1, :], brow[:, a, :], start=False, stop=True)
            ins.then_inc(summed, 1)
            for n in range(KC + 1):
                if n >= 2:
                    pe.wait_ge(t_used, n - 1)
                pe.wait_ge(centred, 3 * KC) if n < KC else pe.wait_ge(biased, 1)
                for c in range(KC):
                    src = wc[:, c, 0, n * P:(n + 1) * P] if n < KC else bq[:, c * P:(c + 1) * P]
                    ins = pe.transpose(psT[n % 2][:, c * P:(c + 1) * P], src, env.ident[:, :])
                ins.then_inc(turned, 1)


def phase_combine(nc, env):
    ctx, sb, ps, sem = scope(nc)
    with ctx:
        y6 = [sb(f"c_y6{i}", [P, TOPK, D]) for i in range(2)]
        slot6 = [sb(f"c_slot6{i}", [P, TOPK], I32) for i in range(2)]
        w6 = sb("c_w6", [P, TOPK])
        sh, s_in, x = ([sb(f"c_{n}{i}", [P, D]) for i in range(2)] for n in ("sh", "s", "x"))
        acc = sb("c_acc", [P, D])
        g = sb("c_g", [P, D])
        x1 = [sb(f"c_x1{i}", [P, D]) for i in range(2)]
        xn = [sb(f"c_xn{i}", [P, D]) for i in range(2)]
        st = sb("c_st", [P, 6])
        mv = sb("c_mv", [P, 2])
        var = sb("c_var", [P, 1])
        var2 = [sb(f"c_var2{i}", [P, 1]) for i in range(2)]
        stat = [sb(f"c_stat{i}", [P, 3]) for i in range(2)]
        r, nmr, r2 = ([s[:, i:i + 1] for s in stat] for i in range(3))
        tmp, tmp_2, tmp_n = (sb("c_" + n, [P, 1]) for n in ("tmp", "tmp_2", "tmp_n"))
        xT = [[sb(f"c_xT{i}{h}", [P, KC, P], F32R) for h in range(2)] for i in range(2)]
        wr = [sb(f"c_wr{h}", [P, KC, NROUTED], F32R) for h in range(2)]
        wr_raw = sb("c_wr_raw", [P, KC, NROUTED])
        trig = [sb(f"c_trig{i}", [P, 2, 2 * RH]) for i in range(2)]
        kv = [sb(f"c_kv{i}", [P, 2, D]) for i in range(2)]
        rc = sb("c_rc", [P, 2, 2 * RH])
        rs = sb("c_rs", [P, 2, RH, 2])
        prod = [sb(f"c_prod{i}", [P, D]) for i in range(2)]
        sq = sb("c_sq", [P, 2, D])
        n2 = [sb(f"c_n2{i}", [P, 2]) for i in range(2)]
        nn = [sb(f"c_nn{i}", [P, 1]) for i in range(2)]
        rn = [sb(f"c_rn{i}", [P, 1]) for i in range(2)]
        psX = [ps(f"c_psX{i}", [P, KC, P]) for i in range(2)]
        psK = [ps(f"c_psK{i}", [P, 2, D]) for i in range(2)]
        psL = ps("c_psL", [P, NROUTED])
        psA = ps("c_psA", [P, KC])

        CR = 2
        done = lambda i: i + 1 + CR
        q_acc, q_g, q_x1, q_var, q_root, q_norm = (sem("c_" + n) for n in ("q_acc", "q_g", "q_x1", "q_var", "q_root", "q_norm"))
        q_root2, q_xn, q_x_full, q_x_hi, q_x_split = (sem("c_" + n) for n in ("q_root2", "q_xn", "q_x_full", "q_x_hi", "q_x_split"))
        q_kv_full, q_kv, q_sq, q_nn, q_n_root, q_rn = (sem("c_" + n) for n in ("q_kv_full", "q_kv", "q_sq", "q_nn", "q_n_root", "q_rn"))
        q_prod, q_a_full, q_a_used, q_l_used, q_out = (sem("c_" + n) for n in ("q_prod", "q_a_full", "q_a_used", "q_l_used", "q_out"))
        credited = (q_acc, q_g, q_x1, q_var, q_root, q_norm, q_root2, q_xn, q_x_full, q_x_hi, q_x_split, q_kv_full,
                    q_kv, q_sq, q_nn, q_n_root, q_rn, q_prod, q_a_full, q_a_used, q_l_used, q_out)
        ld_in = [sem(f"c_ld_in{i}") for i in range(2)]
        y_in = [sem(f"c_y_in{i}") for i in range(2)]
        trig_in = [sem(f"c_trig_in{i}") for i in range(2)]
        x1_out = [sem(f"c_x1_out{i}") for i in range(2)]
        xT_out = [sem(f"c_xT_out{i}") for i in range(2)]
        copied, passed, rot = sem("c_copied"), sem("c_passed"), sem("c_rot")
        step_1, step_2, step_n = sem("c_step_1"), sem("c_step_2"), sem("c_step_n")
        wr_in, wr_hi, wr_split = sem("c_wr_in"), sem("c_wr_hi"), sem("c_wr_split")
        block = ctx.enter_context(nc.Block())
        tiles = lambda d: d.rearrange("(i p) d -> i p d", p=P)

        def loop(eng, first, second, ahead=1):
            for t in range(ahead):
                first(t, t % 2, t // 2)
            for t in (0, 1):
                first(t + ahead, (t + ahead) % 2, (t + ahead) // 2)
                second(t, t, 0)
            last = (TILES - 1 - ahead) // 2
            with eng.Fori(1, last) as tp:
                for b in range(2):
                    t = b + ahead
                    first(2 * tp + t, t % 2, tp + t // 2)
                    second(2 * tp + b, b, tp)
            for t in range(2 * last, TILES):
                if t + ahead < TILES:
                    first(t + ahead, (t + ahead) % 2, (t + ahead) // 2)
                second(t, t % 2, t // 2)

        one = lambda t: slice(t, t + 1) if isinstance(t, int) else bass.ds(t, 1)
        pick = lambda d, t: d[t] if isinstance(t, int) else at(d, t)

        @block.sync
        def _(sp):
            sp.dma_start(wr_raw[:, :, :], env.router_w.rearrange("(c p) n -> p c n", p=P)).then_inc(wr_in, 16)

            def rotation(t, b):
                sp.dma_start(trig[b][:, :, :], pick(env.trig, t)).then_inc(trig_in[b], 16)

            def first(t, b, tp):
                sp.wait_ge(q_x1, done(t - 2))
                for dst, src in ((sh, env.sh_d), (s_in, env.s_d), (x, env.x)):
                    sp.dma_start(dst[b][:, :], pick(tiles(src), t)).then_inc(ld_in[b], 16)

            def second(t, b, tp):
                sp.wait_ge(q_x1, done(t))
                sp.dma_start(pick(tiles(env.x1_d), t), x1[b][:, :]).then_inc(x1_out[b], 16)
                sp.wait_ge(q_x_split, done(t))
                for h in range(2):
                    sp.dma_start(pick(env.xT1_d[h], t), f(xT[b][h][:, :, :])).then_inc(xT_out[b], 16)
                sp.wait_ge(x1_out[b], 16 * tp + 16)
                sp.wait_ge(xT_out[b], 32 * tp + 32)
                sp.sem_inc(q_out, 1)
                sp.wait_ge(q_prod, done(t))
                if not isinstance(t, int) or t + 2 < TILES:
                    rotation(t + 2, b)
            rotation(0, 0)
            rotation(1, 1)
            loop(sp, first, second, 3)

        @block.gpsimd
        def _(pool):
            def first(t, b, tp):
                pool.wait_ge(q_acc, done(t - 2))
                pool.sem_inc(passed, 1)
                pool.tensor_copy(slot6[b][:, :], env.slot_i[:, one(t), :].rearrange("p a k -> p (a k)"))\
                    .then_inc(copied, 1)
                pool.wait_ge(copied, t + 1)
                pool.sem_inc(passed, 1)
                for k in range(TOPK):
                    pool.indirect_dma_start(y6[b][:, k, :], None, env.ys_d,
                                            bass.IndirectOffsetOnAxis(ap=slot6[b][:, k:k + 1].bitcast(U32), axis=0))\
                        .then_inc(y_in[b], 16)

            def second(t, b, tp):
                pool.wait_ge(trig_in[b], 16 * tp + 16)
                pool.wait_ge(q_kv, done(t))
                pool.tensor_tensor(rc[:, :, :], kv[b][:, :, 0:2 * RH],
                                   trig[b][:, 0:1, :].to_broadcast([P, 2, 2 * RH]), ALU.mult).then_inc(rot, 1)
                pairs = kv[b][:, :, 0:2 * RH].rearrange("p a (i o) -> p a i o", o=2)
                sines = trig[b][:, 1:2, :].rearrange("p a (i o) -> p a i o", o=2)
                for o in range(2):
                    pool.tensor_tensor(rs[:, :, :, o], pairs[:, :, :, 1 - o],
                                       sines[:, :, :, o].to_broadcast([P, 2, RH]), ALU.mult).then_inc(rot, 1)
                pool.wait_ge(rot, 4 * t + 3)
                pool.tensor_tensor(rc[:, :, :], rc[:, :, :], rs[:, :, :, :].rearrange("p a i o -> p a (i o)"), ALU.add)\
                    .then_inc(rot, 1)
                pool.wait_ge(q_a_full, done(t - 2))
                pool.tensor_tensor(prod[b][:, 2 * RH:D], kv[b][:, 0, 2 * RH:D], kv[b][:, 1, 2 * RH:D], ALU.mult)
                pool.wait_ge(rot, 4 * t + 4)
                pool.tensor_tensor(prod[b][:, 0:2 * RH], rc[:, 0, :], rc[:, 1, :], ALU.mult).then_inc(q_prod, 1)
            loop(pool, first, second, 3)

        @block.scalar
        def _(act):
            act.wait_ge(wr_in, 16)
            act.activation(wr[0][:, :, :], wr_raw[:, :, :], ACT.Copy).then_inc(wr_hi, 1)

            def first(t, b, tp):
                act.wait_ge(q_x1, done(t - 1))
                act.wait_ge(q_acc, done(t))
                act.activation(g[:, :], acc[:, :], ACT.Silu).then_inc(q_g, 1)
                act.wait_ge(q_var, done(t))
                act.wait_ge(q_xn, done(t - 2))
                act.activation(r[b][:, :], var[:, :], ACT.Sqrt).then_inc(q_root, 1)
                act.wait_ge(q_norm, done(t))
                act.wait_ge(q_x_full, done(t - 2))
                act.activation(xn[b][:, :], x1[b][:, :], ACT.Identity, bias=nmr[b][:, :], scale=r[b][:, :])\
                    .then_inc(q_xn, 1)
                act.wait_ge(q_kv, done(t - 2))
                act.activation(r2[b][:, :], var2[b][:, :], ACT.Sqrt).then_inc(q_root2, 1)

            def n_root(t, b):
                act.wait_ge(q_a_full, done(t - 2))
                act.wait_ge(q_nn, done(t))
                act.activation(rn[b][:, :], nn[b][:, :], ACT.Sqrt).then_inc(q_n_root, 1)

            def second(t, b, tp):
                if not isinstance(t, int) or t:
                    n_root(t - 1, 1 - b)
                act.wait_ge(q_x_full, done(t))
                act.wait_ge(q_out, done(t - 2))
                act.activation(xT[b][0][:, :, :], psX[b][:, :, :], ACT.Copy).then_inc(q_x_hi, 1)
                act.wait_ge(q_kv, done(t))
                for a in range(2):
                    ins = act.activation(sq[:, a, :], kv[b][:, a, :], ACT.Square, accum_out=n2[b][:, a:a + 1])
                ins.then_inc(q_sq, 1)
            loop(act, first, second)
            n_root(TILES - 1, 1)

        @block.vector
        def _(dve):
            for s in credited:
                dve.sem_inc(s, CR)
            dve.wait_ge(wr_hi, 1)
            dve.tensor_tensor(wr[1][:, :, :], wr_raw[:, :, :], f(wr[0][:, :, :]), ALU.subtract).then_inc(wr_split, 1)
            N1, N2, NN = 17, 5, 5

            def first(t, b, tp):
                c = Chain(dve, step_1, t * N1)
                dve.wait_ge(ld_in[b], 48 * tp + 48)
                dve.wait_ge(y_in[b], 16 * TOPK * (tp + 1))
                c(dve.tensor_copy(w6[:, :], env.wexp[:, one(t), :].rearrange("p a k -> p (a k)")))
                c.wait()
                dve.wait_ge(q_g, done(t - 1))
                for k in range(TOPK):
                    src = sh[b] if k == 0 else acc
                    ins = dve.scalar_tensor_tensor(acc[:, :], y6[b][:, k, :], w6[:, k:k + 1], src[:, :],
                                                   ALU.mult, ALU.add)
                    if k < TOPK - 1:
                        c(ins)
                        c.wait()
                ins.then_inc(q_acc, 1)
                dve.wait_ge(q_g, done(t))
                c(dve.tensor_tensor(s_in[b][:, :], s_in[b][:, :], g[:, :], ALU.mult))
                c.wait()
                dve.wait_ge(q_out, done(t - 2))
                dve.wait_ge(q_xn, done(t - 2))
                dve.tensor_tensor(x1[b][:, :], s_in[b][:, :], x[b][:, :], ALU.add).then_inc(q_x1, 1)
                dve.wait_ge(q_x1, done(t))
                c(dve.bn_stats(st[:, :], x1[b][:, :]))
                c.wait()
                c(dve.memset(tmp[:, :], 0.0))
                c(dve.bn_aggr(mv[:, :], st[:, :]))
                c.wait()
                dve.tensor_scalar(var[:, :], mv[:, 1:2], EPS, None, ALU.add).then_inc(q_var, 1)
                dve.wait_ge(q_root, done(t))
                rstd_chain(dve, c, var[:, :], r[b], tmp)
                dve.wait_ge(q_root2, done(t - 2))
                c(dve.scalar_tensor_tensor(var2[b][:, :], r[b][:, :], r[b][:, 0:1], mv[:, 1:2], ALU.mult, ALU.mult))
                c.wait()
                c(dve.tensor_scalar(var2[b][:, :], var2[b][:, :], EPS, None, ALU.add))
                c.wait()
                dve.tensor_scalar(nmr[b][:, :], mv[:, 0:1], r[b][:, 0:1], -1.0, ALU.mult, ALU.mult).then_inc(q_norm, 1)
                assert c.n == N1, c.n

            def norms(t, b):
                dve.wait_ge(q_sq, done(t))
                dve.tensor_tensor(nn[b][:, :], n2[b][:, 0:1], n2[b][:, 1:2], ALU.mult).then_inc(q_nn, 1)

            def over_norms(t, b):
                c = Chain(dve, step_n, t * NN)
                dve.wait_ge(q_n_root, done(t))
                rstd_chain(dve, c, nn[b][:, :], rn[b], tmp_n)
                dve.sem_inc(q_rn, 1)

            def similar(t):
                dve.wait_ge(q_a_full, done(t))
                dve.tensor_copy(env.aparts[:, one(t), :].rearrange("p a k -> p (a k)"), psA[:, :]).then_inc(q_a_used, 1)

            def second(t, b, tp):
                some = not isinstance(t, int) or t
                if some:
                    norms(t - 1, 1 - b)
                c = Chain(dve, step_2, t * N2)
                dve.wait_ge(q_root2, done(t))
                rstd_chain(dve, c, var2[b][:, :], r2[b], tmp_2)
                if some:
                    over_norms(t - 1, 1 - b)
                dve.wait_ge(q_x_hi, done(t))
                dve.tensor_tensor(xT[b][1][:, :, :], psX[b][:, :, :], f(xT[b][0][:, :, :]), ALU.subtract)\
                   .then_inc(q_x_split, 1)
                if not isinstance(t, int) or t > 1:
                    similar(t - 2)
                dve.tensor_copy(env.stat[:, one(t), :].rearrange("p a k -> p (a k)"), stat[b][:, :])
                dve.wait_ge(q_prod, done(t - 2))
                dve.wait_ge(q_kv_full, done(t))
                dve.scalar_tensor_tensor(kv[b][:, :, :], psK[b][:, :, :], r2[b][:, 0:1], env.bkv[:, :, :],
                                         ALU.mult, ALU.add).then_inc(q_kv, 1)
                dve.tensor_copy(env.logits1[:, one(t), :].rearrange("p a k -> p (a k)"), psL[:, :]).then_inc(q_l_used, 1)
            loop(dve, first, second)
            norms(TILES - 1, 1)
            over_norms(TILES - 1, 1)
            similar(TILES - 2)
            similar(TILES - 1)

        @block.tensor
        def _(pe):
            pe.wait_ge(wr_split, 1)

            def first(t, b, tp):
                pass

            def sums(t, b):
                pe.wait_ge(q_prod, done(t))
                pe.wait_ge(q_rn, done(t))
                pe.wait_ge(q_a_used, done(t - 1))
                for c in range(KC):
                    ins = pe.matmul(psA[:, c:c + 1], prod[b][:, c * P:(c + 1) * P], rn[b][:, :], start=True, stop=True)
                ins.then_inc(q_a_full, 1)

            def second(t, b, tp):
                pe.wait_ge(q_x_split, done(t - 2))
                pe.wait_ge(q_xn, done(t))
                for c in range(KC):
                    ins = pe.transpose(psX[b][:, c, :], xn[b][:, c * P:(c + 1) * P], env.ident[:, :])
                ins.then_inc(q_x_full, 1)
                if not isinstance(t, int) or t:
                    sums(t - 1, 1 - b)
                pe.wait_ge(q_x_split, done(t))
                pe.wait_ge(q_l_used, done(t - 1))
                for c in range(KC):
                    mm3(pe, psL[:, :], [xT[b][h][:, c, :] for h in range(2)], [wr[h][:, c, :] for h in range(2)],
                        c == 0, c == KC - 1)
                pe.wait_ge(q_kv, done(t - 2))
                for a in range(2):
                    for c in range(KC):
                        ins = mm3(pe, psK[b][:, a, :], [xT[b][h][:, c, :] for h in range(2)],
                                  [env.wkv1[h][:, c, a, :] for h in range(2)], c == 0, c == KC - 1)
                ins.then_inc(q_kv_full, 1)
            loop(pe, first, second)
            sums(TILES - 1, 1)


def phase_similarity(nc, env):
    ctx, sb, ps, sem = scope(nc)
    with ctx:
        wout = sb("m_wout", [P, KC, D])
        aw = [sb(f"m_aw{i}", [P, KC, D]) for i in range(B)]
        a = sb("m_a", [P, B, KC])
        bout = sb("m_bout", [1, D])
        ones = sb("m_ones", [1, P])
        hi = [sb(f"m_hi{i}", [P, KC, D], F32R) for i in range(B)]
        lo = [sb(f"m_lo{i}", [P, KC, D], F32R) for i in range(B)]
        cb = sb("m_cb", [P, B, D])
        v8 = sb("m_v8", [P, TILES, 8])
        e = sb("m_e", [P, TILES])
        w0 = sb("m_w0", [P, TILES])
        comb = sb("m_comb", [P, TILES])
        rows = sb("m_rows", [TILES, P])
        psM = [ps(f"m_psM{i}", [P, D]) for i in range(4)]
        psC = [ps(f"m_psC{i}", [P, D]) for i in range(B)]
        psT = ps("m_psT", [TILES, P])
        loaded, ready, dve_step = sem("m_loaded"), sem("m_ready"), sem("m_dve")
        diff, exped, combined, turned = sem("m_diff"), sem("m_exped"), sem("m_combined"), sem("m_turned")
        scaled, full, m_hi, m_used = sem("m_scaled"), sem("m_full"), sem("m_m_hi"), sem("m_m_used")
        c_full, c_ready, rows_ready, out = sem("m_c_full"), sem("m_c_ready"), sem("m_rows_ready"), sem("m_out")
        block = ctx.enter_context(nc.Block())

        @block.gpsimd
        def _(pool):
            pool.memset(ones[:, :], 1.0).then_inc(ready, 1)

        @block.sync
        def _(sp):
            sp.dma_start(wout[:, :, :], env.W_out.rearrange("(c p) n -> p c n", p=P)).then_inc(loaded, 16)
            sp.dma_start(bout[:, :], env.b_out.unsqueeze(0)).then_inc(loaded, 16)
            sp.wait_ge(rows_ready, 1)
            sp.dma_start(env.comb_d, rows[:, :]).then_inc(out, 16)
            for b in range(B):
                sp.wait_ge(c_ready, b + 1)
                sp.dma_start(env.cb_d[b], cb[:, b, :]).then_inc(out, 16)
                sp.wait_ge(m_used, KC * (b + 1))
                sp.dma_start(env.m_d[b, 0], f(hi[b][:, :, :])).then_inc(out, 16)
                sp.dma_start(env.m_d[b, 1], f(lo[b][:, :, :])).then_inc(out, 16)
            sp.wait_ge(out, 16 * (1 + 3 * B))

        @block.vector
        def _(dve):
            c = Chain(dve, dve_step)
            c(dve.tensor_reduce(a[:, :, :], env.aparts[:, :, :].rearrange("p (b t) k -> p b k t", b=B), AX.X, ALU.add))
            c.wait()
            c(dve.tensor_scalar(a[:, :, :], a[:, :, :], 0.5, 0.5, ALU.mult, ALU.add))
            c.wait()
            dve.wait_ge(loaded, 32)
            for b in range(B):
                for n in range(KC):
                    dve.tensor_scalar(aw[b][:, n, :], wout[:, n, :], a[:, b, n:n + 1], None, ALU.mult)\
                       .then_inc(scaled, 1)
            for t in range(TILES):
                c(dve.max(v8[:, t, :], env.logits1[:, t, :]))
            c.wait()
            dve.tensor_tensor(e[:, :], v8[:, :, 1], v8[:, :, 0], ALU.subtract).then_inc(diff, 1)
            dve.wait_ge(exped, 1)
            c(dve.tensor_scalar(w0[:, :], e[:, :], 1.0, None, ALU.add))
            c.wait()
            c(dve.reciprocal(w0[:, :], w0[:, :]))
            c.wait()
            c(dve.tensor_tensor(e[:, :], e[:, :], w0[:, :], ALU.mult))
            c.wait()
            dve.tensor_tensor(comb[:, :], e[:, :], w0[:, :], ALU.add).then_inc(combined, 1)
            for b in range(B):
                for k in range(KC):
                    dve.wait_ge(m_hi, KC * b + k + 1)
                    dve.tensor_tensor(lo[b][:, k, :], psM[k][:, :], f(hi[b][:, k, :]), ALU.subtract).then_inc(m_used, 1)
                dve.wait_ge(c_full, b + 1)
                dve.tensor_copy(cb[:, b, :], psC[b][:, :]).then_inc(c_ready, 1)
            dve.wait_ge(turned, 1)
            dve.tensor_copy(rows[:, :], psT[:, :]).then_inc(rows_ready, 1)

        @block.scalar
        def _(act):
            act.wait_ge(diff, 1)
            act.activation(e[:, :], e[:, :], ACT.Exp).then_inc(exped, 1)
            for b in range(B):
                for k in range(KC):
                    act.wait_ge(full, KC * b + k + 1)
                    act.activation(hi[b][:, k, :], psM[k][:, :], ACT.Copy).then_inc(m_hi, 1)

        @block.tensor
        def _(pe):
            for b in range(B):
                pe.wait_ge(scaled, KC * (b + 1))
                for k in range(KC):
                    if b:
                        pe.wait_ge(m_used, KC * (b - 1) + k + 1)
                    for n in range(KC):
                        ins = pe.matmul(psM[k][:, :], env.wqT[:, n, k * P:(k + 1) * P], aw[b][:, n, :],
                                        start=n == 0, stop=n == KC - 1)
                    ins.then_inc(full, 1)
                for n in range(KC):
                    pe.matmul(psC[b][:, :], env.bqT[:, n, :], aw[b][:, n, :], start=n == 0, stop=False)
                if b == 0:
                    pe.wait_ge(ready, 1)
                    pe.wait_ge(loaded, 32)
                pe.matmul(psC[b][:, :], ones[:, :], bout[:, :], start=False, stop=True).then_inc(c_full, 1)
            pe.wait_ge(combined, 1)
            pe.transpose(psT[:, :], comb[:, :], env.ident[:, :]).then_inc(turned, 1)


def program(nc, env):
    dram = lambda name, shape, dt=F32: nc.dram_tensor(name, shape, dt, kind="Internal").ap()
    env.xn_d = dram("xn_d", [T, D])
    env.qk_d = dram("qk_d", [2, 2, D, T])
    env.v_d = dram("v_d", [T, NH * 2 * HD])
    env.xT_d = dram("xT_d", [2, GROUPS, P, KC, G])
    env.ids_d = dram("ids_d", [MAXT * P, 1])
    env.s_d = dram("s_d", [T, D])
    env.sh_d = dram("sh_d", [T, D])
    env.ys_d = dram("ys_d", [MAXT * P, D])
    env.x1_d = dram("x1_d", [T, D])
    env.xT1_d = dram("xT1_d", [2, TILES, P, KC, P])
    env.wgu1_d = dram("wgu1_d", [2, FB, P, KC, 2, P])
    env.comb_d = dram("comb_d", [TILES, P])
    env.m_d = dram("m_d", [B, 2, P, KC, D])
    env.cb_d = dram("cb_d", [B, P, D])
    ctx = ExitStack()
    with ctx:
        sb = lambda name, shape, dt=F32: ctx.enter_context(nc.sbuf_tensor(name, shape, dt))
        env.ident = sb("ident", [P, P])
        env.stat = sb("stat", [P, TILES, 3])
        env.aparts = sb("aparts", [P, TILES, KC])
        env.logits1 = sb("logits1", [P, TILES, NROUTED])
        with ExitStack() as layer0:
            sb0 = lambda name, shape, dt=F32: layer0.enter_context(nc.sbuf_tensor(name, shape, dt))
            env.logits = sb0("logits", [P, TILES, E])
            env.slot_i = sb0("slot_i", [P, TILES, TOPK], I32)
            env.wexp = sb0("wexp", [P, TILES, TOPK])
            env.ids = sb0("ids", [P, MAXT], I32)
            env.first = sb0("first", [P, E + 1], I32)
            phase_front(nc, env)
            phase_route(nc, env)
            phase_attend(nc, env)
            phase_ffn(nc, env, "b", env.xT_d, SHB, SHR, env.wgu0, env.down0, env.sh_d, False)
            phase_experts(nc, env)
            phase_presplit(nc, env)
            with ExitStack() as similar:
                sb1 = lambda name, shape, dt=F32: similar.enter_context(nc.sbuf_tensor(name, shape, dt))
                env.wqT = sb1("wqT", [P, KC, D])
                env.bqT = sb1("bqT", [P, KC, P])
                with ExitStack() as keys:
                    sb2 = lambda name, shape, dt=F32: keys.enter_context(nc.sbuf_tensor(name, shape, dt))
                    env.wkv1 = [sb2(f"wkv1{h}", [P, KC, 2, D], F32R) for h in range(2)]
                    env.bkv = sb2("bkv", [P, 2, D])
                    phase_l1_weights(nc, env)
                    phase_combine(nc, env)
                phase_similarity(nc, env)
        phase_ffn(nc, env, "d", env.xT1_d, FB, P, env.wgu1_d, env.down1, env.out, True)


_INS = ["x", "Wq", "Wkv", "Wk", "Wv", "Wo", "gate_w", "w_gate", "w_up", "w_down", "wgu0", "down0", "mask",
        "W_in", "b_in", "W_out", "b_out", "gamma", "beta", "router_w", "wgu1", "down1", "trig"]


def rotation_table():
    inv = (np.float32(1.0) / np.float32(10000.0) ** (np.arange(0, 2 * RH, 2, dtype=np.float32) / np.float32(2 * RH)))
    ang = np.arange(S, dtype=np.float32)[:, None] * inv.astype(np.float32)[None, :]
    cos, sin = np.cos(ang), np.sin(ang)
    tab = np.stack([np.repeat(cos, 2, 1), np.stack([-sin, sin], -1).reshape(S, 2 * RH)], 1)
    return np.tile(tab.reshape(BT, P, 2, 2 * RH), (B, 1, 1, 1)).astype(np.float32)


def kernel(**inputs):
    import concourse.bacc as bacc
    from concourse.bass_utils import run_bass_kernel_spmd

    a = {k: np.asarray(v) for k, v in inputs.items()}
    kcols = lambda w: w.reshape(KC, P, -1).transpose(1, 0, 2)
    laid = {
        "x": a["L0_attn_x"].reshape(T, D),
        "gate_w": a["L0_ffn_gate_w"],
        "wgu0": np.stack([kcols(a["L0_ffn_sw_gate"]), kcols(a["L0_ffn_sw_up"])], 2),
        "down0": a["L0_ffn_sw_down"],
        "mask": mask_table(),
        "gamma": a["L1_attn_gamma"].reshape(KC, P).T,
        "beta": a["L1_attn_beta"].reshape(KC, P).T,
        "router_w": a["L1_ffn_router_weight"].T,
        "wgu1": np.stack([np.concatenate([a[f"L1_ffn_sh_{w}"], a[f"L1_ffn_r_{w}"]], 0).T
                          .reshape(KC, P, FB, P).transpose(2, 1, 0, 3) for w in ("gate", "up")], 3),
        "down1": np.concatenate([a["L1_ffn_sh_down"].T, a["L1_ffn_r_down"].T], 0),
        "trig": rotation_table(),
    }
    for name in ("Wq", "Wkv", "Wk", "Wv", "Wo"):
        laid[name] = a["L0_attn_" + name]
    for name in ("w_gate", "w_up", "w_down"):
        laid[name] = a["L0_ffn_" + name]
    for name in ("W_in", "b_in", "W_out", "b_out"):
        laid[name] = a["L1_attn_" + name]

    nc = bacc.Bacc("TRN2", target_bir_lowering=False, num_devices=1)
    env, arrays, aps = Env(), {}, {}
    for name in _INS:
        arr = np.ascontiguousarray(laid[name])
        arrays[f"in_{name}"] = arr
        aps[name] = nc.dram_tensor(f"in_{name}", arr.shape, mybir.dt.from_np(arr.dtype), kind="ExternalInput").ap()
    env.out = nc.dram_tensor("out", (T, D), F32, kind="ExternalOutput").ap()
    env.x, env.Wq, env.Wkv, env.Wk, env.Wv, env.Wo = (aps[n] for n in _INS[:6])
    env.gate_w, env.w_gate, env.w_up, env.w_down, env.wgu0, env.down0, env.mask = (aps[n] for n in _INS[6:13])
    env.W_in, env.b_in, env.W_out, env.b_out, env.gamma, env.beta = (aps[n] for n in _INS[13:19])
    env.router_w, env.wgu1, env.down1, env.trig = (aps[n] for n in _INS[19:])
    program(nc, env)
    r = run_bass_kernel_spmd(nc, [arrays], core_ids=[0])
    return r.results[0]["out"].reshape(B, S, D)
```

```python
from contextlib import ExitStack

import concourse.bass as bass
import numpy as np
from concourse import mybir

ALU = mybir.AluOpType
ACT = mybir.ActivationFunctionType
AX = mybir.AxisListType
F32 = mybir.dt.float32
F32R = mybir.dt.float32r
I32 = mybir.dt.int32
U32 = mybir.dt.uint32

P = 128
D = 512
KC = D // P
B, S = 2, 2048
T = B * S
TILES = T // P
GT = 4
G = GT * P
GROUPS = T // G
EPS = 1e-5

NH, HD = 16, 32
WINDOW, PERSIST = 128, 16
SCALE = float(HD) ** -0.5
BT = S // P
LAT = 128
NEG = -1.0e30

E, TOPK, NG, TOPG, EPG = 32, 6, 4, 2, 8
M = 352
MC = 3
MR = M - 2 * P
SH = 2 * M
SHB = 6
SHR = SH - 5 * P
MINT = 4
MAXT = T * TOPK // P + E * MINT
MINTILES = T * TOPK // P
NIDS = 4
IDROW = MAXT // NIDS
SIG_ONE = 16.6355
SIG_ZERO = -88.7

INTER, MOE_INTER = 2048, 256
FB = (INTER + MOE_INTER) // P
NROUTED = 8
RH = D // 4


class Env:
    pass


def mask_table():
    m = np.full((BT, P, 2 * P + PERSIST), NEG, np.float32)
    for i in range(BT):
        qi = i * P + np.arange(P)[:, None]
        ki = np.concatenate([(i - 1) * P + np.arange(2 * P), np.arange(PERSIST)])[None, :]
        own = np.arange(2 * P + PERSIST)[None, :] < 2 * P
        near = (ki <= qi) & (qi - ki < WINDOW)
        seen = np.where(own, near & (ki >= 0) & ((ki >= PERSIST) | (i == 0)), i > 0)
        m[i][seen] = 0.0
    return m


def scope(nc):
    ctx, sems = ExitStack(), []

    def clear():
        if sems:
            nc.clear_and_free_semaphores(sems)
            nc.all_engine_barrier()
    ctx.callback(clear)

    def sem(name):
        sems.append(nc.alloc_semaphore(name))
        return sems[-1]
    sb = lambda name, shape, dt=F32: ctx.enter_context(nc.sbuf_tensor(name, shape, dt))
    ps = lambda name, shape, dt=F32: ctx.enter_context(nc.psum_tensor(name, shape, dt))
    return ctx, sb, ps, sem


def f(ap):
    return ap.bitcast(F32)


def mm3(pe, out, lhs, rhs, first, last, **kw):
    pe.matmul(out, lhs[0], rhs[1], start=first, stop=False, **kw)
    pe.matmul(out, lhs[1], rhs[0], start=False, stop=False, **kw)
    return pe.matmul(out, lhs[0], rhs[0], start=False, stop=last, **kw)


class Chain:

    def __init__(self, eng, sem, base=0):
        self.eng, self.sem, self.base, self.n = eng, sem, base, 0

    def __call__(self, ins):
        self.n += 1
        return ins.then_inc(self.sem, 1)

    def wait(self):
        self.eng.wait_ge(self.sem, self.base + self.n)


def at(ap, i):
    rest = " ".join("bcdefg"[:len(ap.shape) - 1])
    first = rest.split()[0]
    return ap[bass.ds(i, 1)].rearrange(f"a {rest} -> (a {first}) {' '.join(rest.split()[1:])}")


def rstd_chain(dve, c, mv, r, tmp):
    c(dve.reciprocal(r[:, :], r[:, :]))
    c.wait()
    c(dve.tensor_tensor(tmp[:, :], r[:, :], r[:, :], ALU.mult))
    c.wait()
    c(dve.tensor_tensor(tmp[:, :], tmp[:, :], mv, ALU.mult))
    c.wait()
    c(dve.tensor_scalar(tmp[:, :], tmp[:, :], -0.5, 1.5, ALU.mult, ALU.add))
    c.wait()
    c(dve.tensor_tensor(r[:, :], r[:, :], tmp[:, :], ALU.mult))
    c.wait()


def phase_front(nc, env):
    ctx, sb, ps, sem = scope(nc)
    RING = 6
    ROOT_AT = 8
    ITEMS = 18
    x_v = env.x.rearrange("(g j p) d -> g p j d", p=P, j=GT)
    xn_v = env.xn_d.rearrange("(g j p) d -> g p j d", p=P, j=GT)
    v_v = env.v_d.rearrange("(g j p) d -> g p j d", p=P, j=GT)
    with ctx:
        x_sb = [sb(f"f_x{i}", [P, GT, D]) for i in range(2)]
        xn = [sb(f"f_xn{i}", [P, GT, D]) for i in range(2)]
        xT = [[sb(f"f_xT{i}{h}", [P, KC, G], F32R) for h in range(2)] for i in range(2)]
        qk = [sb(f"f_qk{i}", [P, 8, 2, G], F32R) for i in range(2)]
        vst = [sb(f"f_v{i}", [P, GT, NH, 2, HD], F32R) for i in range(2)]
        lat = [sb(f"f_lat{h}", [P, G], F32R) for h in range(2)]
        wraw = xn[1]
        wq = [sb(f"f_wq{h}", [P, KC, D], F32R) for h in range(2)]
        wkv = [sb(f"f_wkv{h}", [P, KC, LAT], F32R) for h in range(2)]
        wk = [sb(f"f_wk{h}", [P, 1, D], F32R) for h in range(2)]
        wv = [sb(f"f_wv{h}", [P, 1, D], F32R) for h in range(2)]
        wg = [sb(f"f_wg{h}", [P, KC, E], F32R) for h in range(2)]
        st = sb("f_st", [P, GT, 6])
        mv = sb("f_mv", [P, GT, 2])
        var = sb("f_var", [P, GT])
        rstd = sb("f_rstd", [P, GT])
        tmp = sb("f_tmp", [P, GT])
        bank = [ps(f"f_ps{i}", [P, D]) for i in range(RING)]

        w_in, w_used, w_hi = sem("f_w_in"), sem("f_w_used"), sem("f_w_hi")
        id_step = sem("f_id")
        x_in = [sem(f"f_x_in{i}") for i in range(2)]
        normed = sem("f_normed")
        xn_out = [sem(f"f_xn_out{i}") for i in range(2)]
        xn_free = sem("f_xn_free")
        var_ready, root_ready = sem("f_var_ready"), sem("f_root_ready")
        dve_step = sem("f_dve_step")
        full = sem("f_full")
        hi_done = sem("f_hi_done")
        lo_done = sem("f_lo_done")
        st_out = [sem(f"f_st_out{i}") for i in range(2)]
        st_free = sem("f_st_free")
        block = ctx.enter_context(nc.Block())

        weights = [
            (env.Wq.rearrange("(c p) n -> p c n", p=P), wq, KC, D),
            (env.Wkv.rearrange("(c p) n -> p c n", p=P), wkv, KC, LAT),
            (env.Wk.rearrange("(c p) n -> p c n", p=P), wk, 1, D),
            (env.Wv.rearrange("(c p) n -> p c n", p=P), wv, 1, D),
            (env.gate_w.rearrange("(c p) n -> p c n", p=P), wg, KC, E),
        ]

        def dest(b, j, h):
            if j < 4:
                return xT[b][h][:, :, j * P:(j + 1) * P]
            if j == 5:
                return lat[h][:, :]
            if j < 14:
                return qk[b][:, j - 6, h, :]
            return vst[b][:, j - 14, :, h, :]

        def psum(b, j):
            src = bank[(b * ITEMS + j) % RING][:, :]
            if j < 4:
                return src.rearrange("p (c t) -> p c t", c=KC)
            return src if j < 14 else src.rearrange("p (h d) -> p h d", d=HD)

        @block.sync
        def _(sp):
            for i, (src, _, c, n) in enumerate(weights):
                if i:
                    sp.wait_ge(w_used, i)
                sp.dma_start(wraw[:, 0:c, 0:n], src).then_inc(w_in, 16)
            for b in range(2):
                sp.dma_start(x_sb[b][:, :, :], x_v[b]).then_inc(x_in[b], 16)

            def group(g, b, tok, more):
                pick = (lambda d: d[g]) if isinstance(g, int) else (lambda d: at(d, g))
                sp.wait_ge(normed, g + 3)
                sp.dma_start(pick(xn_v), xn[b][:, :, :]).then_inc(xn_out[b], 16)
                if more:
                    sp.dma_start(x_sb[b][:, :, :], at(x_v, g + 2)).then_inc(x_in[b], 16)
                sp.wait_ge(lo_done, g * ITEMS + 4 + RING)
                for h in range(2):
                    sp.dma_start(pick(env.xT_d[h]), f(xT[b][h][:, :, :])).then_inc(st_out[b], 16)
                for w in range(2):
                    sp.wait_ge(lo_done, g * ITEMS + 10 + 4 * w + RING)
                    for h in range(2):
                        sp.dma_start(env.qk_d[w, h, :, tok].rearrange("(m p) t -> p m t", p=P),
                                     f(qk[b][:, 4 * w:4 * w + 4, h, :])).then_inc(st_out[b], 16)
                sp.wait_ge(lo_done, (g + 1) * ITEMS + RING)
                sp.dma_start(pick(v_v), f(vst[b][:, :, :, :, :]).rearrange("p j h l d -> p j (h l d)"))\
                  .then_inc(st_out[b], 16)
            with sp.Fori(0, GROUPS // 2 - 1) as gp:
                for b in range(2):
                    group(2 * gp + b, b, bass.ds((2 * gp + b) * G, G), True)
            for g in (GROUPS - 2, GROUPS - 1):
                group(g, g % 2, slice(g * G, (g + 1) * G), False)

        @block.gpsimd
        def _(pool):
            pool.memset(env.ident[:, :], 0.0).then_inc(id_step, 1)
            pool.wait_ge(id_step, 1)
            pool.affine_select(out=env.ident[:, :], in_=env.ident[:, :], compare_op=ALU.not_equal, fill=1.0,
                               base=0, pattern=[[-1, P]], channel_multiplier=1).then_inc(id_step, 1)
            with pool.Fori(0, GROUPS // 2) as gp:
                for b in range(2):
                    pool.wait_ge(xn_out[b], 16 * gp + 16)
                    pool.sem_inc(xn_free, 1)
                    pool.wait_ge(st_out[b], 112 * gp + 112)
                    pool.sem_inc(st_free, 1)

        @block.scalar
        def _(act):
            for i, (_, dst, c, n) in enumerate(weights):
                act.wait_ge(w_in, 16 * (i + 1))
                act.activation(dst[0][:, :, :], wraw[:, 0:c, 0:n], ACT.Copy).then_inc(w_hi, 1)

            def root(g):
                act.wait_ge(var_ready, g + 1)
                act.activation(rstd[:, :], var[:, :], ACT.Sqrt).then_inc(root_ready, 1)

            def hi(g, b, more=True):
                act.wait_ge(st_free, g + 1)
                for j in range(ITEMS):
                    if j == ROOT_AT and more:
                        root(g + 1)
                    if j == 4:
                        continue
                    act.wait_ge(full, g * ITEMS + j + 1)
                    act.activation(dest(b, j, 0), psum(b, j), ACT.Copy).then_inc(hi_done, 1)
            root(0)
            with act.Fori(0, GROUPS // 2 - 1) as gp:
                for b in range(2):
                    hi(2 * gp + b, b)
            hi(GROUPS - 2, 0)
            hi(GROUPS - 1, 1, False)

        @block.vector
        def _(dve):
            dve.sem_inc(normed, 2)
            dve.sem_inc(xn_free, 2)
            dve.sem_inc(st_free, 2)
            dve.sem_inc(lo_done, RING)
            for i, (_, dst, c, n) in enumerate(weights):
                dve.wait_ge(w_hi, i + 1)
                dve.tensor_tensor(dst[1][:, :, :], wraw[:, 0:c, 0:n], f(dst[0][:, :, :]), ALU.subtract)\
                   .then_inc(w_used, 1)

            class Norm:

                def __init__(self, g, b, gp):
                    self.g, self.b, self.gp = g, b, gp
                    self.c = Chain(dve, dve_step, g * (2 * GT + 5))

                def stats(self, j):
                    if j == 0:
                        dve.wait_ge(x_in[self.b], 16 * self.gp + 16)
                    self.c(dve.bn_stats(st[:, j, :], x_sb[self.b][:, j, :]))

                def variance(self):
                    self.c.wait()
                    dve.memset(tmp[:, 0:1], 0.0)
                    for j in range(GT):
                        self.c(dve.bn_aggr(mv[:, j, :], st[:, j, :]))
                    self.c.wait()
                    dve.tensor_scalar(var[:, :], mv[:, :, 1], EPS, None, ALU.add).then_inc(var_ready, 1)

                def deviation(self):
                    dve.wait_ge(root_ready, self.g + 1)
                    rstd_chain(dve, self.c, var[:, :], rstd, tmp)
                    dve.wait_ge(xn_free, self.g + 1)

                def apply(self, j):
                    b = self.b
                    ins = dve.tensor_scalar(xn[b][:, j, :], x_sb[b][:, j, :], mv[:, j, 0:1], rstd[:, j:j + 1],
                                            ALU.subtract, ALU.mult)
                    if j == GT - 1:
                        ins.then_inc(normed, 1)

            def norm(g, b, gp):
                n = Norm(g, b, gp)
                for j in range(GT):
                    n.stats(j)
                n.variance()
                n.deviation()
                for j in range(GT):
                    n.apply(j)

            def lo(g, b, n=None):
                for j in range(ITEMS):
                    if j == 4:
                        dve.wait_ge(full, g * ITEMS + j + 1)
                        dve.tensor_copy(env.logits[:, bass.ds(g * GT, GT), :],
                                        psum(b, j)[:, 0:GT * E].rearrange("p (j e) -> p j e", e=E))\
                           .then_inc(lo_done, 1)
                    else:
                        dve.wait_ge(hi_done, g * (ITEMS - 1) + j + (j < 4))
                        dve.tensor_tensor(dest(b, j, 1), psum(b, j), f(dest(b, j, 0)), ALU.subtract)\
                           .then_inc(lo_done, 1)
                    if n is not None:
                        if j in (5, 6):
                            n.stats(2 * (j - 5))
                            n.stats(2 * (j - 5) + 1)
                        if j == ROOT_AT - 1:
                            n.variance()
                        if j == ROOT_AT:
                            n.deviation()
                        if j in (ROOT_AT, ROOT_AT + 1):
                            n.apply(2 * (j - ROOT_AT))
                            n.apply(2 * (j - ROOT_AT) + 1)
            norm(0, 0, 0)
            with dve.Fori(0, GROUPS // 2 - 1) as gp:
                lo(2 * gp, 0, Norm(2 * gp + 1, 1, gp))
                lo(2 * gp + 1, 1, Norm(2 * gp + 2, 0, gp + 1))
            lo(GROUPS - 2, 0, Norm(GROUPS - 1, 1, GROUPS // 2 - 1))
            lo(GROUPS - 1, 1)

        @block.tensor
        def _(pe):
            pe.wait_ge(id_step, 2)
            pe.wait_ge(w_used, len(weights))
            with pe.Fori(0, GROUPS // 2) as gp:
                for b in range(2):
                    g = 2 * gp + b

                    def out(j):
                        pe.wait_ge(lo_done, g * ITEMS + j + 1)
                        return bank[(b * ITEMS + j) % RING]
                    pe.wait_ge(normed, g + 3)
                    for j in range(GT):
                        o = out(j)
                        for c in range(KC):
                            ins = pe.transpose(o[:, c * P:(c + 1) * P], xn[b][:, j, c * P:(c + 1) * P],
                                               env.ident[:, :])
                        ins.then_inc(full, 1)
                    pe.wait_ge(lo_done, g * ITEMS + 4 + RING)
                    x2 = lambda c, t: [xT[b][h][:, c, t] for h in range(2)]
                    o = out(4)
                    for j in range(GT):
                        for c in range(KC):
                            ins = mm3(pe, o[:, j * E:(j + 1) * E], x2(c, slice(j * P, j * P + P)),
                                      [wg[h][:, c, :] for h in range(2)], c == 0, c == KC - 1)
                    ins.then_inc(full, 1)
                    o = out(5)
                    for c in range(KC):
                        ins = mm3(pe, o[:, :], [wkv[h][:, c, :] for h in range(2)], x2(c, slice(0, G)),
                                  c == 0, c == KC - 1)
                    ins.then_inc(full, 1)
                    for m in range(4):
                        o = out(6 + m)
                        for c in range(KC):
                            ins = mm3(pe, o[:, :], [wq[h][:, c, m * P:(m + 1) * P] for h in range(2)],
                                      x2(c, slice(0, G)), c == 0, c == KC - 1)
                        ins.then_inc(full, 1)
                    pe.wait_ge(lo_done, g * ITEMS + 6 + RING)
                    for m in range(4):
                        o = out(10 + m)
                        ins = mm3(pe, o[:, :], [wk[h][:, 0, m * P:(m + 1) * P] for h in range(2)],
                                  [lat[h][:, :] for h in range(2)], True, True)
                        ins.then_inc(full, 1)
                    for j in range(GT):
                        o = out(14 + j)
                        ins = mm3(pe, o[:, :], [lat[h][:, j * P:(j + 1) * P] for h in range(2)],
                                  [wv[h][:, 0, :] for h in range(2)], True, True)
                        ins.then_inc(full, 1)


def phase_route(nc, env):
    ctx, sb, ps, sem = scope(nc)
    TE = TILES * E
    with ctx:
        lc = sb("r_lc", [P, TILES, NG, EPG])
        gmax = sb("r_gmax", [P, TILES, NG])
        cmp = sb("r_cmp", [P, TILES, NG])
        rank = sb("r_rank", [P, TILES, NG])
        v8 = sb("r_v8", [P, TILES, 8])
        i8 = sb("r_i8", [P, TILES, 8], U32)
        i8f = sb("r_i8f", [P, TILES, 8])
        ex = sb("r_ex", [P, TILES, TOPK])
        wsum = sb("r_wsum", [P, TILES])
        eid = sb("r_eid", [P, E])
        hot = [sb(f"r_hot{k}", [P, TILES, E]) for k in range(TOPK)]
        hit = sb("r_hit", [P, TILES, E])
        before = sb("r_before", [P, P])
        ones = sb("r_ones", [P, P])
        one_row = sb("r_one_row", [P, TE])
        cnt = sb("r_cnt", [P, E, TILES])
        run = sb("r_run", [P, E, TILES])
        start = sb("r_start", [P, E])
        tot = sb("r_tot", [P, E])
        nt_i = sb("r_nt_i", [P, E], I32)
        nt_s = sb("r_nt_s", [P, E], I32)
        nt = sb("r_nt", [P, E])
        last = sb("r_last", [P, E])
        base = sb("r_base", [P, E])
        pos = sb("r_pos", [P, TILES, E])
        prod = sb("r_prod", [P, TILES, E])
        slot = sb("r_slot", [P, TILES, TOPK])
        first_f = sb("r_first_f", [P, E + 1])
        zero = sb("r_zero", [IDROW, P])
        pr = ps("r_pr", [P, 2, 512])
        pc = ps("r_pc", [P, 2, 512])

        dve_step, c_ready, e_in, e_out = sem("r_dve"), sem("r_c"), sem("r_e_in"), sem("r_e_out")
        hits, counted, zeroed = sem("r_hits"), sem("r_counted"), sem("r_zeroed")
        block = ctx.enter_context(nc.Block())
        te = lambda t: t.rearrange("p t e -> p (t e)")

        @block.gpsimd
        def _(pool):
            c = Chain(pool, c_ready)
            c(pool.iota(eid[:, :], [[1, E]], base=0, channel_multiplier=0,
                        allow_small_or_imprecise_dtypes=True))
            c(pool.iota(env.tokid[:, :], [[P, TILES]], base=0, channel_multiplier=1,
                        allow_small_or_imprecise_dtypes=True))
            c(pool.memset(ones[:, :], 1.0))
            c(pool.memset(one_row[:, :], 1.0))
            c(pool.memset(zero[:, :], 0.0))
            c(pool.memset(before[:, :], 1.0))
            c.wait()
            c(pool.affine_select(out=before[:, :], in_=before[:, :], compare_op=ALU.is_gt, fill=0.0,
                                 base=0, pattern=[[1, P]], channel_multiplier=-1))

        @block.sync
        def _(sp):
            sp.wait_ge(c_ready, 7)
            rows = env.ids_d.rearrange("(h r n) a -> h r (n a)", n=P, h=NIDS)
            for h in range(NIDS):
                sp.dma_start(rows[h], zero[:, :]).then_inc(zeroed, 16)
            sp.wait_ge(zeroed, 16 * NIDS)

        @block.scalar
        def _(act):
            act.wait_ge(e_in, 1)
            act.activation(ex[:, :, :], v8[:, :, 0:TOPK], ACT.Exp, scale=-1.0).then_inc(e_out, 1)

        @block.tensor
        def _(pe):
            pe.wait_ge(hits, 1)
            pe.wait_ge(c_ready, 7)
            for h in range(2):
                rhs = te(hit[:, :, :])[:, 512 * h:512 * h + 512]
                pe.matmul(pr[:, h, :], before[:, :], rhs, start=True, stop=True)
                ins = pe.matmul(pc[:, h, :], ones[:, :], rhs, start=True, stop=True)
            ins.then_inc(counted, 1)

        @block.vector
        def _(dve):
            c = Chain(dve, dve_step)

            def do(ins):
                c(ins)
                c.wait()
            do(dve.tensor_scalar(te(lc[:, :, :, :].rearrange("p t g e -> p t (g e)")), te(env.logits[:, :, :]),
                                 SIG_ONE, SIG_ZERO, ALU.min, ALU.max))
            do(dve.tensor_reduce(gmax[:, :, :], lc[:, :, :, :], AX.X, ALU.max))
            do(dve.memset(rank[:, :, :], 0.0))
            for h in range(NG):
                for lo, hi, op in ((0, h, ALU.is_gt), (h + 1, NG, ALU.is_ge)):
                    if lo == hi:
                        continue
                    do(dve.tensor_tensor(cmp[:, :, lo:hi],
                                         gmax[:, :, h:h + 1].to_broadcast([P, TILES, hi - lo]),
                                         gmax[:, :, lo:hi], op))
                    do(dve.tensor_tensor(rank[:, :, lo:hi], rank[:, :, lo:hi], cmp[:, :, lo:hi], ALU.add))
            do(dve.tensor_scalar(rank[:, :, :], rank[:, :, :], TOPG - 0.5, NEG, ALU.is_gt, ALU.mult))
            do(dve.tensor_tensor(lc[:, :, :, :], lc[:, :, :, :],
                                 rank[:, :, :].unsqueeze(3).to_broadcast([P, TILES, NG, EPG]), ALU.add))
            flat = lc[:, :, :, :].rearrange("p t g e -> p t (g e)")
            for t in range(TILES):
                c(dve.max(v8[:, t, :], flat[:, t, :]))
            c.wait()
            for t in range(TILES):
                ins = dve.max_index(i8[:, t, :], v8[:, t, :], flat[:, t, :])
                c(ins)
            c.wait()
            dve.sem_inc(e_in, 1)
            do(dve.tensor_copy(i8f[:, :, :], i8[:, :, :]))
            dve.wait_ge(c_ready, 7)
            for k in range(TOPK):
                c(dve.tensor_tensor(hot[k][:, :, :], i8f[:, :, k:k + 1].to_broadcast([P, TILES, E]),
                                    eid[:, :].unsqueeze(1).to_broadcast([P, TILES, E]), ALU.is_equal))
            c.wait()
            do(dve.tensor_tensor(hit[:, :, :], hot[0][:, :, :], hot[1][:, :, :], ALU.add))
            for k in range(2, TOPK):
                do(dve.tensor_tensor(hit[:, :, :], hit[:, :, :], hot[k][:, :, :], ALU.add))
            dve.sem_inc(hits, 1)
            dve.wait_ge(e_out, 1)
            do(dve.tensor_scalar(ex[:, :, :], ex[:, :, :], 1.0, None, ALU.add))
            do(dve.reciprocal(ex[:, :, :], ex[:, :, :]))
            do(dve.tensor_reduce(wsum[:, :], ex[:, :, :], AX.X, ALU.add))
            do(dve.reciprocal(wsum[:, :], wsum[:, :]))
            do(dve.tensor_tensor(env.wexp[:, :, :], ex[:, :, :],
                                 wsum[:, :].unsqueeze(2).to_broadcast([P, TILES, TOPK]), ALU.mult))
            dve.wait_ge(counted, 1)
            do(dve.tensor_copy(cnt[:, :, :].rearrange("p e t -> p t e"),
                               pc[:, :, :].rearrange("p h (t e) -> p (h t) e", e=E)))
            do(dve.tensor_tensor_scan(run[:, :, :].rearrange("p e t -> p (e t)"), one_row[:, :],
                                      cnt[:, :, :].rearrange("p e t -> p (e t)"), 0.0, ALU.mult, ALU.add))
            c(dve.memset(start[:, 0:1], 0.0))
            do(dve.tensor_copy(start[:, 1:E], run[:, 0:E - 1, TILES - 1]))
            do(dve.tensor_tensor(tot[:, :], run[:, :, TILES - 1], start[:, :], ALU.subtract))
            do(dve.tensor_scalar(nt_i[:, :], tot[:, :], float(P - 1), None, ALU.add))
            do(dve.tensor_scalar(nt_s[:, :], nt_i[:, :], 7, None, ALU.logical_shift_right))
            do(dve.tensor_scalar(nt[:, :], nt_s[:, :], float(MINT), None, ALU.max))
            do(dve.tensor_tensor_scan(last[:, :], one_row[:, 0:E], nt[:, :], 0.0, ALU.mult, ALU.add))
            c(dve.memset(first_f[:, 0:1], 0.0))
            do(dve.tensor_copy(first_f[:, 1:E + 1], last[:, :]))
            c(dve.tensor_copy(env.first[:, :], first_f[:, :]))
            do(dve.tensor_scalar(base[:, :], first_f[:, 0:E], float(P), None, ALU.mult))
            do(dve.tensor_tensor(base[:, :], base[:, :], start[:, :], ALU.subtract))
            do(dve.tensor_tensor(run[:, :, :], run[:, :, :], cnt[:, :, :], ALU.subtract))
            do(dve.tensor_tensor(pos[:, :, :].rearrange("p t e -> p e t"), run[:, :, :],
                                 base[:, :].unsqueeze(2).to_broadcast([P, E, TILES]), ALU.add))
            do(dve.tensor_tensor(te(pos[:, :, :]), te(pos[:, :, :]),
                                 pr[:, :, :].rearrange("p h n -> p (h n)"), ALU.add))
            for k in range(TOPK):
                do(dve.tensor_tensor(prod[:, :, :], pos[:, :, :], hot[k][:, :, :], ALU.mult))
                do(dve.tensor_reduce(slot[:, :, k], prod[:, :, :], AX.X, ALU.add))
            do(dve.tensor_copy(env.slot_i[:, :, :], slot[:, :, :]))


def phase_ids(nc, env):
    ctx, sb, ps, sem = scope(nc)
    with ctx:
        ids = [sb(f"t_ids{i}", [IDROW, P]) for i in range(NIDS)]
        pt = ps("t_pt", [P, NIDS, 512])
        ids_in, turned = sem("t_ids_in"), sem("t_turned")
        block = ctx.enter_context(nc.Block())

        @block.sync
        def _(sp):
            rows = env.ids_d.rearrange("(h r n) a -> h r (n a)", n=P, h=NIDS)
            for h in range(NIDS):
                sp.dma_start(ids[h][:, :], rows[h]).then_inc(ids_in, 16)

        @block.tensor
        def _(pe):
            pe.wait_ge(ids_in, 16 * NIDS)
            for h in range(NIDS):
                ins = pe.transpose(pt[:, h, 0:IDROW], ids[h][:, :], env.ident[0:IDROW, 0:IDROW])
            ins.then_inc(turned, 1)

        @block.vector
        def _(dve):
            dve.wait_ge(turned, 1)
            for h in range(NIDS):
                dve.tensor_copy(env.ids[:, h * IDROW:(h + 1) * IDROW], pt[:, h, 0:IDROW])


def split_weights(nc, name, weights, raw):
    ctx, _, _, sem = scope(nc)
    R = len(raw)
    with ctx:
        w_in = [sem(f"{name}_in{i}") for i in range(R)]
        w_hi, w_used = sem(name + "_hi"), sem(name + "_used")
        block = ctx.enter_context(nc.Block())

        @block.sync
        def _(sp):
            for i, (src, _, c, n) in enumerate(weights):
                if i >= R:
                    sp.wait_ge(w_used, i - R + 1)
                sp.dma_start(raw[i % R][:, 0:c, 0:n], src).then_inc(w_in[i % R], 16)

        @block.scalar
        def _(act):
            for i, (_, dst, c, n) in enumerate(weights):
                act.wait_ge(w_in[i % R], 16 * (i // R + 1))
                act.activation(dst[0], raw[i % R][:, 0:c, 0:n], ACT.Copy).then_inc(w_hi, 1)

        @block.vector
        def _(dve):
            for i, (_, dst, c, n) in enumerate(weights):
                dve.wait_ge(w_hi, i + 1)
                dve.tensor_tensor(dst[1], raw[i % R][:, 0:c, 0:n], f(dst[0]), ALU.subtract).then_inc(w_used, 1)


def phase_attend(nc, env):
    ctx, sb, ps, sem = scope(nc)
    U = 8
    N = U * NH
    HH = NH // 2
    W = 2 * P + PERSIST
    ST = 3 * HD
    LAG = 3
    RT = 4
    with ctx:
        qs = [sb(f"a_q{i}", [ST, NH, P], F32R) for i in range(2)]
        ks = [sb(f"a_k{i}", [ST, NH, P], F32R) for i in range(U)]
        vb = [sb(f"a_v{i}", [P, NH, 2 * HD], F32R) for i in range(U)]
        kp = sb("a_kp", [ST, B, NH, PERSIST], F32R)
        vp = sb("a_vp", [P, B, 2, HH, 2 * HD], F32R)
        mask = [sb(f"a_mask{i}", [P, W]) for i in range(2)]
        sm = [sb(f"a_sm{i}", [P, W]) for i in range(2)]
        nmax = [sb(f"a_nmax{i}", [P, 1]) for i in range(2)]
        pr = [sb(f"a_pr{i}", [P, HH, W]) for i in range(2)]
        pp = [sb(f"a_pp{i}", [P, P]) for i in range(2)]
        rs = [sb(f"a_rs{i}", [P, HH]) for i in range(2)]
        rl = sb("a_rl", [P, HH])
        pT = [[sb(f"a_pT{i}{h}", [P, 2 * P], F32R) for h in range(2)] for i in range(RT)]
        ppT = [sb(f"a_ppT{h}", [P, P], F32R) for h in range(2)]
        o1 = sb("a_o1", [P, HH, HD])
        o2 = sb("a_o2", [P, HH, HD])
        o = sb("a_o", [P, NH, HD])
        oT = [sb(f"a_oT{h}", [P, KC, P], F32R) for h in range(2)]
        wo = [sb(f"a_wo{h}", [P, KC, D], F32R) for h in range(2)]
        wraw = sb("a_wraw", [P, KC, D])
        y = [sb(f"a_y{i}", [P, D]) for i in range(2)]
        split_weights(nc, "a_ws", [(env.Wo.rearrange("(c p) n -> p c n", p=P),
                                   [w[:, :, :] for w in wo], KC, D)], [wraw])

        psS = [ps(f"a_psS{i}", [P, D]) for i in range(2)]
        psP = [ps(f"a_psP{i}", [P, D]) for i in range(2)]
        psO = [ps(f"a_psO{i}", [P, HH, 2, HD]) for i in range(2)]
        psX = ps("a_psX", [P, KC, P])
        psY = ps("a_psY", [P, D])

        slot6 = [sb(f"a_slot6{i}", [P, TOPK], I32) for i in range(2)]
        tok1 = [sb(f"a_tok1{i}", [P, 1]) for i in range(2)]
        scat = [sem(f"a_scat{i}") for i in range(2)]
        copied = sem("a_copied")
        once, cleared = sem("a_once"), sem("a_cleared")
        pool_passed, dve_passed = sem("a_pool_passed"), sem("a_dve_passed")
        q_in = [sem(f"a_q_in{i}") for i in range(2)]
        kv_in = [sem(f"a_kv_in{i}") for i in range(U)]
        s_full, s_used = sem("a_s_full"), sem("a_s_used")
        p_ready, pT_full = sem("a_p_ready"), sem("a_pT_full")
        pT_hi, pT_split, pv_done = sem("a_pT_hi"), sem("a_pT_split"), sem("a_pv_done")
        o_full, o_used = sem("a_o_full"), sem("a_o_used")
        o_ready = sem("a_o_ready")
        x_full, x_hi, x_split = sem("a_x_full"), sem("a_x_hi"), sem("a_x_split")
        y_full, y_ready = sem("a_y_full"), sem("a_y_ready")
        y_out = [sem(f"a_y_out{i}") for i in range(2)]
        y_free = sem("a_y_free")
        dve_step, pp_ready = sem("a_dve"), sem("a_pp_ready")
        block = ctx.enter_context(nc.Block())
        v_v = env.v_d.rearrange("(i p) n -> i p n", p=P)
        s_v = env.s_d.rearrange("(i p) n -> i p n", p=P)

        def turns(eng, body):
            with eng.Fori(0, B) as b:
                with eng.Fori(0, BT // U) as q:
                    body(b, q, b * BT + q * U)

        EXTRA = {}
        for u in range(U):
            for at_step, what in ((9, ("persT", u, 0)), (11, ("persV", u, 0)), (17, ("persT", u, 1)),
                                  (19, ("persV", u, 1)), (22, ("oT", u, 0)), (24, ("proj", u, 0))):
                EXTRA.setdefault(u * NH + at_step, []).append(what)
        STEPS = range(max(EXTRA) + 1)

        @block.gpsimd
        def _(pool):
            pool.memset(f(vp[:, :, :, :, :]).rearrange("p b a h d -> p (b a h d)"), 0.0).then_inc(cleared, 1)
            pool.memset(f(ks[U - 1][:, :, :]), 0.0).then_inc(cleared, 1)
            pool.memset(f(vb[U - 1][:, :, :]), 0.0).then_inc(cleared, 1)


            def body(b, q, t0):
                def persistent(u, half):
                    n = 2 * (t0 + u) + half
                    pool.wait_ge(x_full, 3 * (t0 + u) + half + 1)
                    pool.wait_ge(p_ready, (t0 + u) * NH + (half + 1) * HH + 2)
                    pool.sem_inc(pool_passed, 1)
                    pool.tensor_copy(pp[half][:, :].rearrange("p (h k) -> p h k", h=HH), pr[half][:, :, 2 * P:W])\
                        .then_inc(pp_ready, 1)

                def store(u):
                    pool.wait_ge(y_ready, t0 + u + 2)
                    pool.dma_start(at(s_v, t0 + u), y[u % 2][:, :]).then_inc(y_out[u % 2], 16)
                    pool.wait_ge(y_out[u % 2], 16 * (b * (BT // 2) + q * (U // 2) + u // 2 + 1))
                    pool.sem_inc(y_free, 1)

                def scatter(u):
                    t = t0 + u
                    pool.tensor_copy(slot6[u % 2][:, :],
                                     env.slot_i[:, bass.ds(t, 1), :].rearrange("p a k -> p (a k)")).then_inc(copied, 1)
                    pool.tensor_copy(tok1[u % 2][:, :], env.tokid[:, bass.ds(t, 1)]).then_inc(copied, 1)
                    pool.wait_ge(copied, 2 * t + 2)
                    pool.sem_inc(pool_passed, 1)
                    for k in range(TOPK):
                        pool.indirect_dma_start(
                            env.ids_d, bass.IndirectOffsetOnAxis(ap=slot6[u % 2][:, k:k + 1].bitcast(U32), axis=0),
                            tok1[u % 2][:, :], None).then_inc(scat[u % 2], 16)
                for u in range(U):
                    persistent(u, 0)
                    scatter(u)
                    if u:
                        store(u - 1)
                    persistent(u, 1)
                    pool.wait_ge(scat[u % 2], 16 * TOPK * (b * (BT // 2) + q * (U // 2) + u // 2 + 1))
                store(U - 1)
            turns(pool, body)

        @block.sync
        def _(sp):
            sp.wait_ge(cleared, 3)
            for b in range(B):
                for j, h in ((0, 0), (1, 0), (2, 1)):
                    sp.dma_start(f(kp[j * HD:(j + 1) * HD, b, :, :]),
                                 env.qk_d[1, h, :, b * S:b * S + PERSIST].rearrange("(m p) t -> p m t", p=HD))\
                      .then_inc(once, 16)
                for h in range(NH):
                    sp.dma_start(f(vp[PERSIST * (h % HH):PERSIST * (h % HH + 1), b, h // HH, h % HH, :]),
                                 env.v_d[b * S:b * S + PERSIST, 2 * HD * h:2 * HD * (h + 1)]).then_inc(once, 16)

            def body(b, q, t0):
                for u in range(U):
                    sp.wait_ge(pv_done, (t0 + u + 1) * NH)
                    tok = bass.ds((t0 + u) * P, P)
                    src = lambda w, h: env.qk_d[w, h, :, tok].rearrange("(m p) t -> p m t", p=HD)
                    for j, (hq, hk) in enumerate(((0, 0), (1, 0), (0, 1))):
                        sp.dma_start(f(qs[u % 2][j * HD:(j + 1) * HD, :, :]), src(0, hq)).then_inc(q_in[u % 2], 16)
                        sp.dma_start(f(ks[u][j * HD:(j + 1) * HD, :, :]), src(1, hk)).then_inc(kv_in[u], 16)
                    sp.dma_start(f(vb[u][:, :, :]).rearrange("p h d -> p (h d)"), at(v_v, t0 + u))\
                      .then_inc(kv_in[u], 16)
                    sp.dma_start(mask[u % 2][:, :], at(env.mask, q * U + u)).then_inc(q_in[u % 2], 16)
            turns(sp, body)

        def loaded(b, q, u):
            return 64 * (b * (BT // 2) + q * (U // 2) + u // 2 + 1)

        @block.tensor
        def _(pe):
            pe.wait_ge(once, 16 * B * (3 + NH))

            def body(b, q, t0):
                n0 = t0 * NH

                def score(s):
                    u, h = divmod(s, NH)
                    if h == 0:
                        pe.wait_ge(q_in[u % 2], loaded(b, q, u))
                        pe.wait_ge(kv_in[u], 64 * (b * (BT // U) + q + 1))
                    pe.wait_ge(s_used, n0 + s + 1)
                    out, w = psS[s % 2], qs[u % 2][:, h, :]
                    pe.matmul(out[:, 0:P], w, ks[(u - 1) % U][:, h, :], start=True, stop=True)
                    pe.matmul(out[:, P:2 * P], w, ks[u][:, h, :], start=True, stop=True)
                    pe.matmul(out[:, 2 * P:W], w, kp[:, bass.ds(b, 1), h, :].rearrange("p a k -> p (a k)"),
                              start=True, stop=True).then_inc(s_full, 1)

                def turn(s):
                    u, h = divmod(s, NH)
                    pe.wait_ge(p_ready, n0 + s + 3)
                    pe.wait_ge(pT_split, n0 + s + 1)
                    for c in range(2):
                        ins = pe.transpose(psP[s % 2][:, c * P:(c + 1) * P],
                                           pr[(h // HH) % 2][:, h % HH, c * P:(c + 1) * P], env.ident[:, :])
                    ins.then_inc(pT_full, 1)

                def values(s):
                    u, h = divmod(s, NH)
                    half = h // HH
                    pe.wait_ge(pT_split, n0 + s + 3)
                    if h % HH == 0:
                        pe.wait_ge(o_used, 2 * (t0 + u) + half + 1)
                    out = psO[half][:, h % HH, :, :]
                    for k, (c, v, part) in enumerate((c, v, part) for c, v in ((0, vb[(u - 1) % U]), (1, vb[u]))
                                                     for part in (1, 0)):
                        ins = pe.matmul(out, pT[s % RT][part][:, c * P:(c + 1) * P],
                                        v[:, h, :].rearrange("p (a d) -> p a d", a=2),
                                        start=(h % HH == 0 and k == 0), stop=False, skip_group_check=True)
                    ins.then_inc(pv_done, 1)

                def extra(what, u, half):
                    x = 3 * (t0 + u)
                    if what == "persT":
                        pe.wait_ge(x_split, x + half + 1)
                        pe.wait_ge(pp_ready, 2 * (t0 + u) + half + 3)
                        pe.transpose(psX[:, 0, :], pp[half][:, :], env.ident[:, :]).then_inc(x_full, 1)
                    if what == "persV":
                        pe.wait_ge(x_split, x + half + 2)
                        for part in (1, 0):
                            ins = pe.matmul(psO[half][:, :, :, :].rearrange("p h a d -> p (h a d)"), ppT[part][:, :],
                                            vp[:, bass.ds(b, 1), half, :, :].rearrange("p a h d -> p (a h d)"),
                                            start=False, stop=(part == 0), skip_group_check=True)
                        ins.then_inc(o_full, 1)
                    if what == "oT":
                        pe.wait_ge(o_ready, 2 * (t0 + u) + 2)
                        pe.wait_ge(x_split, x + 3)
                        for c in range(KC):
                            ins = pe.transpose(psX[:, c, :], o[:, c * 4:(c + 1) * 4, :].rearrange("p h d -> p (h d)"),
                                               env.ident[:, :])
                        ins.then_inc(x_full, 1)
                    if what == "proj":
                        pe.wait_ge(x_split, x + 4)
                        pe.wait_ge(y_ready, t0 + u + 1)
                        for c in range(KC):
                            ins = mm3(pe, psY[:, :], [oT[h][:, c, :] for h in range(2)],
                                      [wo[h][:, c, :] for h in range(2)], c == 0, c == KC - 1)
                        ins.then_inc(y_full, 1)

                score(0)
                score(1)
                for s in STEPS:
                    if s + 2 < N:
                        score(s + 2)
                    if s < N:
                        turn(s)
                    if LAG <= s < N + LAG:
                        values(s - LAG)
                    for e in EXTRA.get(s, []):
                        extra(*e)
            turns(pe, body)

        @block.scalar
        def _(act):
            def body(b, q, t0):
                n0 = t0 * NH

                def exps(s):
                    u, h = divmod(s, NH)
                    half = h // HH
                    if h % HH == 0:
                        act.wait_ge(pp_ready, 2 * (t0 + u) + half + 1)
                        act.wait_ge(o_used, 2 * (t0 + u) + half + 1)
                    act.wait_ge(s_used, n0 + s + 3)
                    act.activation(pr[half][:, h % HH, :], sm[s % 2][:, :], ACT.Exp, bias=nmax[s % 2][:, :],
                                   scale=-1.0, accum_out=rs[half][:, h % HH:h % HH + 1]).then_inc(p_ready, 1)

                def hi(s):
                    act.wait_ge(pv_done, n0 + s + 2 * NH - RT + 1)
                    act.wait_ge(pT_full, n0 + s + 1)
                    act.activation(pT[s % RT][0][:, :], psP[s % 2][:, 0:2 * P], ACT.Copy).then_inc(pT_hi, 1)

                def extra(what, u, half):
                    x = 3 * (t0 + u)
                    if what == "persT":
                        act.wait_ge(o_full, 2 * (t0 + u) + half + 1)
                        act.wait_ge(x_full, x + half + 4)
                        act.activation(ppT[0][:, :], psX[:, 0, :], ACT.Copy).then_inc(x_hi, 1)
                    if what == "oT":
                        act.wait_ge(y_full, t0 + u + 1)
                        act.wait_ge(x_full, x + 6)
                        act.activation(oT[0][:, :, :], psX[:, :, :], ACT.Copy).then_inc(x_hi, 1)

                exps(0)
                for s in STEPS:
                    if s + 1 < N:
                        exps(s + 1)
                    if s < N:
                        hi(s)
                    for e in EXTRA.get(s, []):
                        extra(*e)
            turns(act, body)

        @block.vector
        def _(dve):
            for s, k in ((s_used, 2), (p_ready, 2), (pT_split, 2), (pv_done, 2 * NH), (x_full, 3), (pp_ready, 2), (o_used, 2),
                         (x_split, 1), (o_full, 1), (y_full, 1), (y_ready, 1), (y_free, 2)):
                dve.sem_inc(s, k)

            def body(b, q, t0):
                n0 = t0 * NH
                c = Chain(dve, dve_step, t0 * 4)

                def top(s):
                    u, h = divmod(s, NH)
                    if h == 0:
                        dve.wait_ge(q_in[u % 2], loaded(b, q, u))
                    dve.wait_ge(p_ready, n0 + s + 1)
                    dve.wait_ge(s_full, n0 + s + 1)
                    dve.sem_inc(dve_passed, 1)
                    dve.tensor_tensor_reduce(out=sm[s % 2][:, :], in0=psS[s % 2][:, 0:W], in1=mask[u % 2][:, :],
                                             scale=-SCALE, scalar=3.0e38, op0=ALU.add, op1=ALU.min,
                                             accum_out=nmax[s % 2][:, :]).then_inc(s_used, 1)

                def lo(s):
                    dve.wait_ge(pT_hi, n0 + s + 1)
                    dve.tensor_tensor(pT[s % RT][1][:, :], psP[s % 2][:, 0:2 * P], f(pT[s % RT][0][:, :]),
                                      ALU.subtract).then_inc(pT_split, 1)

                def extra(what, u, half):
                    x = 3 * (t0 + u)
                    if what == "persT":
                        dve.wait_ge(x_hi, x + half + 1)
                        dve.tensor_tensor(ppT[1][:, :], psX[:, 0, :], f(ppT[0][:, :]), ALU.subtract)\
                           .then_inc(x_split, 1)
                    if what == "persV":
                        dve.wait_ge(o_full, 2 * (t0 + u) + half + 2)
                        c(dve.reciprocal(rl[:, :], rs[half][:, :]))
                        c.wait()
                        rb = rl[:, :].unsqueeze(2).to_broadcast([P, HH, HD])
                        c(dve.tensor_tensor(o1[:, :, :], psO[half][:, :, 0, :], rb, ALU.mult))
                        dve.tensor_tensor(o2[:, :, :], psO[half][:, :, 1, :], rb, ALU.mult).then_inc(o_used, 1)
                        dve.wait_ge(o_used, 2 * (t0 + u) + half + 3)
                        dve.tensor_tensor(o[:, half * HH:(half + 1) * HH, :], o1[:, :, :], o2[:, :, :], ALU.add)\
                           .then_inc(o_ready, 1)
                    if what == "oT":
                        dve.wait_ge(x_hi, x + 3)
                        dve.tensor_tensor(oT[1][:, :, :], psX[:, :, :], f(oT[0][:, :, :]), ALU.subtract)\
                           .then_inc(x_split, 1)
                    if what == "proj":
                        dve.wait_ge(y_free, t0 + u + 1)
                        dve.wait_ge(y_full, t0 + u + 2)
                        dve.tensor_copy(y[u % 2][:, :], psY[:, :]).then_inc(y_ready, 1)

                top(0)
                top(1)
                for s in STEPS:
                    if s + 2 < N:
                        top(s + 2)
                    if s < N:
                        lo(s)
                    for e in EXTRA.get(s, []):
                        extra(*e)
            turns(dve, body)


def phase_ffn(nc, env, name, xT_d, blocks, last, wgu, down, out_d, final):
    ctx, sb, ps, sem = scope(nc)
    stream = final
    SPLIT_AT = (3, 4)
    RW = 3 if stream else 1
    with ctx:
        x2 = [[sb(f"{name}_x{i}{h}", [P, KC, G], F32R) for h in range(2)] for i in range(2)]
        wd = [sb(f"{name}_wd{h}", [P, blocks, D], F32R) for h in range(2)]
        if stream:
            gu = [[sb(f"{name}_gu{i}{h}", [P, KC, 2, P], F32R) for h in range(2)] for i in range(RW)]
        else:
            gu = [[sb(f"{name}_gu{h}", [P, KC, 2, SH], F32R) for h in range(2)]]
        sg = [sb(f"{name}_sg{i}", [P, G]) for i in range(2)]
        hv = [sb(f"{name}_h{i}", [P, G]) for i in range(2)]
        h2 = [[sb(f"{name}_hT{i}{h}", [P, G], F32R) for h in range(2)] for i in range(2)]
        y = [sb(f"{name}_y{i}", [P, D]) for i in range(2)]
        if final:
            cmb = [sb(f"{name}_cmb{i}", [P, G]) for i in range(2)]
            m2 = [sb(f"{name}_m{h}", [P, KC, D], F32R) for h in range(2)]
            cb = sb(f"{name}_cb", [P, D])
            x1 = sb(f"{name}_x1", [P, GT, D])
            xn = sb(f"{name}_xn", [P, GT, D])
            stat = sb(f"{name}_stat", [P, GT, 3])
            res = [sb(f"{name}_res{i}", [P, D]) for i in range(2)]
        else:
            zrow = sb(f"{name}_zrow", [P, D])
            raw1 = [sb(f"{name}_raw1{i}", [P, KC, 2, P]) for i in range(2)]
            out1 = [[sb(f"{name}_out1{i}{h}", [P, KC, 2, P], F32R) for h in range(2)] for i in range(2)]
        wctx, wsb, _, _ = scope(nc)
        with wctx:
            raw = [wsb(f"{name}_raw{i}", [P, 2, D]) for i in range(2)]
            ws = []
            full_blocks = blocks if last == P else blocks - 1
            dv = down[0:full_blocks * P, :].rearrange("(c p) n -> p c n", p=P)
            for c in range(0, full_blocks, 2):
                k = min(2, full_blocks - c)
                ws.append((dv[:, c:c + k, :], [w[:, c:c + k, :] for w in wd], k, D))
            if not stream:
                for c in range(KC):
                    for a in range(2):
                        for n0 in (0, SH // 2):
                            ws.append((wgu[:, c, a, n0:n0 + SH // 2].unsqueeze(1),
                                       [w[:, c, a, n0:n0 + SH // 2].unsqueeze(1) for w in gu[0]], 1, SH // 2))
            split_weights(nc, name + "_ws", ws, raw)
            if last != P:
                lw = wsb(f"{name}_rawl", [last, 1, D])
                split_weights(nc, name + "_wl", [(down[full_blocks * P:, :].unsqueeze(1),
                                                  [w[0:last, full_blocks:, :] for w in wd], 1, D)], [lw])
        psG = [ps(f"{name}_psG{i}", [P, G]) for i in range(2)]
        psU = [ps(f"{name}_psU{i}", [P, G]) for i in range(2)]
        psY = [ps(f"{name}_psY{i}", [P, D]) for i in range(GT)]
        x_in = [sem(f"{name}_x_in{i}") for i in range(2)]
        w_in = [sem(f"{name}_w_in{i}") for i in range(RW)]
        gu_full = sem(f"{name}_gu_full")
        sg_ready, h_ready = sem(f"{name}_sg"), sem(f"{name}_h")
        h_hi, h_split = sem(f"{name}_h_hi"), sem(f"{name}_h_split")
        d_done = sem(f"{name}_d_done")
        y_ready, y_free = sem(f"{name}_y_ready"), sem(f"{name}_y_free")
        y_out = [sem(f"{name}_y_out{i}") for i in range(2)]
        dve_step = sem(f"{name}_dve")
        block = ctx.enter_context(nc.Block())
        width = lambda m: P if m < blocks - 1 else last
        routed = lambda m: final and m >= blocks - 2
        NR = 2 + 1 + 2 * GT if final else 0
        XN = 16 * (2 * GT + 1 if final else 2)
        if final:
            m_in, m_ready = sem(f"{name}_m_in"), sem(f"{name}_m_ready")
            x1_in, stat_ready, xn_ready = sem(f"{name}_x1_in"), sem(f"{name}_stat_ready"), sem(f"{name}_xn_ready")
            p_full, p_used = sem(f"{name}_p_full"), sem(f"{name}_p_used")
            res_ready = sem(f"{name}_res_ready")
            proj = [psG[0], psU[0], psG[1], psU[1]]
        out_v = out_d.rearrange("(i p) d -> i p d", p=P)
        if not final:
            zeroed, tail = sem(f"{name}_zeroed"), sem(f"{name}_tail")
            raw_in = [sem(f"{name}_raw_in{i}") for i in range(2)]
            o_out = [sem(f"{name}_o_out{i}") for i in range(2)]
            s_hi, s_lo, o_free = sem(f"{name}_s_hi"), sem(f"{name}_s_lo"), sem(f"{name}_o_free")
            passed = sem(f"{name}_passed")
            tiles = env.ys_d.rearrange("(i p) d -> i p d", p=P)
            unused = (MAXT - MINTILES) // GROUPS


        @block.sync
        def _(sp):
            if not final:
                sp.wait_ge(zeroed, 1)
            with sp.Fori(0, GROUPS // 2) as gp:
                for b in range(2):
                    g = 2 * gp + b
                    sp.wait_ge(gu_full, (g + 1) * blocks + 2)
                    for h in range(2):
                        if final:
                            for j in range(GT):
                                sp.dma_start(f(x2[b][h][:, :, j * P:(j + 1) * P]), at(xT_d[h], g * GT + j))\
                                  .then_inc(x_in[b], 16)
                        else:
                            sp.dma_start(f(x2[b][h][:, :, :]), at(xT_d[h], g)).then_inc(x_in[b], 16)
                    if final:
                        sp.dma_start(cmb[b][:, :], at(env.comb_d.rearrange("(g j) t -> g (j t)", j=GT), g)
                                     .unsqueeze(0).to_broadcast([P, G])).then_inc(x_in[b], 16)
                    if not final:
                        for k in range(unused):
                            sp.dma_start(at(tiles, MINTILES + g * unused + k), zrow[:, :]).then_inc(tail, 16)
                    if stream:
                        for m in range(blocks):
                            sp.wait_ge(gu_full, g * blocks + m + 2 * blocks + 1 - RW)
                            for h in range(2):
                                sp.dma_start(f(gu[m % RW][h][:, :, :, :]), wgu[h, m]).then_inc(w_in[m % RW], 16)
                            if m == blocks // 2:
                                sp.wait_ge(res_ready, g * GT + 1)
                                sp.dma_start(x1[:, :, :], at(env.x1_d.rearrange("(g j p) d -> g p j d", j=GT, p=P), g))\
                                  .then_inc(x1_in, 16)
            if not final:
                sp.wait_ge(tail, 16 * unused * GROUPS)

        @block.gpsimd
        def _(pool):
            done, buf = (res_ready, res) if final else (y_ready, y)

            def store(g):
                for j in range(GT):
                    pool.wait_ge(done, g * GT + j + 1 + (1 if final else GT))
                    pool.dma_start(at(out_v, g * GT + j), buf[j % 2][:, :]).then_inc(y_out[j % 2], 16)
                    pool.wait_ge(y_out[j % 2], g * (16 * GT // 2) + 16 * (j // 2 + 1))
                    pool.sem_inc(y_free, 1)
            if final:
                with pool.Fori(0, B) as bt:
                    for h in range(2):
                        pool.dma_start(f(m2[h][:, :, :]), at(env.m_d[:, h], bt)).then_inc(m_in, 16)
                    pool.dma_start(cb[:, :], at(env.cb_d, bt)).then_inc(m_in, 16)
                    pool.wait_ge(m_in, 48 * bt + 48)
                    pool.sem_inc(m_ready, GROUPS // B)
                    with pool.Fori(0, GROUPS // B) as g:
                        store(bt * (GROUPS // B) + g)
            else:
                pool.memset(zrow[:, :], 0.0).then_inc(zeroed, 1)

                def load_raw(g):
                    for k in range(2):
                        blk = at(env.wgu1, 2 * g + k) if not isinstance(g, int) else env.wgu1[2 * g + k]
                        pool.dma_start(raw1[k][:, :, :, :], blk).then_inc(raw_in[k], 16)

                def store_split(g):
                    for k in range(2):
                        pool.wait_ge(s_lo, 2 * g + k + 1)
                        pool.sem_inc(passed, 1)
                        for h in range(2):
                            dst = env.wgu1_d[h]
                            dst = at(dst, 2 * g + k) if not isinstance(g, int) else dst[2 * g + k]
                            pool.dma_start(dst, f(out1[k][h][:, :, :, :])).then_inc(o_out[k], 16)

                def free_split(g):
                    for k in range(2):
                        pool.wait_ge(o_out[k], 32 * g + 32)
                    pool.sem_inc(o_free, 1)
                with pool.Fori(0, GROUPS) as g:
                    load_raw(g)
                    store_split(g)
                    store(g)
                    free_split(g)
                load_raw(GROUPS)
                store_split(GROUPS)
                free_split(GROUPS)

        @block.tensor
        def _(pe):
            with pe.Fori(0, GROUPS // 2) as gp:
                for b in range(2):
                    g = 2 * gp + b
                    m0 = g * blocks

                    def down_of(m):
                        pe.wait_ge(h_split, m0 + m + 1)
                        k = width(m)
                        for j in range(GT):
                            if m == 0:
                                pe.wait_ge(y_ready, g * GT + j + 1)
                            ins = mm3(pe, psY[j][:, :], [h2[m % 2][h][0:k, j * P:(j + 1) * P] for h in range(2)],
                                      [wd[h][0:k, m, :] for h in range(2)], m == 0, m == blocks - 1)
                        ins.then_inc(d_done, 1)
                    pe.wait_ge(x_in[b], XN * (gp + 1))
                    def attend(j):
                        if j % 2 == 0:
                            pe.wait_ge(h_ready, m0 + blocks + 1 + j // 2)
                        for c in range(KC):
                            ins = mm3(pe, proj[j][:, :], [x2[b][h][:, c, j * P:(j + 1) * P] for h in range(2)],
                                      [m2[h][:, c, :] for h in range(2)], c == 0, c == KC - 1)
                        ins.then_inc(p_full, 1)
                    for m in range(blocks):
                        if final and m < 2:
                            pe.wait_ge(p_used, g * GT + 2 * m + 2)
                        if stream:
                            pe.wait_ge(w_in[m % RW], 32 * (g * (blocks // RW) + m // RW + 1))
                        pe.wait_ge(h_ready, m0 + m + 1)
                        k = width(m)
                        for a, dst in ((0, psG), (1, psU)):
                            for c in range(KC):
                                if stream:
                                    w = [gu[m % RW][h][:, c, a, :] for h in range(2)]
                                else:
                                    w = [gu[0][h][:, c, a, m * P:m * P + k] for h in range(2)]
                                ins = mm3(pe, dst[m % 2][0:k, :], w, [x2[b][h][:, c, :] for h in range(2)],
                                          c == 0, c == KC - 1)
                        ins.then_inc(gu_full, 1)
                        if m:
                            down_of(m - 1)
                    if final:
                        pe.wait_ge(m_ready, g + 1)
                        attend(0)
                        attend(1)
                    down_of(blocks - 1)
                    if final:
                        attend(2)
                        attend(3)

        @block.scalar
        def _(act):
            def split(g, k):
                act.wait_ge(o_free, g + 1)
                act.wait_ge(raw_in[k], 16 * g + 16)
                act.activation(out1[k][0][:, :, :, :], raw1[k][:, :, :, :], ACT.Copy).then_inc(s_hi, 1)
            with act.Fori(0, GROUPS) as g:
                m0 = g * blocks

                def hi(m):
                    act.wait_ge(d_done, m0 + m + 1)
                    act.wait_ge(h_ready, m0 + m + 3)
                    k = width(m)
                    act.activation(h2[m % 2][0][0:k, :], hv[m % 2][0:k, :], ACT.Copy).then_inc(h_hi, 1)
                for m in range(blocks):
                    act.wait_ge(gu_full, m0 + m + 1 + 2 * blocks)
                    act.wait_ge(h_ready, m0 + m + 1)
                    k = width(m)
                    act.activation(sg[m % 2][0:k, :], psG[m % 2][0:k, :], ACT.Silu).then_inc(sg_ready, 1)
                    hi(m)
                    if not final and m in SPLIT_AT:
                        split(g, SPLIT_AT.index(m))
                    if final and m == blocks - 5:
                        act.wait_ge(x1_in, 16 * g + 16)
                        act.wait_ge(stat_ready, g + 1)
                        for j in range(GT):
                            ins = act.activation(xn[:, j, :], x1[:, j, :], ACT.Identity, bias=stat[:, j, 1:2],
                                                 scale=stat[:, j, 0:1])
                        ins.then_inc(xn_ready, 1)
                for j in range(GT):
                    act.wait_ge(d_done, m0 + blocks + 2)
                    act.wait_ge(y_free, g * GT + j + 1)
                    act.activation(y[j % 2][:, :], psY[j][:, :], ACT.Silu if final else ACT.Copy).then_inc(y_ready, 1)
            if not final:
                split(GROUPS, 0)
                split(GROUPS, 1)

        @block.vector
        def _(dve):
            for s, k in ((gu_full, 2 * blocks), (h_ready, 2), (d_done, 2), (y_ready, GT), (y_free, 2)):
                dve.sem_inc(s, k)
            def split(g, k):
                dve.wait_ge(s_hi, 2 * g + k + 1)
                dve.tensor_tensor(out1[k][1][:, :, :, :], raw1[k][:, :, :, :], f(out1[k][0][:, :, :, :]), ALU.subtract)\
                   .then_inc(s_lo, 1)
            if not final:
                dve.sem_inc(o_free, 1)
            if final:
                dve.sem_inc(res_ready, 1)
                dve.sem_inc(p_used, GT)
            with dve.Fori(0, GROUPS // 2) as gp:
                for b in range(2):
                    g = 2 * gp + b
                    m0 = g * blocks
                    c = Chain(dve, dve_step, g * NR)
                    for m in range(blocks):
                        if final and m == 4:
                            c(dve.tensor_copy(stat[:, :, :], env.stat[:, bass.ds(g * GT, GT), :]))
                            c.wait()
                            dve.sem_inc(stat_ready, 1)
                        k = width(m)
                        dve.wait_ge(sg_ready, m0 + m + 1)
                        ins = dve.tensor_tensor(hv[m % 2][0:k, :], sg[m % 2][0:k, :], psU[m % 2][0:k, :], ALU.mult)
                        if routed(m):
                            c(ins)
                            c.wait()
                            dve.wait_ge(x_in[b], XN * (gp + 1))
                            ins = dve.tensor_tensor(hv[m % 2][0:k, :], hv[m % 2][0:k, :], cmb[b][0:k, :], ALU.mult)
                        ins.then_inc(h_ready, 1)
                        dve.wait_ge(h_hi, m0 + m + 1)
                        dve.tensor_tensor(h2[m % 2][1][0:k, :], hv[m % 2][0:k, :], f(h2[m % 2][0][0:k, :]),
                                          ALU.subtract).then_inc(h_split, 1)
                        if not final and m in SPLIT_AT:
                            split(g, SPLIT_AT.index(m))
                    if final:
                        for j in range(GT):
                            r = res[j % 2][:, :]
                            dve.wait_ge(y_free, g * GT + j + 1)
                            dve.wait_ge(p_full, g * GT + j + 1)
                            dve.scalar_tensor_tensor(r, proj[j][:, :], stat[:, j, 2:3], cb[:, :], ALU.mult, ALU.add)\
                               .then_inc(p_used, 1)
                            dve.wait_ge(p_used, g * GT + j + 1 + GT)
                            dve.wait_ge(xn_ready, g + 1)
                            c(dve.tensor_tensor(r, r, xn[:, j, :], ALU.add))
                            c.wait()
                            dve.wait_ge(y_ready, g * GT + j + 1 + GT)
                            c(dve.tensor_tensor(r, r, y[j % 2][:, :], ALU.mult))
                            c.wait()
                            dve.tensor_tensor(r, r, x1[:, j, :], ALU.add).then_inc(res_ready, 1)
            if not final:
                split(GROUPS, 0)
                split(GROUPS, 1)


def phase_experts(nc, env):
    ctx, sb, ps, sem = scope(nc)
    with ctx:
        raw_gu = [sb(f"e_rawgu{i}", [P, KC, 2, M]) for i in range(2)]
        raw_d = [sb(f"e_rawd{i}", [P, MC, D]) for i in range(2)]
        gu = [[sb(f"e_gu{i}{h}", [P, KC, 2, M], F32R) for h in range(2)] for i in range(2)]
        wd = [[sb(f"e_wd{i}{h}", [P, MC, D], F32R) for h in range(2)] for i in range(2)]
        idx = sb("e_idx", [P, 1], I32)
        xg = sb("e_xg", [P, D])
        xT = [sb(f"e_xT{h}", [P, KC, P], F32R) for h in range(2)]
        sg = sb("e_sg", [P, M])
        hv = sb("e_h", [P, M])
        hT = [sb(f"e_hT{h}", [P, MC, P], F32R) for h in range(2)]
        y = sb("e_y", [P, D])
        psX = ps("e_psX", [P, KC, P])
        psH = ps("e_psH", [P, MC, P])
        psG = ps("e_psG", [P, D])
        psU = ps("e_psU", [P, D])
        psY = ps("e_psY", [P, D])

        CR = 3
        done = lambda i: i + 1 + CR
        cleared, passed = sem("e_cleared"), sem("e_passed")
        w_in = [sem(f"e_w_in{i}") for i in range(2)]
        w_hi, w_split = sem("e_w_hi"), sem("e_w_split")
        idx_ready, x_in = sem("e_idx_ready"), sem("e_x_in")
        xT_full, xT_hi, xT_split = sem("e_xT_full"), sem("e_xT_hi"), sem("e_xT_split")
        gu_full, sg_ready, h_ready = sem("e_gu_full"), sem("e_sg_ready"), sem("e_h_ready")
        hT_full, hT_hi, hT_split = sem("e_hT_full"), sem("e_hT_hi"), sem("e_hT_split")
        y_full, y_ready, y_free, y_out = sem("e_y_full"), sem("e_y_ready"), sem("e_y_free"), sem("e_y_out")
        block = ctx.enter_context(nc.Block())
        ys_v = env.ys_d.rearrange("(i p) d -> i p d", p=P)

        def first_of(eng, e, most=MAXT):
            e = slice(e, e + 1) if isinstance(e, int) else bass.ds(e, 1)
            return eng.value_load(env.first[0:1, e], min_val=0, max_val=most)

        def experts(eng, begin, tile, split, load, finish):
            def one(e, half, b, first=False):
                start, end = first_of(eng, e, MAXT - MINT), first_of(eng, e + 1)
                begin(e)
                for j in range(3):
                    part = lambda: None
                    if not (isinstance(e, int) and e == E - 1):
                        part = lambda: split(e + 1, half + b, 1 - b, start, j)
                    tile(start + j, b, b if j == 2 else None if first else 1 - b, j, part)
                with eng.Fori(start + 3, end) as i:
                    tile(i, b, b, 2, lambda: None)
                if not (isinstance(e, int) and e + 3 >= E):
                    load(e + 3, 1 - b)
            load(0, 0)
            load(1, 1)
            for j in range(3):
                split(0, 0, 0, None, j)
            load(2, 0)
            one(0, 0, 0, True)
            with eng.Fori(0, E // 2 - 2) as ep:
                one(2 * ep + 1, ep, 1)
                one(2 * ep + 2, ep + 1, 0)
            for e in range(E - 3, E):
                one(e, e // 2, e % 2)
            finish(first_of(eng, E), 1)

        nothing = lambda *_: None

        @block.gpsimd
        def _(pool):
            for i in range(2):
                pool.memset(raw_d[i][:, :, :], 0.0).then_inc(cleared, 1)
            total = first_of(pool, E)
            with pool.Fori(0, total) as i:
                pool.wait_ge(xT_full, done(i - 1))
                pool.sem_inc(passed, 1)
                pool.tensor_copy(idx[:, :], env.ids[:, bass.ds(i, 1)]).then_inc(idx_ready, 1)
                pool.wait_ge(idx_ready, i + 1)
                pool.sem_inc(passed, 1)
                pool.indirect_dma_start(xg[:, :], None, env.xn_d,
                                        bass.IndirectOffsetOnAxis(ap=idx[:, :].bitcast(U32), axis=0))\
                    .then_inc(x_in, 16)

        @block.sync
        def _(sp):
            sp.wait_ge(cleared, 2)

            def load(e, b):
                if not (isinstance(e, int) and e < 2):
                    sp.wait_ge(w_split, e - 1)
                wgt = lambda w: w[e] if isinstance(e, int) else at(w, e)
                for a, w in enumerate((env.w_gate, env.w_up)):
                    sp.dma_start(raw_gu[b][:, :, a, :], wgt(w).rearrange("(c p) m -> p c m", p=P)).then_inc(w_in[b], 16)
                sp.dma_start(raw_d[b][:, 0:MC - 1, :],
                              wgt(env.w_down)[0:2 * P, :].rearrange("(c p) n -> p c n", p=P)).then_inc(w_in[b], 16)
                sp.dma_start(raw_d[b][0:MR, MC - 1, :], wgt(env.w_down)[2 * P:M, :]).then_inc(w_in[b], 16)

            def store(i, *_):
                sp.wait_ge(y_ready, done(i))
                sp.dma_start(at(ys_v, i), y[:, :]).then_inc(y_out, 16)
                sp.wait_ge(y_out, 16 * i + 16)
                sp.sem_inc(y_free, 1)
            experts(sp, nothing, store, nothing, load, nothing)

        @block.tensor
        def _(pe):
            def turn_h(i):
                pe.wait_ge(h_ready, done(i))
                pe.wait_ge(hT_split, done(i - 1))
                for c in range(MC):
                    k = P if c < MC - 1 else MR
                    ins = pe.transpose(psH[0:k, c, :], hv[:, c * P:c * P + k], env.ident[:, :])
                ins.then_inc(hT_full, 1)

            def down(i, b):
                pe.wait_ge(hT_split, done(i))
                pe.wait_ge(y_ready, done(i - 1))
                for c in range(MC):
                    k = P if c < MC - 1 else MR
                    ins = mm3(pe, psY[:, :], [hT[h][0:k, c, :] for h in range(2)],
                              [wd[b][h][0:k, c, :] for h in range(2)], c == 0, c == MC - 1)
                ins.then_inc(y_full, 1)

            def tile(i, b, old, j, part):
                pe.wait_ge(x_in, 16 * i + 16)
                pe.wait_ge(xT_split, done(i - 1))
                for c in range(KC):
                    ins = pe.transpose(psX[:, c, :], xg[:, c * P:(c + 1) * P], env.ident[:, :])
                ins.then_inc(xT_full, 1)
                if old is not None:
                    down(i - 2, old)
                if old is not None or j:
                    turn_h(i - 1)
                pe.wait_ge(xT_split, done(i))
                pe.wait_ge(h_ready, done(i - 1))
                for a, dst in ((0, psG), (1, psU)):
                    for c in range(KC):
                        ins = mm3(pe, dst[:, 0:M], [xT[h][:, c, :] for h in range(2)],
                                  [gu[b][h][:, c, a, :] for h in range(2)], c == 0, c == KC - 1)
                ins.then_inc(gu_full, 1)

            def finish(n, b):
                down(n - 2, b)
                turn_h(n - 1)
                down(n - 1, b)
            experts(pe, lambda e: pe.wait_ge(w_split, e + 1), tile, nothing, nothing, finish)

        @block.scalar
        def _(act):
            def split(e, half, b, start, part):
                if part == 0:
                    act.wait_ge(w_in[b], 64 * (half + 1))
                if part < 2:
                    c = slice(2 * part, 2 * part + 2)
                    act.activation(gu[b][0][:, c, :, :], raw_gu[b][:, c, :, :], ACT.Copy).then_inc(w_hi, 1)
                else:
                    if start is not None:
                        act.wait_ge(y_full, done(start - 1))
                    act.activation(wd[b][0][:, :, :], raw_d[b][:, :, :], ACT.Copy).then_inc(w_hi, 1)

            def hi_h(i):
                act.wait_ge(y_full, done(i - 1))
                act.wait_ge(hT_full, done(i))
                act.activation(hT[0][:, :, :], psH[:, :, :], ACT.Copy).then_inc(hT_hi, 1)

            def tile(i, b, old, j, part):
                act.wait_ge(gu_full, done(i - 1))
                act.wait_ge(xT_full, done(i))
                act.activation(xT[0][:, :, :], psX[:, :, :], ACT.Copy).then_inc(xT_hi, 1)
                if old is not None or j:
                    hi_h(i - 1)
                part()
                act.wait_ge(gu_full, done(i))
                act.wait_ge(h_ready, done(i - 1))
                act.activation(sg[:, :], psG[:, 0:M], ACT.Silu).then_inc(sg_ready, 1)
            experts(act, nothing, tile, split, nothing, lambda n, b: hi_h(n - 1))

        @block.vector
        def _(dve):
            for s in (xT_full, xT_hi, xT_split, gu_full, sg_ready, h_ready, hT_full, hT_hi, hT_split,
                      y_full, y_ready, y_free):
                dve.sem_inc(s, CR)
            dve.memset(psH[:, :, :], 0.0)

            def split(e, half, b, start, part):
                dve.wait_ge(w_hi, 3 * e + part + 1)
                if part < 2:
                    c = slice(2 * part, 2 * part + 2)
                    dve.tensor_tensor(gu[b][1][:, c, :, :], raw_gu[b][:, c, :, :], f(gu[b][0][:, c, :, :]),
                                      ALU.subtract)
                else:
                    dve.tensor_tensor(wd[b][1][:, :, :], raw_d[b][:, :, :], f(wd[b][0][:, :, :]), ALU.subtract)\
                       .then_inc(w_split, 1)

            def lo_h(i):
                dve.wait_ge(hT_hi, done(i))
                dve.tensor_tensor(hT[1][:, :, :], psH[:, :, :], f(hT[0][:, :, :]), ALU.subtract).then_inc(hT_split, 1)

            def out(i):
                dve.wait_ge(y_free, done(i - 1))
                dve.wait_ge(y_full, done(i))
                dve.tensor_copy(y[:, :], psY[:, :]).then_inc(y_ready, 1)

            def tile(i, b, old, j, part):
                dve.wait_ge(xT_hi, done(i))
                dve.tensor_tensor(xT[1][:, :, :], psX[:, :, :], f(xT[0][:, :, :]), ALU.subtract).then_inc(xT_split, 1)
                if old is not None:
                    out(i - 2)
                if old is not None or j:
                    lo_h(i - 1)
                part()
                dve.wait_ge(sg_ready, done(i))
                dve.wait_ge(hT_full, done(i - 1))
                dve.tensor_tensor(hv[:, :], sg[:, :], psU[:, 0:M], ALU.mult).then_inc(h_ready, 1)

            def finish(n, b):
                out(n - 2)
                lo_h(n - 1)
                out(n - 1)
            experts(dve, nothing, tile, split, nothing, finish)


def phase_l1_weights(nc, env):
    ctx, sb, ps, sem = scope(nc)
    with ctx:
        w = sb("i_w", [P, KC, 3, D])
        wc = sb("i_wc", [P, KC, 3, D])
        gamma = sb("i_gamma", [P, KC])
        beta = sb("i_beta", [P, KC])
        brow = sb("i_brow", [1, 3, D])
        ones = sb("i_ones", [P, P])
        mean = sb("i_mean", [P, P])
        betar = sb("i_betar", [P, KC, P])
        bq = sb("i_bq", [P, D])
        psM = [ps(f"i_psM{a}", [P, D]) for a in range(3)]
        psB = [ps(f"i_psB{a}", [P, D]) for a in range(3)]
        psT = [ps(f"i_psT{a}", [P, D]) for a in range(2)]
        loaded, ready, scaled = sem("i_loaded"), sem("i_ready"), sem("i_scaled")
        summed, centred, hi_done, biased = sem("i_summed"), sem("i_centred"), sem("i_hi"), sem("i_biased")
        turned, t_used = sem("i_turned"), sem("i_t_used")
        block = ctx.enter_context(nc.Block())

        @block.sync
        def _(sp):
            sp.dma_start(w[:, :, :, :].rearrange("p c a n -> p c (a n)"), env.W_in.rearrange("(c p) n -> p c n", p=P))\
                .then_inc(loaded, 16)
            sp.dma_start(gamma[:, :], env.gamma).then_inc(loaded, 16)
            sp.dma_start(beta[:, :], env.beta).then_inc(loaded, 16)
            sp.dma_start(brow[:, :, :].rearrange("p a n -> p (a n)"), env.b_in.unsqueeze(0)).then_inc(loaded, 16)

        @block.gpsimd
        def _(pool):
            pool.memset(ones[:, :], 1.0).then_inc(ready, 1)
            pool.memset(mean[:, :], 1.0 / D).then_inc(ready, 1)

        @block.vector
        def _(dve):
            dve.wait_ge(loaded, 64)
            for c in range(KC):
                dve.tensor_scalar(wc[:, c, :, :], w[:, c, :, :], gamma[:, c:c + 1], None, ALU.mult)\
                    .then_inc(scaled, 1)
            dve.wait_ge(ready, 2)
            for c in range(KC):
                dve.tensor_scalar(betar[:, c, :], ones[:, :], beta[:, c:c + 1], None, ALU.mult).then_inc(scaled, 1)
            dve.wait_ge(summed, 1)
            dve.wait_ge(scaled, 2 * KC)
            for c in range(KC):
                for a in range(3):
                    dve.tensor_tensor(wc[:, c, a, :], wc[:, c, a, :], psM[a][:, :], ALU.subtract).then_inc(centred, 1)
            dve.wait_ge(summed, 2)
            dve.tensor_copy(bq[:, :], psB[0][:, :]).then_inc(biased, 1)
            for a in range(2):
                dve.tensor_copy(env.bkv[:, a, :], psB[1 + a][:, :])
            for c in range(KC):
                dve.wait_ge(hi_done, c + 1)
                dve.tensor_tensor(env.wkv1[1][:, c, :, :], wc[:, c, 1:3, :], f(env.wkv1[0][:, c, :, :]), ALU.subtract)
            for n in range(KC + 1):
                dve.wait_ge(turned, n + 1)
                src = psT[n % 2][:, :].rearrange("p (c k) -> p c k", c=KC)
                dst = env.wqT[:, n, :].rearrange("p (c k) -> p c k", c=KC) if n < KC else env.bqT[:, :, :]
                dve.tensor_copy(dst, src).then_inc(t_used, 1)

        @block.scalar
        def _(act):
            for c in range(KC):
                act.wait_ge(centred, 3 * c + 3)
                act.activation(env.wkv1[0][:, c, :, :], wc[:, c, 1:3, :], ACT.Copy).then_inc(hi_done, 1)

        @block.tensor
        def _(pe):
            pe.wait_ge(scaled, 2 * KC)
            pe.wait_ge(ready, 2)
            for a in range(3):
                for c in range(KC):
                    ins = pe.matmul(psM[a][:, :], mean[:, :], wc[:, c, a, :], start=c == 0, stop=c == KC - 1)
            ins.then_inc(summed, 1)
            for a in range(3):
                for c in range(KC):
                    pe.matmul(psB[a][:, :], betar[:, c, :], w[:, c, a, :], start=c == 0, stop=False)
                ins = pe.matmul(psB[a][:, :], ones[0:1, :], brow[:, a, :], start=False, stop=True)
            ins.then_inc(summed, 1)
            for n in range(KC + 1):
                if n >= 2:
                    pe.wait_ge(t_used, n - 1)
                pe.wait_ge(centred, 3 * KC) if n < KC else pe.wait_ge(biased, 1)
                for c in range(KC):
                    src = wc[:, c, 0, n * P:(n + 1) * P] if n < KC else bq[:, c * P:(c + 1) * P]
                    ins = pe.transpose(psT[n % 2][:, c * P:(c + 1) * P], src, env.ident[:, :])
                ins.then_inc(turned, 1)


def phase_combine(nc, env):
    ctx, sb, ps, sem = scope(nc)
    with ctx:
        y6 = [sb(f"c_y6{i}", [P, TOPK, D]) for i in range(2)]
        slot6 = [sb(f"c_slot6{i}", [P, TOPK], I32) for i in range(2)]
        w6 = sb("c_w6", [P, TOPK])
        sh, s_in, x = ([sb(f"c_{n}{i}", [P, D]) for i in range(2)] for n in ("sh", "s", "x"))
        acc = sb("c_acc", [P, D])
        g = sb("c_g", [P, D])
        x1 = [sb(f"c_x1{i}", [P, D]) for i in range(2)]
        xn = [sb(f"c_xn{i}", [P, D]) for i in range(2)]
        st = sb("c_st", [P, 6])
        mv = sb("c_mv", [P, 2])
        var = sb("c_var", [P, 1])
        var2 = [sb(f"c_var2{i}", [P, 1]) for i in range(2)]
        stat = [sb(f"c_stat{i}", [P, 3]) for i in range(2)]
        r, nmr, r2 = ([s[:, i:i + 1] for s in stat] for i in range(3))
        tmp, tmp_2, tmp_n = (sb("c_" + n, [P, 1]) for n in ("tmp", "tmp_2", "tmp_n"))
        xT = [[sb(f"c_xT{i}{h}", [P, KC, P], F32R) for h in range(2)] for i in range(2)]
        wr = [sb(f"c_wr{h}", [P, KC, NROUTED], F32R) for h in range(2)]
        wr_raw = sb("c_wr_raw", [P, KC, NROUTED])
        trig = [sb(f"c_trig{i}", [P, 2, 2 * RH]) for i in range(2)]
        kv = [sb(f"c_kv{i}", [P, 2, D]) for i in range(2)]
        rc = sb("c_rc", [P, 2, 2 * RH])
        rs = sb("c_rs", [P, 2, RH, 2])
        prod = [sb(f"c_prod{i}", [P, D]) for i in range(2)]
        sq = sb("c_sq", [P, 2, D])
        n2 = [sb(f"c_n2{i}", [P, 2]) for i in range(2)]
        nn = [sb(f"c_nn{i}", [P, 1]) for i in range(2)]
        rn = [sb(f"c_rn{i}", [P, 1]) for i in range(2)]
        psX = [ps(f"c_psX{i}", [P, KC, P]) for i in range(2)]
        psK = [ps(f"c_psK{i}", [P, 2, D]) for i in range(2)]
        psL = ps("c_psL", [P, NROUTED])
        psA = ps("c_psA", [P, KC])

        CR = 2
        done = lambda i: i + 1 + CR
        q_acc, q_g, q_x1, q_var, q_root, q_norm = (sem("c_" + n) for n in ("q_acc", "q_g", "q_x1", "q_var", "q_root", "q_norm"))
        q_root2, q_xn, q_x_full, q_x_hi, q_x_split = (sem("c_" + n) for n in ("q_root2", "q_xn", "q_x_full", "q_x_hi", "q_x_split"))
        q_kv_full, q_kv, q_sq, q_nn, q_n_root, q_rn = (sem("c_" + n) for n in ("q_kv_full", "q_kv", "q_sq", "q_nn", "q_n_root", "q_rn"))
        q_prod, q_a_full, q_a_used, q_l_used, q_out = (sem("c_" + n) for n in ("q_prod", "q_a_full", "q_a_used", "q_l_used", "q_out"))
        credited = (q_acc, q_g, q_x1, q_var, q_root, q_norm, q_root2, q_xn, q_x_full, q_x_hi, q_x_split, q_kv_full,
                    q_kv, q_sq, q_nn, q_n_root, q_rn, q_prod, q_a_full, q_a_used, q_l_used, q_out)
        ld_in = [sem(f"c_ld_in{i}") for i in range(2)]
        y_in = [sem(f"c_y_in{i}") for i in range(2)]
        trig_in = [sem(f"c_trig_in{i}") for i in range(2)]
        x1_out = [sem(f"c_x1_out{i}") for i in range(2)]
        xT_out = [sem(f"c_xT_out{i}") for i in range(2)]
        copied, passed, rot = sem("c_copied"), sem("c_passed"), sem("c_rot")
        step_1, step_2, step_n = sem("c_step_1"), sem("c_step_2"), sem("c_step_n")
        wr_in, wr_hi, wr_split = sem("c_wr_in"), sem("c_wr_hi"), sem("c_wr_split")
        block = ctx.enter_context(nc.Block())
        tiles = lambda d: d.rearrange("(i p) d -> i p d", p=P)

        def loop(eng, first, second, ahead=1):
            def both(t, b, tp, first, second):
                if first:
                    first(t + ahead, (b + ahead) % 2, tp + (b + ahead) // 2)
                second(t, b, tp)
            for t in range(ahead):
                first(t, t % 2, t // 2)
            for t in range(4):
                both(t, t % 2, t // 2, first, second)
            last = (TILES - 1 - ahead) // 2
            with eng.Fori(2, last) as tp:
                for b in range(2):
                    both(2 * tp + b, b, tp, first, second)
            for t in range(2 * last, TILES):
                both(t, t % 2, t // 2, first if t + ahead < TILES else None, second)

        from_ = lambda t, k: not isinstance(t, int) or t >= k
        one = lambda t: slice(t, t + 1) if isinstance(t, int) else bass.ds(t, 1)
        pick = lambda d, t: d[t] if isinstance(t, int) else at(d, t)

        @block.sync
        def _(sp):
            sp.dma_start(wr_raw[:, :, :], env.router_w.rearrange("(c p) n -> p c n", p=P)).then_inc(wr_in, 16)

            def first(t, b, tp):
                sp.wait_ge(q_x1, done(t - 2))
                for dst, src in ((sh, env.sh_d), (s_in, env.s_d), (x, env.x)):
                    sp.dma_start(dst[b][:, :], pick(tiles(src), t)).then_inc(ld_in[b], 16)

            def second(t, b, tp):
                sp.wait_ge(q_x1, done(t))
                sp.dma_start(pick(tiles(env.x1_d), t), x1[b][:, :]).then_inc(x1_out[b], 16)
                sp.wait_ge(q_x_split, done(t))
                for h in range(2):
                    sp.dma_start(pick(env.xT1_d[h], t), f(xT[b][h][:, :, :])).then_inc(xT_out[b], 16)
                sp.wait_ge(x1_out[b], 16 * tp + 16)
                sp.wait_ge(xT_out[b], 32 * tp + 32)
                sp.sem_inc(q_out, 1)
            loop(sp, first, second, 3)

        @block.gpsimd
        def _(pool):
            def first(t, b, tp):
                pool.wait_ge(q_acc, done(t - 2))
                pool.sem_inc(passed, 1)
                pool.tensor_copy(slot6[b][:, :], env.slot_i[:, one(t), :].rearrange("p a k -> p (a k)"))\
                    .then_inc(copied, 1)
                pool.wait_ge(copied, t + 1)
                pool.sem_inc(passed, 1)
                for k in range(TOPK):
                    pool.indirect_dma_start(y6[b][:, k, :], None, env.ys_d,
                                            bass.IndirectOffsetOnAxis(ap=slot6[b][:, k:k + 1].bitcast(U32), axis=0))\
                        .then_inc(y_in[b], 16)

            def second(t, b, tp):
                pool.wait_ge(trig_in[b], 16 * tp + 16)
                pool.wait_ge(q_prod, done(t - 1))
                pool.wait_ge(q_kv, done(t))
                pool.tensor_tensor(rc[:, :, :], kv[b][:, :, 0:2 * RH],
                                   trig[b][:, 0:1, :].to_broadcast([P, 2, 2 * RH]), ALU.mult).then_inc(rot, 1)
                pairs = kv[b][:, :, 0:2 * RH].rearrange("p a (i o) -> p a i o", o=2)
                sines = trig[b][:, 1:2, :].rearrange("p a (i o) -> p a i o", o=2)
                for o in range(2):
                    pool.tensor_tensor(rs[:, :, :, o], pairs[:, :, :, 1 - o],
                                       sines[:, :, :, o].to_broadcast([P, 2, RH]), ALU.mult).then_inc(rot, 1)
                pool.wait_ge(rot, 4 * t + 3)
                pool.tensor_tensor(rc[:, :, :], rc[:, :, :], rs[:, :, :, :].rearrange("p a i o -> p a (i o)"), ALU.add)\
                    .then_inc(rot, 1)
                pool.wait_ge(q_a_full, done(t - 2))
                pool.tensor_tensor(prod[b][:, 2 * RH:D], kv[b][:, 0, 2 * RH:D], kv[b][:, 1, 2 * RH:D], ALU.mult)
                pool.wait_ge(rot, 4 * t + 4)
                pool.tensor_tensor(prod[b][:, 0:2 * RH], rc[:, 0, :], rc[:, 1, :], ALU.mult).then_inc(q_prod, 1)
                if not isinstance(t, int) or t + 2 < TILES:
                    pool.wait_ge(rot, 4 * t + 4)
                    pool.sem_inc(passed, 1)
                    pool.dma_start(trig[b][:, :, :], pick(env.trig, t + 2)).then_inc(trig_in[b], 16)
            for t in range(2):
                pool.dma_start(trig[t][:, :, :], env.trig[t]).then_inc(trig_in[t], 16)
            loop(pool, first, second, 4)

        @block.scalar
        def _(act):
            act.wait_ge(wr_in, 16)
            act.activation(wr[0][:, :, :], wr_raw[:, :, :], ACT.Copy).then_inc(wr_hi, 1)

            def first(t, b, tp):
                act.wait_ge(q_xn, done(t - 2))
                act.wait_ge(q_x1, done(t - 1))
                act.wait_ge(q_acc, done(t))
                act.activation(g[:, :], acc[:, :], ACT.Silu).then_inc(q_g, 1)
                act.wait_ge(q_var, done(t))
                act.activation(r[b][:, :], var[:, :], ACT.Sqrt).then_inc(q_root, 1)
                act.wait_ge(q_norm, done(t))
                act.wait_ge(q_x_full, done(t - 2))
                act.activation(xn[b][:, :], x1[b][:, :], ACT.Identity, bias=nmr[b][:, :], scale=r[b][:, :])\
                    .then_inc(q_xn, 1)
                act.wait_ge(q_kv, done(t - 2))
                act.activation(r2[b][:, :], var2[b][:, :], ACT.Sqrt).then_inc(q_root2, 1)

            def n_root(t, b):
                act.wait_ge(q_a_full, done(t - 2))
                act.wait_ge(q_nn, done(t))
                act.activation(rn[b][:, :], nn[b][:, :], ACT.Sqrt).then_inc(q_n_root, 1)

            def second(t, b, tp):
                act.wait_ge(q_x_full, done(t))
                act.wait_ge(q_out, done(t - 2))
                act.activation(xT[b][0][:, :, :], psX[b][:, :, :], ACT.Copy).then_inc(q_x_hi, 1)
                if from_(t, 2):
                    n_root(t - 2, b)
                if from_(t, 1):
                    squares(t - 1, 1 - b)

            def squares(t, b):
                act.wait_ge(q_kv, done(t))
                for a in range(2):
                    ins = act.activation(sq[:, a, :], kv[b][:, a, :], ACT.Square, accum_out=n2[b][:, a:a + 1])
                ins.then_inc(q_sq, 1)
            loop(act, first, second)
            n_root(TILES - 2, 0)
            squares(TILES - 1, 1)
            n_root(TILES - 1, 1)

        @block.vector
        def _(dve):
            for s in credited:
                dve.sem_inc(s, CR)
            dve.wait_ge(wr_hi, 1)
            dve.tensor_tensor(wr[1][:, :, :], wr_raw[:, :, :], f(wr[0][:, :, :]), ALU.subtract).then_inc(wr_split, 1)
            N1, N2, NN = 17, 5, 5

            def first(t, b, tp):
                c = Chain(dve, step_1, t * N1)
                dve.wait_ge(ld_in[b], 48 * tp + 48)
                dve.wait_ge(y_in[b], 16 * TOPK * (tp + 1))
                c(dve.tensor_copy(w6[:, :], env.wexp[:, one(t), :].rearrange("p a k -> p (a k)")))
                c.wait()
                dve.wait_ge(q_g, done(t - 1))
                for k in range(TOPK):
                    src = sh[b] if k == 0 else acc
                    ins = dve.scalar_tensor_tensor(acc[:, :], y6[b][:, k, :], w6[:, k:k + 1], src[:, :],
                                                   ALU.mult, ALU.add)
                    if k < TOPK - 1:
                        c(ins)
                        c.wait()
                ins.then_inc(q_acc, 1)
                dve.wait_ge(q_g, done(t))
                c(dve.tensor_tensor(s_in[b][:, :], s_in[b][:, :], g[:, :], ALU.mult))
                c.wait()
                dve.wait_ge(q_out, done(t - 2))
                dve.wait_ge(q_xn, done(t - 2))
                dve.tensor_tensor(x1[b][:, :], s_in[b][:, :], x[b][:, :], ALU.add).then_inc(q_x1, 1)
                dve.wait_ge(q_x1, done(t))
                c(dve.bn_stats(st[:, :], x1[b][:, :]))
                c.wait()
                c(dve.memset(tmp[:, :], 0.0))
                c(dve.bn_aggr(mv[:, :], st[:, :]))
                c.wait()
                dve.tensor_scalar(var[:, :], mv[:, 1:2], EPS, None, ALU.add).then_inc(q_var, 1)
                dve.wait_ge(q_root, done(t))
                rstd_chain(dve, c, var[:, :], r[b], tmp)
                dve.wait_ge(q_root2, done(t - 2))
                c(dve.scalar_tensor_tensor(var2[b][:, :], r[b][:, :], r[b][:, 0:1], mv[:, 1:2], ALU.mult, ALU.mult))
                c.wait()
                c(dve.tensor_scalar(var2[b][:, :], var2[b][:, :], EPS, None, ALU.add))
                c.wait()
                dve.tensor_scalar(nmr[b][:, :], mv[:, 0:1], r[b][:, 0:1], -1.0, ALU.mult, ALU.mult).then_inc(q_norm, 1)
                assert c.n == N1, c.n

            def norms(t, b):
                dve.wait_ge(q_sq, done(t))
                dve.tensor_tensor(nn[b][:, :], n2[b][:, 0:1], n2[b][:, 1:2], ALU.mult).then_inc(q_nn, 1)

            def over_norms(t, b):
                c = Chain(dve, step_n, t * NN)
                dve.wait_ge(q_n_root, done(t))
                rstd_chain(dve, c, nn[b][:, :], rn[b], tmp_n)
                dve.sem_inc(q_rn, 1)

            def similar(t):
                dve.wait_ge(q_a_full, done(t))
                dve.tensor_copy(env.aparts[:, one(t), :].rearrange("p a k -> p (a k)"), psA[:, :]).then_inc(q_a_used, 1)

            def keys(t, b):
                dve.wait_ge(q_prod, done(t - 2))
                dve.wait_ge(q_kv_full, done(t))
                dve.scalar_tensor_tensor(kv[b][:, :, :], psK[b][:, :, :], r2[b][:, 0:1], env.bkv[:, :, :],
                                         ALU.mult, ALU.add).then_inc(q_kv, 1)
                dve.tensor_copy(env.logits1[:, one(t), :].rearrange("p a k -> p (a k)"), psL[:, :]).then_inc(q_l_used, 1)

            def second(t, b, tp):
                if from_(t, 2):
                    norms(t - 2, b)
                if from_(t, 1):
                    keys(t - 1, 1 - b)
                c = Chain(dve, step_2, t * N2)
                dve.wait_ge(q_root2, done(t))
                rstd_chain(dve, c, var2[b][:, :], r2[b], tmp_2)
                dve.tensor_copy(env.stat[:, one(t), :].rearrange("p a k -> p (a k)"), stat[b][:, :])
                dve.wait_ge(q_x_hi, done(t))
                dve.tensor_tensor(xT[b][1][:, :, :], psX[b][:, :, :], f(xT[b][0][:, :, :]), ALU.subtract)\
                   .then_inc(q_x_split, 1)
                if from_(t, 2):
                    over_norms(t - 2, b)
                if from_(t, 3):
                    similar(t - 3)
            loop(dve, first, second)
            norms(TILES - 2, 0)
            keys(TILES - 1, 1)
            over_norms(TILES - 2, 0)
            similar(TILES - 3)
            norms(TILES - 1, 1)
            over_norms(TILES - 1, 1)
            similar(TILES - 2)
            similar(TILES - 1)

        @block.tensor
        def _(pe):
            pe.wait_ge(wr_split, 1)

            def first(t, b, tp):
                pass

            def sums(t, b):
                pe.wait_ge(q_prod, done(t))
                pe.wait_ge(q_rn, done(t))
                pe.wait_ge(q_a_used, done(t - 1))
                for c in range(KC):
                    ins = pe.matmul(psA[:, c:c + 1], prod[b][:, c * P:(c + 1) * P], rn[b][:, :], start=True, stop=True)
                ins.then_inc(q_a_full, 1)

            def second(t, b, tp):
                pe.wait_ge(q_x_split, done(t - 2))
                pe.wait_ge(q_xn, done(t))
                for c in range(KC):
                    ins = pe.transpose(psX[b][:, c, :], xn[b][:, c * P:(c + 1) * P], env.ident[:, :])
                ins.then_inc(q_x_full, 1)
                pe.wait_ge(q_x_split, done(t))
                pe.wait_ge(q_l_used, done(t - 1))
                for c in range(KC):
                    mm3(pe, psL[:, :], [xT[b][h][:, c, :] for h in range(2)], [wr[h][:, c, :] for h in range(2)],
                        c == 0, c == KC - 1)
                pe.wait_ge(q_kv, done(t - 2))
                for a in range(2):
                    for c in range(KC):
                        ins = mm3(pe, psK[b][:, a, :], [xT[b][h][:, c, :] for h in range(2)],
                                  [env.wkv1[h][:, c, a, :] for h in range(2)], c == 0, c == KC - 1)
                ins.then_inc(q_kv_full, 1)
                if from_(t, 2):
                    sums(t - 2, b)
            loop(pe, first, second)
            sums(TILES - 2, 0)
            sums(TILES - 1, 1)


def phase_similarity(nc, env):
    ctx, sb, ps, sem = scope(nc)
    with ctx:
        wout = sb("m_wout", [P, KC, D])
        aw = [sb(f"m_aw{i}", [P, KC, D]) for i in range(B)]
        a = sb("m_a", [P, B, KC])
        bout = sb("m_bout", [1, D])
        ones = sb("m_ones", [1, P])
        hi = [sb(f"m_hi{i}", [P, KC, D], F32R) for i in range(B)]
        lo = [sb(f"m_lo{i}", [P, KC, D], F32R) for i in range(B)]
        cb = sb("m_cb", [P, B, D])
        v8 = sb("m_v8", [P, TILES, 8])
        e = sb("m_e", [P, TILES])
        w0 = sb("m_w0", [P, TILES])
        comb = sb("m_comb", [P, TILES])
        rows = sb("m_rows", [TILES, P])
        psM = [ps(f"m_psM{i}", [P, D]) for i in range(4)]
        psC = [ps(f"m_psC{i}", [P, D]) for i in range(B)]
        psT = ps("m_psT", [TILES, P])
        loaded, ready, dve_step = sem("m_loaded"), sem("m_ready"), sem("m_dve")
        diff, exped, combined, turned = sem("m_diff"), sem("m_exped"), sem("m_combined"), sem("m_turned")
        scaled, full, m_hi, m_used = sem("m_scaled"), sem("m_full"), sem("m_m_hi"), sem("m_m_used")
        c_full, c_ready, rows_ready, out = sem("m_c_full"), sem("m_c_ready"), sem("m_rows_ready"), sem("m_out")
        block = ctx.enter_context(nc.Block())

        @block.gpsimd
        def _(pool):
            pool.memset(ones[:, :], 1.0).then_inc(ready, 1)

        @block.sync
        def _(sp):
            sp.dma_start(wout[:, :, :], env.W_out.rearrange("(c p) n -> p c n", p=P)).then_inc(loaded, 16)
            sp.dma_start(bout[:, :], env.b_out.unsqueeze(0)).then_inc(loaded, 16)
            sp.wait_ge(rows_ready, 1)
            sp.dma_start(env.comb_d, rows[:, :]).then_inc(out, 16)
            for b in range(B):
                sp.wait_ge(c_ready, b + 1)
                sp.dma_start(env.cb_d[b], cb[:, b, :]).then_inc(out, 16)
                sp.wait_ge(m_used, KC * (b + 1))
                sp.dma_start(env.m_d[b, 0], f(hi[b][:, :, :])).then_inc(out, 16)
                sp.dma_start(env.m_d[b, 1], f(lo[b][:, :, :])).then_inc(out, 16)
            sp.wait_ge(out, 16 * (1 + 3 * B))

        @block.vector
        def _(dve):
            c = Chain(dve, dve_step)
            c(dve.tensor_reduce(a[:, :, :], env.aparts[:, :, :].rearrange("p (b t) k -> p b k t", b=B), AX.X, ALU.add))
            c.wait()
            c(dve.tensor_scalar(a[:, :, :], a[:, :, :], 0.5, 0.5, ALU.mult, ALU.add))
            c.wait()
            dve.wait_ge(loaded, 32)
            for b in range(B):
                for n in range(KC):
                    dve.tensor_scalar(aw[b][:, n, :], wout[:, n, :], a[:, b, n:n + 1], None, ALU.mult)\
                       .then_inc(scaled, 1)
            for t in range(TILES):
                c(dve.max(v8[:, t, :], env.logits1[:, t, :]))
            c.wait()
            dve.tensor_tensor(e[:, :], v8[:, :, 1], v8[:, :, 0], ALU.subtract).then_inc(diff, 1)
            dve.wait_ge(exped, 1)
            c(dve.tensor_scalar(w0[:, :], e[:, :], 1.0, None, ALU.add))
            c.wait()
            c(dve.reciprocal(w0[:, :], w0[:, :]))
            c.wait()
            c(dve.tensor_tensor(e[:, :], e[:, :], w0[:, :], ALU.mult))
            c.wait()
            dve.tensor_tensor(comb[:, :], e[:, :], w0[:, :], ALU.add).then_inc(combined, 1)
            for b in range(B):
                for k in range(KC):
                    dve.wait_ge(m_hi, KC * b + k + 1)
                    dve.tensor_tensor(lo[b][:, k, :], psM[k][:, :], f(hi[b][:, k, :]), ALU.subtract).then_inc(m_used, 1)
                dve.wait_ge(c_full, b + 1)
                dve.tensor_copy(cb[:, b, :], psC[b][:, :]).then_inc(c_ready, 1)
            dve.wait_ge(turned, 1)
            dve.tensor_copy(rows[:, :], psT[:, :]).then_inc(rows_ready, 1)

        @block.scalar
        def _(act):
            act.wait_ge(diff, 1)
            act.activation(e[:, :], e[:, :], ACT.Exp).then_inc(exped, 1)
            for b in range(B):
                for k in range(KC):
                    act.wait_ge(full, KC * b + k + 1)
                    act.activation(hi[b][:, k, :], psM[k][:, :], ACT.Copy).then_inc(m_hi, 1)

        @block.tensor
        def _(pe):
            for b in range(B):
                pe.wait_ge(scaled, KC * (b + 1))
                for k in range(KC):
                    if b:
                        pe.wait_ge(m_used, KC * (b - 1) + k + 1)
                    for n in range(KC):
                        ins = pe.matmul(psM[k][:, :], env.wqT[:, n, k * P:(k + 1) * P], aw[b][:, n, :],
                                        start=n == 0, stop=n == KC - 1)
                    ins.then_inc(full, 1)
                for n in range(KC):
                    pe.matmul(psC[b][:, :], env.bqT[:, n, :], aw[b][:, n, :], start=n == 0, stop=False)
                if b == 0:
                    pe.wait_ge(ready, 1)
                    pe.wait_ge(loaded, 32)
                pe.matmul(psC[b][:, :], ones[:, :], bout[:, :], start=False, stop=True).then_inc(c_full, 1)
            pe.wait_ge(combined, 1)
            pe.transpose(psT[:, :], comb[:, :], env.ident[:, :]).then_inc(turned, 1)


def program(nc, env):
    dram = lambda name, shape, dt=F32: nc.dram_tensor(name, shape, dt, kind="Internal").ap()
    env.xn_d = dram("xn_d", [T, D])
    env.qk_d = dram("qk_d", [2, 2, D, T])
    env.v_d = dram("v_d", [T, NH * 2 * HD])
    env.xT_d = dram("xT_d", [2, GROUPS, P, KC, G])
    env.ids_d = dram("ids_d", [MAXT * P, 1])
    env.s_d = dram("s_d", [T, D])
    env.sh_d = dram("sh_d", [T, D])
    env.ys_d = dram("ys_d", [MAXT * P, D])
    env.x1_d = dram("x1_d", [T, D])
    env.xT1_d = dram("xT1_d", [2, TILES, P, KC, P])
    env.wgu1_d = dram("wgu1_d", [2, FB, P, KC, 2, P])
    env.comb_d = dram("comb_d", [TILES, P])
    env.m_d = dram("m_d", [B, 2, P, KC, D])
    env.cb_d = dram("cb_d", [B, P, D])
    ctx = ExitStack()
    with ctx:
        sb = lambda name, shape, dt=F32: ctx.enter_context(nc.sbuf_tensor(name, shape, dt))
        env.ident = sb("ident", [P, P])
        env.stat = sb("stat", [P, TILES, 3])
        env.aparts = sb("aparts", [P, TILES, KC])
        env.logits1 = sb("logits1", [P, TILES, NROUTED])
        with ExitStack() as layer0:
            sb0 = lambda name, shape, dt=F32: layer0.enter_context(nc.sbuf_tensor(name, shape, dt))
            env.logits = sb0("logits", [P, TILES, E])
            env.slot_i = sb0("slot_i", [P, TILES, TOPK], I32)
            env.wexp = sb0("wexp", [P, TILES, TOPK])
            env.ids = sb0("ids", [P, MAXT], I32)
            env.tokid = sb0("tokid", [P, TILES])
            env.first = sb0("first", [P, E + 1], I32)
            phase_front(nc, env)
            phase_route(nc, env)
            phase_attend(nc, env)
            phase_ids(nc, env)
            phase_ffn(nc, env, "b", env.xT_d, SHB, SHR, env.wgu0, env.down0, env.sh_d, False)
            phase_experts(nc, env)
            with ExitStack() as similar:
                sb1 = lambda name, shape, dt=F32: similar.enter_context(nc.sbuf_tensor(name, shape, dt))
                env.wqT = sb1("wqT", [P, KC, D])
                env.bqT = sb1("bqT", [P, KC, P])
                with ExitStack() as keys:
                    sb2 = lambda name, shape, dt=F32: keys.enter_context(nc.sbuf_tensor(name, shape, dt))
                    env.wkv1 = [sb2(f"wkv1{h}", [P, KC, 2, D], F32R) for h in range(2)]
                    env.bkv = sb2("bkv", [P, 2, D])
                    phase_l1_weights(nc, env)
                    phase_combine(nc, env)
                phase_similarity(nc, env)
        phase_ffn(nc, env, "d", env.xT1_d, FB, P, env.wgu1_d, env.down1, env.out, True)


_INS = ["x", "Wq", "Wkv", "Wk", "Wv", "Wo", "gate_w", "w_gate", "w_up", "w_down", "wgu0", "down0", "mask",
        "W_in", "b_in", "W_out", "b_out", "gamma", "beta", "router_w", "wgu1", "down1", "trig"]


def rotation_table():
    inv = (np.float32(1.0) / np.float32(10000.0) ** (np.arange(0, 2 * RH, 2, dtype=np.float32) / np.float32(2 * RH)))
    ang = np.arange(S, dtype=np.float32)[:, None] * inv.astype(np.float32)[None, :]
    cos, sin = np.cos(ang), np.sin(ang)
    tab = np.stack([np.repeat(cos, 2, 1), np.stack([-sin, sin], -1).reshape(S, 2 * RH)], 1)
    return np.tile(tab.reshape(BT, P, 2, 2 * RH), (B, 1, 1, 1)).astype(np.float32)


def kernel(**inputs):
    import concourse.bacc as bacc
    from concourse.bass_utils import run_bass_kernel_spmd

    a = {k: np.asarray(v) for k, v in inputs.items()}
    kcols = lambda w: w.reshape(KC, P, -1).transpose(1, 0, 2)
    laid = {
        "x": a["L0_attn_x"].reshape(T, D),
        "gate_w": a["L0_ffn_gate_w"],
        "wgu0": np.stack([kcols(a["L0_ffn_sw_gate"]), kcols(a["L0_ffn_sw_up"])], 2),
        "down0": a["L0_ffn_sw_down"],
        "mask": mask_table(),
        "gamma": a["L1_attn_gamma"].reshape(KC, P).T,
        "beta": a["L1_attn_beta"].reshape(KC, P).T,
        "router_w": a["L1_ffn_router_weight"].T,
        "wgu1": np.stack([np.concatenate([a[f"L1_ffn_sh_{w}"], a[f"L1_ffn_r_{w}"]], 0).T
                          .reshape(KC, P, FB, P).transpose(2, 1, 0, 3) for w in ("gate", "up")], 3),
        "down1": np.concatenate([a["L1_ffn_sh_down"].T, a["L1_ffn_r_down"].T], 0),
        "trig": rotation_table(),
    }
    for name in ("Wq", "Wkv", "Wk", "Wv", "Wo"):
        laid[name] = a["L0_attn_" + name]
    for name in ("w_gate", "w_up", "w_down"):
        laid[name] = a["L0_ffn_" + name]
    for name in ("W_in", "b_in", "W_out", "b_out"):
        laid[name] = a["L1_attn_" + name]

    nc = bacc.Bacc("TRN2", target_bir_lowering=False, num_devices=1)
    env, arrays, aps = Env(), {}, {}
    for name in _INS:
        arr = np.ascontiguousarray(laid[name])
        arrays[f"in_{name}"] = arr
        aps[name] = nc.dram_tensor(f"in_{name}", arr.shape, mybir.dt.from_np(arr.dtype), kind="ExternalInput").ap()
    env.out = nc.dram_tensor("out", (T, D), F32, kind="ExternalOutput").ap()
    env.x, env.Wq, env.Wkv, env.Wk, env.Wv, env.Wo = (aps[n] for n in _INS[:6])
    env.gate_w, env.w_gate, env.w_up, env.w_down, env.wgu0, env.down0, env.mask = (aps[n] for n in _INS[6:13])
    env.W_in, env.b_in, env.W_out, env.b_out, env.gamma, env.beta = (aps[n] for n in _INS[13:19])
    env.router_w, env.wgu1, env.down1, env.trig = (aps[n] for n in _INS[19:])
    program(nc, env)
    r = run_bass_kernel_spmd(nc, [arrays], core_ids=[0])
    return r.results[0]["out"].reshape(B, S, D)
```
